# Optimizing a Trainium2 kernel written in Bass

```python
import numpy as np
import jax
import jax.numpy as jnp

def _softmax(x, axis=-1):
    return jax.nn.softmax(x, axis=axis)

def _gelu(x):
    return jax.nn.gelu(x, approximate=True)

def _silu(x):
    return jax.nn.silu(x)

def _sigmoid(x):
    return jax.nn.sigmoid(x)

def _layernorm(x, axis=-1, eps=1e-05):
    m = jnp.mean(x, axis=axis, keepdims=True)
    v = jnp.var(x, axis=axis, keepdims=True)
    return (x - m) / jnp.sqrt(v + eps)

def _scatter_add(tgt, idx, src, axis=0):
    return tgt.at[idx].add(src)

def _segment_sum(src, seg, n):
    return jax.ops.segment_sum(src, seg, n)
kernel_name = 'mk_flamingo_gated_d4_seqx_r4_63bc36'

def setup_inputs(seed: int=0):
    np.random.seed(seed)
    _w = jnp.asarray

    def _rec_inputs():
        import jax
        import jax.numpy as jnp
        _rk = jax.random.key(seed)
        x = 7.22e-05 + 1 * jax.random.normal(jax.random.fold_in(_rk, 1), (4, 1024, 256), jnp.float32)
        _lenS = 1024 - jax.random.randint(jax.random.fold_in(_rk, 7), (4,), 0, max(1, 1024 // 4) + 1, jnp.int32)
        _lenS2 = 77 - jax.random.randint(jax.random.fold_in(_rk, 8), (4,), 0, max(1, 77 // 4) + 1, jnp.int32)
        _ctx_1024P = jax.random.normal(jax.random.fold_in(_rk, 11), (4, 16, 256), jnp.float32)
        _ctx_1024c = jax.random.dirichlet(jax.random.fold_in(_rk, 511), 0.3 * jnp.ones((16,), jnp.float32), (4, 77))
        _ctx_1024t = jnp.einsum('bsk,bkd->bsd', _ctx_1024c, _ctx_1024P)
        _ctx_1024t = _ctx_1024t * jax.lax.rsqrt(jnp.mean(jnp.square(_ctx_1024t)) + 1e-12) * 0.953939
        ctx_1024 = 4.13588e-05 + 0.999923 * (_ctx_1024t + 0.3 * jax.random.normal(jax.random.fold_in(_rk, 611), (4, 77, 256), jnp.float32))
        _validS = jnp.arange(1024)[None, :] < _lenS[:, None]
        _validS2 = jnp.arange(77)[None, :] < _lenS2[:, None]
        _causal = jnp.tril(jnp.ones((1024, 1024), dtype=bool))
        mask_BxSxS2_ik1 = jnp.where(jnp.broadcast_to(_validS2[:, None, :], (4, 1024, 77)), 1, 0).astype(jnp.int32)
        _g = jax.random.normal(jax.random.fold_in(_rk, 9001), (2, 4), jnp.float32)
        _g = jnp.sign(_g) * jnp.maximum(jnp.abs(_g), 1.0) + (_g == 0) * 1.0
        g_xattn = _g[0]
        g_ffn = _g[1]
        return (x, ctx_1024, mask_BxSxS2_ik1, g_xattn, g_ffn)
    x, ctx_1024, mask_BxSxS2_ik1, g_xattn, g_ffn = _rec_inputs()

    def _L0_xattn_setup():
        import jax, jax.numpy as jnp
        import numpy as np
        INPUT_DIM = 256
        HEADS = 16
        D_K = INPUT_DIM // HEADS
        B, S = (4, 512)
        key = jax.random.key(seed)
        ks = jax.random.split(key, 12)
        scale = 1.0 / np.sqrt(INPUT_DIM)
        inp = {'q': jax.random.normal(ks[0], (B, S, INPUT_DIM), jnp.float32), 'k': jax.random.normal(ks[1], (B, S, INPUT_DIM), jnp.float32), 'v': jax.random.normal(ks[2], (B, S, INPUT_DIM), jnp.float32), 'mask': jax.random.randint(ks[3], (B, S, S), 0, 2, jnp.int32), 'Wq': jax.random.normal(ks[4], (INPUT_DIM, INPUT_DIM), jnp.float32) * scale, 'bq': jnp.zeros((INPUT_DIM,), jnp.float32), 'Wk': jax.random.normal(ks[5], (INPUT_DIM, INPUT_DIM), jnp.float32) * scale, 'bk': jnp.zeros((INPUT_DIM,), jnp.float32), 'Wv': jax.random.normal(ks[6], (INPUT_DIM, INPUT_DIM), jnp.float32) * scale, 'bv': jnp.zeros((INPUT_DIM,), jnp.float32), 'Wo': jax.random.normal(ks[7], (INPUT_DIM, INPUT_DIM), jnp.float32) * scale, 'bo': jnp.zeros((INPUT_DIM,), jnp.float32)}
        return inp
    _L0_xattn_all = _L0_xattn_setup()
    _L0_xattn_in = {k: v for k, v in _L0_xattn_all.items() if k in ('Wq', 'bq', 'Wk', 'bk', 'Wv', 'bv', 'Wo', 'bo')}
    del _L0_xattn_all

    def _L0_ffn_setup():
        import jax, jax.numpy as jnp
        import numpy as np
        IN_DIM, OUT_DIM, N_PROTO, RANK = (256, 256, 32, 16)
        key = jax.random.key(seed)
        ks = jax.random.split(key, 5)
        x = jax.random.normal(ks[0], (2, 1024, IN_DIM), dtype=jnp.float32)
        prototypes = jax.random.normal(ks[1], (N_PROTO, IN_DIM), dtype=jnp.float32) * 0.02
        B = jax.random.normal(ks[2], (N_PROTO, RANK, IN_DIM), dtype=jnp.float32) * 0.02
        A = jax.random.normal(ks[3], (N_PROTO, OUT_DIM, RANK), dtype=jnp.float32) * 0.02
        bias = jnp.zeros((N_PROTO, OUT_DIM), dtype=jnp.float32)
        temp = jnp.asarray(1.0, dtype=jnp.float32)
        return {'x': x, 'prototypes': prototypes, 'B': B, 'A': A, 'bias': bias, 'temp': temp}
    _L0_ffn_all = _L0_ffn_setup()
    _L0_ffn_in = {k: v for k, v in _L0_ffn_all.items() if k in ('prototypes', 'B', 'A', 'bias', 'temp')}
    del _L0_ffn_all

    def _L1_xattn_setup():
        import jax, jax.numpy as jnp
        import numpy as np
        DIM = 256
        HEADS = 16
        HEAD_DIM = 64
        INNER = HEADS * HEAD_DIM

        def _split_heads(t):
            b, n, _ = t.shape
            return t.reshape(b, n, HEADS, HEAD_DIM).transpose(0, 2, 1, 3)
        key = jax.random.key(seed)
        ks = jax.random.split(key, 7)
        b, n, m = (2, 512, 512)
        s = 0.02
        return {'x': jax.random.normal(ks[0], (b, n, DIM), dtype=jnp.float32), 'context': jax.random.normal(ks[1], (b, m, DIM), dtype=jnp.float32), 'w_kv': jax.random.normal(ks[2], (DIM, 2 * INNER), dtype=jnp.float32) * s, 'w_q': jax.random.normal(ks[3], (DIM, INNER), dtype=jnp.float32) * s, 'w_out1': jax.random.normal(ks[4], (INNER, DIM), dtype=jnp.float32) * s, 'w_out2': jax.random.normal(ks[5], (DIM, DIM), dtype=jnp.float32) * s, 'gamma': jnp.ones((DIM,), dtype=jnp.float32)}
    _L1_xattn_all = _L1_xattn_setup()
    _L1_xattn_in = {k: v for k, v in _L1_xattn_all.items() if k in ('w_kv', 'w_q', 'w_out1', 'w_out2', 'gamma')}
    del _L1_xattn_all

    def _L1_ffn_setup():
        import jax, jax.numpy as jnp
        import numpy as np
        HIDDEN = 256
        INNER = 1024

        def _weight_quant(w):
            scale = 1.0 / jnp.clip(jnp.mean(jnp.abs(w)), 1e-05)
            wq = jnp.clip(jnp.round(w * scale), -1.0, 1.0) / scale
            return w + jax.lax.stop_gradient(wq - w)

        def _act_quant(x):
            scale = 127.0 / jnp.clip(jnp.max(jnp.abs(x), axis=-1, keepdims=True), 1e-05)
            xq = jnp.clip(jnp.round(x * scale), -128.0, 127.0) / scale
            return x + jax.lax.stop_gradient(xq - x)

        def _bitlinear(x, w):
            return jnp.einsum('bsi,oi->bso', _act_quant(x), _weight_quant(w))
        key = jax.random.key(seed)
        k0, k1, k2, k3 = jax.random.split(key, 4)
        x = jax.random.normal(k0, (4, 512, HIDDEN), dtype=jnp.float32)
        w_gate = jax.random.normal(k1, (INNER, HIDDEN), dtype=jnp.float32) / np.sqrt(HIDDEN)
        w_up = jax.random.normal(k2, (INNER, HIDDEN), dtype=jnp.float32) / np.sqrt(HIDDEN)
        w_down = jax.random.normal(k3, (HIDDEN, INNER), dtype=jnp.float32) / np.sqrt(INNER)
        return {'x': x, 'w_gate': w_gate, 'w_up': w_up, 'w_down': w_down}
    _L1_ffn_all = _L1_ffn_setup()
    _L1_ffn_in = {k: v for k, v in _L1_ffn_all.items() if k in ('w_gate', 'w_up', 'w_down')}
    del _L1_ffn_all

    def _L2_xattn_setup():
        import jax, jax.numpy as jnp
        import numpy as np
        B, S, SC, E, H = (2, 512, 512, 256, 16)
        D = E // H
        EPS = 1e-06

        def _layernorm(x, g, b):
            m = jnp.mean(x, axis=-1, keepdims=True)
            v = jnp.mean((x - m) ** 2, axis=-1, keepdims=True)
            return (x - m) / jnp.sqrt(v + EPS) * g + b

        def _mha(xk, xv, xq, Wk, Wv, Wq, Wo, bo, masked):
            K = jnp.einsum('bse,hed->bhsd', xk, Wk)
            V = jnp.einsum('bse,hed->bhsd', xv, Wv)
            Q = jnp.einsum('bqe,hed->bhqd', xq, Wq)
            scores = jnp.einsum('bhqd,bhkd->bhqk', Q, K)
            sk = xk.shape[1]
            if masked:
                causal = jnp.triu(jnp.ones((xq.shape[1], sk), dtype=bool), k=1)
                scores = jnp.where(causal, -jnp.inf, scores)
            att = jax.nn.softmax(scores / jnp.sqrt(jnp.asarray(sk, scores.dtype)), axis=-1)
            out = jnp.einsum('bhqk,bhkd->bhqd', att, V)
            out = out.transpose(0, 2, 1, 3).reshape(out.shape[0], out.shape[2], -1)
            return jax.nn.relu(out @ Wo + bo)
        key = jax.random.key(seed)
        ks = jax.random.split(key, 16)
        w = lambda k, shape: jax.random.normal(k, shape, jnp.float32) * 0.02
        return {'inputs': jax.random.normal(ks[0], (B, S, E), jnp.float32), 'context_seq': jax.random.normal(ks[1], (B, SC, E), jnp.float32), 'Wk1': w(ks[2], (H, E, D)), 'Wv1': w(ks[3], (H, E, D)), 'Wq1': w(ks[4], (H, E, D)), 'Wo1': w(ks[5], (E, E)), 'bo1': jnp.zeros((E,), jnp.float32), 'Wk2': w(ks[6], (H, E, D)), 'Wv2': w(ks[7], (H, E, D)), 'Wq2': w(ks[8], (H, E, D)), 'Wo2': w(ks[9], (E, E)), 'bo2': jnp.zeros((E,), jnp.float32), 'Wf': w(ks[10], (E, E)), 'bf': jnp.zeros((E,), jnp.float32), 'g1': jnp.ones((E,), jnp.float32), 'b1': jnp.zeros((E,), jnp.float32), 'g2': jnp.ones((E,), jnp.float32), 'b2': jnp.zeros((E,), jnp.float32), 'g3': jnp.ones((E,), jnp.float32), 'b3': jnp.zeros((E,), jnp.float32)}
    _L2_xattn_all = _L2_xattn_setup()
    _L2_xattn_in = {k: v for k, v in _L2_xattn_all.items() if k in ('Wk1', 'Wv1', 'Wq1', 'Wo1', 'bo1', 'Wk2', 'Wv2', 'Wq2', 'Wo2', 'bo2', 'Wf', 'bf', 'g1', 'b1', 'g2', 'b2', 'g3', 'b3')}
    del _L2_xattn_all

    def _L2_ffn_setup():
        import jax, jax.numpy as jnp
        import numpy as np
        NUM_EXPERTS = 8
        HIDDEN = 256
        INTER = 256
        BATCH = 2
        SEQ = 256
        TOP_K = 2
        SWIGLU_ALPHA = 1.702
        LIMIT = 7.0

        def _grouped_mm(x, w, expert_ids):
            onehot = jax.nn.one_hot(expert_ids, w.shape[0], dtype=x.dtype)
            y_all = jnp.einsum('tk,ekn->etn', x, w)
            return jnp.einsum('te,etn->tn', onehot, y_all)

        def _gpt_oss_swiglu(x):
            gate = jnp.minimum(x[..., ::2], LIMIT)
            up = jnp.clip(x[..., 1::2], -LIMIT, LIMIT)
            glu = gate * jax.nn.sigmoid(gate * SWIGLU_ALPHA)
            return (up + 1.0) * glu
        key = jax.random.key(seed)
        ks = jax.random.split(key, 7)
        hidden_states = jax.random.normal(ks[0], (BATCH, SEQ, HIDDEN), jnp.float32)
        router_indices = jax.random.randint(ks[1], (BATCH * SEQ, TOP_K), 0, NUM_EXPERTS)
        routing_weights = jax.nn.softmax(jax.random.normal(ks[2], (BATCH * SEQ, NUM_EXPERTS), jnp.float32), axis=-1)
        scale = 0.02
        gate_up_proj = jax.random.normal(ks[3], (NUM_EXPERTS, HIDDEN, 2 * INTER), jnp.float32) * scale
        gate_up_proj_bias = jax.random.normal(ks[4], (NUM_EXPERTS, 2 * INTER), jnp.float32) * scale
        down_proj = jax.random.normal(ks[5], (NUM_EXPERTS, INTER, HIDDEN), jnp.float32) * scale
        down_proj_bias = jax.random.normal(ks[6], (NUM_EXPERTS, HIDDEN), jnp.float32) * scale
        return {'hidden_states': hidden_states, 'router_indices': router_indices, 'routing_weights': routing_weights, 'gate_up_proj': gate_up_proj, 'gate_up_proj_bias': gate_up_proj_bias, 'down_proj': down_proj, 'down_proj_bias': down_proj_bias}
    _L2_ffn_all = _L2_ffn_setup()
    _L2_ffn_in = {k: v for k, v in _L2_ffn_all.items() if k in ('router_indices', 'routing_weights', 'gate_up_proj', 'gate_up_proj_bias', 'down_proj', 'down_proj_bias')}
    del _L2_ffn_all

    def _L3_xattn_setup():
        import jax, jax.numpy as jnp
        import numpy as np
        Q_DIM = 256
        KV_DIM = 256
        key = jax.random.key(seed)
        ks = jax.random.split(key, 8)
        B, LQ, LK = (4, 512, 512)
        scale = 0.02
        return {'q': jax.random.normal(ks[0], (B, LQ, Q_DIM), dtype=jnp.float32), 'kv': jax.random.normal(ks[1], (B, LK, KV_DIM), dtype=jnp.float32), 'Wq': jax.random.normal(ks[2], (Q_DIM, KV_DIM), dtype=jnp.float32) * scale, 'bq': jnp.zeros((KV_DIM,), dtype=jnp.float32), 'Wk': jax.random.normal(ks[3], (KV_DIM, KV_DIM), dtype=jnp.float32) * scale, 'bk': jnp.zeros((KV_DIM,), dtype=jnp.float32), 'Wv': jax.random.normal(ks[4], (KV_DIM, KV_DIM), dtype=jnp.float32) * scale, 'bv': jnp.zeros((KV_DIM,), dtype=jnp.float32)}
    _L3_xattn_all = _L3_xattn_setup()
    _L3_xattn_in = {k: v for k, v in _L3_xattn_all.items() if k in ('Wq', 'bq', 'Wk', 'bk', 'Wv', 'bv')}
    del _L3_xattn_all

    def _L3_ffn_setup():
        import jax, jax.numpy as jnp
        import numpy as np
        NUM_EXPERTS = 8
        TOP_K = 2
        key = jax.random.key(seed)
        ks = jax.random.split(key, 5)
        B, L, E, H, N = (2, 512, 256, 512, NUM_EXPERTS)
        return {'x': jax.random.normal(ks[0], (B, L, E), dtype=jnp.float32), 'gate_kernel': jax.random.normal(ks[1], (E, N), dtype=jnp.float32) / np.sqrt(E), 'w0_kernel': jax.random.normal(ks[2], (N, E, H), dtype=jnp.float32) / np.sqrt(E), 'w1_kernel': jax.random.normal(ks[3], (N, E, H), dtype=jnp.float32) / np.sqrt(E), 'wo_kernel': jax.random.normal(ks[4], (N, H, E), dtype=jnp.float32) / np.sqrt(H)}
    _L3_ffn_all = _L3_ffn_setup()
    _L3_ffn_in = {k: v for k, v in _L3_ffn_all.items() if k in ('gate_kernel', 'w0_kernel', 'w1_kernel', 'wo_kernel')}
    del _L3_ffn_all
    return {'x': x, 'ctx_1024': ctx_1024, 'mask_BxSxS2_ik1': mask_BxSxS2_ik1, 'g_xattn': g_xattn, 'g_ffn': g_ffn, 'L0_xattn_Wq': _L0_xattn_in['Wq'], 'L0_xattn_bq': _L0_xattn_in['bq'], 'L0_xattn_Wk': _L0_xattn_in['Wk'], 'L0_xattn_bk': _L0_xattn_in['bk'], 'L0_xattn_Wv': _L0_xattn_in['Wv'], 'L0_xattn_bv': _L0_xattn_in['bv'], 'L0_xattn_Wo': _L0_xattn_in['Wo'], 'L0_xattn_bo': _L0_xattn_in['bo'], 'L0_ffn_prototypes': _L0_ffn_in['prototypes'], 'L0_ffn_B': _L0_ffn_in['B'], 'L0_ffn_A': _L0_ffn_in['A'], 'L0_ffn_bias': _L0_ffn_in['bias'], 'L0_ffn_temp': _L0_ffn_in['temp'], 'L1_xattn_w_kv': _L1_xattn_in['w_kv'], 'L1_xattn_w_q': _L1_xattn_in['w_q'], 'L1_xattn_w_out1': _L1_xattn_in['w_out1'], 'L1_xattn_w_out2': _L1_xattn_in['w_out2'], 'L1_xattn_gamma': _L1_xattn_in['gamma'], 'L1_ffn_w_gate': _L1_ffn_in['w_gate'], 'L1_ffn_w_up': _L1_ffn_in['w_up'], 'L1_ffn_w_down': _L1_ffn_in['w_down'], 'L2_xattn_Wk1': _L2_xattn_in['Wk1'], 'L2_xattn_Wv1': _L2_xattn_in['Wv1'], 'L2_xattn_Wq1': _L2_xattn_in['Wq1'], 'L2_xattn_Wo1': _L2_xattn_in['Wo1'], 'L2_xattn_bo1': _L2_xattn_in['bo1'], 'L2_xattn_Wk2': _L2_xattn_in['Wk2'], 'L2_xattn_Wv2': _L2_xattn_in['Wv2'], 'L2_xattn_Wq2': _L2_xattn_in['Wq2'], 'L2_xattn_Wo2': _L2_xattn_in['Wo2'], 'L2_xattn_bo2': _L2_xattn_in['bo2'], 'L2_xattn_Wf': _L2_xattn_in['Wf'], 'L2_xattn_bf': _L2_xattn_in['bf'], 'L2_xattn_g1': _L2_xattn_in['g1'], 'L2_xattn_b1': _L2_xattn_in['b1'], 'L2_xattn_g2': _L2_xattn_in['g2'], 'L2_xattn_b2': _L2_xattn_in['b2'], 'L2_xattn_g3': _L2_xattn_in['g3'], 'L2_xattn_b3': _L2_xattn_in['b3'], 'L2_ffn_router_indices': _L2_ffn_in['router_indices'], 'L2_ffn_routing_weights': _L2_ffn_in['routing_weights'], 'L2_ffn_gate_up_proj': _L2_ffn_in['gate_up_proj'], 'L2_ffn_gate_up_proj_bias': _L2_ffn_in['gate_up_proj_bias'], 'L2_ffn_down_proj': _L2_ffn_in['down_proj'], 'L2_ffn_down_proj_bias': _L2_ffn_in['down_proj_bias'], 'L3_xattn_Wq': _L3_xattn_in['Wq'], 'L3_xattn_bq': _L3_xattn_in['bq'], 'L3_xattn_Wk': _L3_xattn_in['Wk'], 'L3_xattn_bk': _L3_xattn_in['bk'], 'L3_xattn_Wv': _L3_xattn_in['Wv'], 'L3_xattn_bv': _L3_xattn_in['bv'], 'L3_ffn_gate_kernel': _L3_ffn_in['gate_kernel'], 'L3_ffn_w0_kernel': _L3_ffn_in['w0_kernel'], 'L3_ffn_w1_kernel': _L3_ffn_in['w1_kernel'], 'L3_ffn_wo_kernel': _L3_ffn_in['wo_kernel']}

def reference(x, ctx_1024, mask_BxSxS2_ik1, g_xattn, g_ffn, L0_xattn_Wq, L0_xattn_bq, L0_xattn_Wk, L0_xattn_bk, L0_xattn_Wv, L0_xattn_bv, L0_xattn_Wo, L0_xattn_bo, L0_ffn_prototypes, L0_ffn_B, L0_ffn_A, L0_ffn_bias, L0_ffn_temp, L1_xattn_w_kv, L1_xattn_w_q, L1_xattn_w_out1, L1_xattn_w_out2, L1_xattn_gamma, L1_ffn_w_gate, L1_ffn_w_up, L1_ffn_w_down, L2_xattn_Wk1, L2_xattn_Wv1, L2_xattn_Wq1, L2_xattn_Wo1, L2_xattn_bo1, L2_xattn_Wk2, L2_xattn_Wv2, L2_xattn_Wq2, L2_xattn_Wo2, L2_xattn_bo2, L2_xattn_Wf, L2_xattn_bf, L2_xattn_g1, L2_xattn_b1, L2_xattn_g2, L2_xattn_b2, L2_xattn_g3, L2_xattn_b3, L2_ffn_router_indices, L2_ffn_routing_weights, L2_ffn_gate_up_proj, L2_ffn_gate_up_proj_bias, L2_ffn_down_proj, L2_ffn_down_proj_bias, L3_xattn_Wq, L3_xattn_bq, L3_xattn_Wk, L3_xattn_bk, L3_xattn_Wv, L3_xattn_bv, L3_ffn_gate_kernel, L3_ffn_w0_kernel, L3_ffn_w1_kernel, L3_ffn_wo_kernel):
    import jax
    import jax.numpy as jnp

    def _L0_xattn_ref(q, k, v, mask, Wq, bq, Wk, bk, Wv, bv, Wo, bo):
        import jax, jax.numpy as jnp
        import numpy as np
        INPUT_DIM = 256
        HEADS = 16
        D_K = INPUT_DIM // HEADS
        B, S = (4, 512)
        bs = q.shape[0]

        def proj(x, W, b):
            return (x @ W.T + b).reshape(bs, -1, HEADS, D_K).transpose(0, 2, 1, 3)
        qh, kh, vh = (proj(q, Wq, bq), proj(k, Wk, bk), proj(v, Wv, bv))
        scores = jnp.einsum('bhqd,bhkd->bhqk', qh, kh) / jnp.sqrt(jnp.float32(D_K))
        scores = jnp.where(mask[:, None] == 0, jnp.float32(-1000000000.0), scores)
        attn = jax.nn.softmax(scores, axis=-1)
        ctx = jnp.einsum('bhqk,bhkd->bhqd', attn, vh)
        concat = ctx.transpose(0, 2, 1, 3).reshape(bs, -1, INPUT_DIM)
        return concat @ Wo.T + bo

    def _L0_ffn_ref(x, prototypes, B, A, bias, temp):
        import jax, jax.numpy as jnp
        import numpy as np
        IN_DIM, OUT_DIM, N_PROTO, RANK = (256, 256, 32, 16)
        lead = x.shape[:-1]
        xf = x.reshape(-1, IN_DIM)
        x2 = jnp.sum(xf * xf, axis=1, keepdims=True)
        p2 = jnp.sum(prototypes * prototypes, axis=1)
        d2 = x2 + p2[None, :] - 2.0 * (xf @ prototypes.T)
        dists = jnp.sqrt(jnp.maximum(d2, 0.0))
        t = jnp.maximum(jnp.abs(temp), 0.1)
        w = jax.nn.softmax(-dists / t, axis=1)
        topw, topi = jax.lax.top_k(w, 2)
        topw = topw / jnp.sum(topw, axis=1, keepdims=True)
        out = jnp.zeros((xf.shape[0], OUT_DIM), dtype=xf.dtype)
        for tslot in range(2):
            idx = topi[:, tslot]
            wt = topw[:, tslot:tslot + 1]
            h = jnp.einsum('nri,ni->nr', B[idx], xf)
            y = jnp.einsum('nor,nr->no', A[idx], h) + bias[idx]
            out = out + wt * y
        return out.reshape(*lead, OUT_DIM)

    def _L1_xattn_ref(x, context, w_kv, w_q, w_out1, w_out2, gamma):
        import jax, jax.numpy as jnp
        import numpy as np
        DIM = 256
        HEADS = 16
        HEAD_DIM = 64
        INNER = HEADS * HEAD_DIM

        def _split_heads(t):
            b, n, _ = t.shape
            return t.reshape(b, n, HEADS, HEAD_DIM).transpose(0, 2, 1, 3)
        scale = HEAD_DIM ** (-0.5)
        kv = context @ w_kv
        k, v = jnp.split(kv, 2, axis=-1)
        q = _split_heads(x @ w_q)
        k = _split_heads(k)
        v = _split_heads(v)
        dots = jnp.einsum('bhid,bhjd->bhij', q, k) * scale
        attn = jax.nn.softmax(dots, axis=-1)
        out = jnp.einsum('bhij,bhjd->bhid', attn, v)
        b, h, n, d = out.shape
        out = out.transpose(0, 2, 1, 3).reshape(b, n, h * d)
        out = jax.nn.relu(out @ w_out1) @ w_out2
        mean = jnp.mean(out, axis=-1, keepdims=True)
        var = jnp.var(out, axis=-1, keepdims=True)
        return (out - mean) * jax.lax.rsqrt(var + 1e-05) * gamma

    def _L1_ffn_ref(x, w_gate, w_up, w_down):
        import jax, jax.numpy as jnp
        import numpy as np
        HIDDEN = 256
        INNER = 1024

        def _weight_quant(w):
            scale = 1.0 / jnp.clip(jnp.mean(jnp.abs(w)), 1e-05)
            wq = jnp.clip(jnp.round(w * scale), -1.0, 1.0) / scale
            return w + jax.lax.stop_gradient(wq - w)

        def _act_quant(x):
            scale = 127.0 / jnp.clip(jnp.max(jnp.abs(x), axis=-1, keepdims=True), 1e-05)
            xq = jnp.clip(jnp.round(x * scale), -128.0, 127.0) / scale
            return x + jax.lax.stop_gradient(xq - x)

        def _bitlinear(x, w):
            return jnp.einsum('bsi,oi->bso', _act_quant(x), _weight_quant(w))
        gate = jax.nn.silu(_bitlinear(x, w_gate))
        up = _bitlinear(x, w_up)
        return _bitlinear(gate * up, w_down)

    def _L2_xattn_ref(inputs, context_seq, Wk1, Wv1, Wq1, Wo1, bo1, Wk2, Wv2, Wq2, Wo2, bo2, Wf, bf, g1, b1, g2, b2, g3, b3):
        import jax, jax.numpy as jnp
        import numpy as np
        B, S, SC, E, H = (2, 512, 512, 256, 16)
        D = E // H
        EPS = 1e-06

        def _layernorm(x, g, b):
            m = jnp.mean(x, axis=-1, keepdims=True)
            v = jnp.mean((x - m) ** 2, axis=-1, keepdims=True)
            return (x - m) / jnp.sqrt(v + EPS) * g + b

        def _mha(xk, xv, xq, Wk, Wv, Wq, Wo, bo, masked):
            K = jnp.einsum('bse,hed->bhsd', xk, Wk)
            V = jnp.einsum('bse,hed->bhsd', xv, Wv)
            Q = jnp.einsum('bqe,hed->bhqd', xq, Wq)
            scores = jnp.einsum('bhqd,bhkd->bhqk', Q, K)
            sk = xk.shape[1]
            if masked:
                causal = jnp.triu(jnp.ones((xq.shape[1], sk), dtype=bool), k=1)
                scores = jnp.where(causal, -jnp.inf, scores)
            att = jax.nn.softmax(scores / jnp.sqrt(jnp.asarray(sk, scores.dtype)), axis=-1)
            out = jnp.einsum('bhqk,bhkd->bhqd', att, V)
            out = out.transpose(0, 2, 1, 3).reshape(out.shape[0], out.shape[2], -1)
            return jax.nn.relu(out @ Wo + bo)
        a = _mha(inputs, inputs, inputs, Wk1, Wv1, Wq1, Wo1, bo1, masked=True)
        a = _layernorm(inputs + a, g1, b1)
        c = _mha(context_seq, context_seq, a, Wk2, Wv2, Wq2, Wo2, bo2, masked=False)
        c = _layernorm(c + c, g2, b2)
        f = jax.nn.relu(c @ Wf + bf)
        return _layernorm(c + f, g3, b3)

    def _L2_ffn_ref(hidden_states, router_indices, routing_weights, gate_up_proj, gate_up_proj_bias, down_proj, down_proj_bias):
        import jax, jax.numpy as jnp
        import numpy as np
        NUM_EXPERTS = 8
        HIDDEN = 256
        INTER = 256
        BATCH = 2
        SEQ = 256
        TOP_K = 2
        SWIGLU_ALPHA = 1.702
        LIMIT = 7.0

        def _grouped_mm(x, w, expert_ids):
            onehot = jax.nn.one_hot(expert_ids, w.shape[0], dtype=x.dtype)
            y_all = jnp.einsum('tk,ekn->etn', x, w)
            return jnp.einsum('te,etn->tn', onehot, y_all)

        def _gpt_oss_swiglu(x):
            gate = jnp.minimum(x[..., ::2], LIMIT)
            up = jnp.clip(x[..., 1::2], -LIMIT, LIMIT)
            glu = gate * jax.nn.sigmoid(gate * SWIGLU_ALPHA)
            return (up + 1.0) * glu
        B = hidden_states.shape[0]
        H = hidden_states.shape[-1]
        x = hidden_states.reshape(-1, H)
        M = x.shape[0]
        top_k = router_indices.shape[1]
        num_experts = gate_up_proj.shape[0]
        topk_weights = jnp.take_along_axis(routing_weights, router_indices, axis=1)
        flat_experts = router_indices.reshape(-1)
        sort_idx = jnp.argsort(flat_experts)
        sorted_pos = sort_idx // top_k
        expert_sorted = flat_experts[sort_idx]
        grouped = x[sorted_pos]
        gate_up = _grouped_mm(grouped, gate_up_proj, expert_sorted)
        gate_up = gate_up + gate_up_proj_bias[expert_sorted]
        inter = _gpt_oss_swiglu(gate_up)
        down = _grouped_mm(inter, down_proj, expert_sorted)
        down = down + down_proj_bias[expert_sorted]
        down = down * topk_weights.reshape(-1)[sort_idx][:, None]
        out = jnp.zeros((M, H), x.dtype).at[sorted_pos].add(down)
        return out.reshape(B, -1, H)

    def _L3_xattn_ref(q, kv, Wq, bq, Wk, bk, Wv, bv):
        import jax, jax.numpy as jnp
        import numpy as np
        Q_DIM = 256
        KV_DIM = 256
        Q = jnp.einsum('bld,de->ble', q, Wq) + bq
        K = jnp.einsum('bld,de->ble', kv, Wk) + bk
        V = jnp.einsum('bld,de->ble', kv, Wv) + bv
        dim = K.shape[-1]
        score = jnp.einsum('bid,bkd->bik', Q, K) / jnp.sqrt(jnp.asarray(dim, Q.dtype))
        probs = jax.nn.softmax(score, axis=-1)
        out = jnp.einsum('bik,bkd->bid', probs, V)
        return out

    def _L3_ffn_ref(x, gate_kernel, w0_kernel, w1_kernel, wo_kernel):
        import jax, jax.numpy as jnp
        import numpy as np
        NUM_EXPERTS = 8
        TOP_K = 2
        B, L, E = x.shape
        gate_logits = jnp.einsum('ble,en->bln', x, gate_kernel)
        top_k_weights, top_k_indices = jax.lax.top_k(gate_logits, TOP_K)
        softmax_probs = jax.nn.softmax(top_k_weights.astype(jnp.float32), axis=-1)
        weights = jnp.zeros_like(gate_logits)
        b_idx = jnp.arange(B)[:, None, None]
        l_idx = jnp.arange(L)[:, None]
        weights = weights.at[b_idx, l_idx, top_k_indices].set(softmax_probs)
        layer_w0 = jnp.einsum('ble,neh->blnh', x, w0_kernel)
        layer_w1 = jnp.einsum('ble,neh->blnh', x, w1_kernel)
        layer_mult = jax.nn.silu(layer_w0) * layer_w1
        intermediate = jnp.einsum('blnh,nhe->blne', layer_mult, wo_kernel)
        output = jnp.einsum('blne,bln->ble', intermediate, weights)
        return output
    x = x + jnp.tanh(g_xattn[0]) * _L0_xattn_ref(_layernorm(x, axis=-1), ctx_1024, ctx_1024, mask_BxSxS2_ik1, L0_xattn_Wq, L0_xattn_bq, L0_xattn_Wk, L0_xattn_bk, L0_xattn_Wv, L0_xattn_bv, L0_xattn_Wo, L0_xattn_bo)
    x = x + jnp.tanh(g_ffn[0]) * _L0_ffn_ref(_layernorm(x, axis=-1), L0_ffn_prototypes, L0_ffn_B, L0_ffn_A, L0_ffn_bias, L0_ffn_temp)
    x = x + jnp.tanh(g_xattn[1]) * _L1_xattn_ref(_layernorm(x, axis=-1), ctx_1024, L1_xattn_w_kv, L1_xattn_w_q, L1_xattn_w_out1, L1_xattn_w_out2, L1_xattn_gamma)
    x = x + jnp.tanh(g_ffn[1]) * _L1_ffn_ref(_layernorm(x, axis=-1), L1_ffn_w_gate, L1_ffn_w_up, L1_ffn_w_down)
    x = x + jnp.tanh(g_xattn[2]) * _L2_xattn_ref(_layernorm(x, axis=-1), ctx_1024, L2_xattn_Wk1, L2_xattn_Wv1, L2_xattn_Wq1, L2_xattn_Wo1, L2_xattn_bo1, L2_xattn_Wk2, L2_xattn_Wv2, L2_xattn_Wq2, L2_xattn_Wo2, L2_xattn_bo2, L2_xattn_Wf, L2_xattn_bf, L2_xattn_g1, L2_xattn_b1, L2_xattn_g2, L2_xattn_b2, L2_xattn_g3, L2_xattn_b3)
    x = x + jnp.tanh(g_ffn[2]) * _L2_ffn_ref(_layernorm(x, axis=-1), L2_ffn_router_indices, L2_ffn_routing_weights, L2_ffn_gate_up_proj, L2_ffn_gate_up_proj_bias, L2_ffn_down_proj, L2_ffn_down_proj_bias)
    x = x + jnp.tanh(g_xattn[3]) * _L3_xattn_ref(_layernorm(x, axis=-1), ctx_1024, L3_xattn_Wq, L3_xattn_bq, L3_xattn_Wk, L3_xattn_bk, L3_xattn_Wv, L3_xattn_bv)
    x = x + jnp.tanh(g_ffn[3]) * _L3_ffn_ref(_layernorm(x, axis=-1), L3_ffn_gate_kernel, L3_ffn_w0_kernel, L3_ffn_w1_kernel, L3_ffn_wo_kernel)
    return x

_drawn_inputs = setup_inputs


def setup_inputs(seed=0):
    import zlib

    import numpy as np

    out = dict(_drawn_inputs(seed))
    spreads = {'L0_xattn_bq': (0.0, 0.287),
     'L0_xattn_bk': (0.0, 2.0),
     'L0_xattn_bv': (0.0, 0.1),
     'L0_xattn_bo': (0.0, 0.1),
     'L0_ffn_bias': (0.0, 0.1),
     'L1_xattn_gamma': (1.0, 0.2),
     'L2_xattn_bo1': (0.0, 0.8),
     'L2_xattn_bo2': (0.0, 0.1),
     'L2_xattn_bf': (0.0, 0.1),
     'L2_xattn_g1': (1.0, 0.6),
     'L2_xattn_b1': (0.0, 0.8),
     'L2_xattn_g2': (1.0, 0.2),
     'L2_xattn_b2': (0.0, 0.1),
     'L2_xattn_g3': (1.0, 0.2),
     'L2_xattn_b3': (0.0, 0.1),
     'L3_xattn_bq': (0.0, 2.0),
     'L3_xattn_bk': (0.0, 2.0),
     'L3_xattn_bv': (0.0, 0.558)}
    factors = {'g_ffn': 30.864,
     'L0_ffn_B': 2.888,
     'L0_ffn_A': 3.152,
     'L2_xattn_Wk1': 32.346,
     'L2_xattn_Wv1': 8.0,
     'L2_xattn_Wq1': 35.264,
     'L2_xattn_Wo1': 8.0,
     'L2_xattn_Wk2': 4.057,
     'L2_xattn_Wq2': 3.948,
     'L2_ffn_routing_weights': 8.0,
     'L2_ffn_gate_up_proj': 8.0,
     'L2_ffn_gate_up_proj_bias': 8.0,
     'L2_ffn_down_proj': 8.0,
     'L2_ffn_down_proj_bias': 34.666,
     'L3_xattn_Wq': 15.624,
     'L3_xattn_Wk': 15.321}
    for name, (base, spread) in spreads.items():
        noise = np.random.default_rng([zlib.crc32(name.encode()), seed]).standard_normal(out[name].shape)
        drawn = base * np.exp(spread * noise) if base else spread * noise
        out[name] = jnp.asarray(drawn.astype(out[name].dtype))
    for name, factor in factors.items():
        out[name] = (out[name] * factor).astype(out[name].dtype)
    return out
```

```python
from contextlib import ExitStack

import concourse.bass as bass
from concourse import mybir
import numpy as np

P = 128
D = 256
KD = D // P
B, S = 4, 1024
T = B * S // P
TB = S // P
CH = 4
CT = CH * P
NC = 77
H = 16
HH = 8
HK = HH * NC
BK = HK // 2
KCH = -(-HK // P)
KLAST = HK - (KCH - 1) * P
UN = 2 * CH
PBUF = 4

F32 = mybir.dt.float32
BF16 = mybir.dt.bfloat16
I32 = mybir.dt.int32
U32 = mybir.dt.uint32
ACT = mybir.ActivationFunctionType
ALU = mybir.AluOpType
AX = mybir.AxisListType

VEC = ["L0_xattn_bv", "L0_xattn_bo", "L1_xattn_gamma", "L2_xattn_bo1", "L2_xattn_bo2", "L2_xattn_bf",
       "L2_xattn_g1", "L2_xattn_b1", "L2_xattn_g2", "L2_xattn_b2", "L2_xattn_g3", "L2_xattn_b3", "L3_xattn_bv"]
WEIGHTS = {"L0": ["L0_Wq", "L0_Wk", "L0_Wv", "L0_Wo"],
           "L0F": ["L0F_protoT", "L0F_BT", "L0F_A", "L0F_bias"],
           "L1": ["L1_Wk", "L1_Wv", "L1_WqT", "L1_Wo1", "L1_Wo"],
           "L1F": ["L1F_gate", "L1F_up", "L1F_down"],
           "L2S": ["L2S_Wq", "L2S_Wk", "L2S_Wv", "L2S_Wo"],
           "L2": ["L2_Wq", "L2_Wk", "L2_Wv", "L2_Wo", "L2_Wf"],
           "L3": ["L3_WqT", "L3_Wk", "L3_Wv"]}
ZONE_B = 34 * 256
ARENA = ZONE_B + 24 * 256
COL = ["L0_xattn_bq", "L0_xattn_bk", "L3_xattn_bq", "L3_xattn_bk"]


class Count:

    def __init__(self, sem, start=0):
        self.sem, self.base, self.k = sem, start, 0

    def enter(self, base):
        self.base, self.k = base, 0

    def up(self, n=1):
        self.k += n
        return self.base + self.k


class Chip:

    def __init__(self, nc, ctx):
        self.nc, self.ctx = nc, ctx

    def keep(self, name, shape, dt=F32):
        return self.ctx.enter_context(self.nc.sbuf_tensor(name, shape, dt))

    def zone(self, names, dram, offset):
        for name in names:
            shape = dram[name].shape
            n = int(np.prod(shape[1:]))
            v = self.arena[0:shape[0], offset:offset + n]
            if len(shape) == 3:
                v = v.rearrange("p (a n) -> p a n", a=shape[1])
            self.w[name] = v
            offset += n

    def load(self, sp, names, dram):
        for name in names:
            sp.dma_start(self.w[name], dram[name]).then_inc(self.w_in[name], 16)

    def settle(self, eng):
        eng.sem_inc(self.settled[str(eng.engine)], 1)

    def col(self, name):
        n = COL.index(name)
        return self.cols[:, 2 * n:2 * n + 2]

    def vec(self, name):
        n = VEC.index(name)
        return self.vecs[:, n * D:(n + 1) * D]


def wide(ap, shape):
    return ap.to_broadcast(shape)


N_LOADED = 16 * (3 + len(VEC) + len(COL) + B)


def load_stage(chip, dram):
    nc = chip.nc
    with ExitStack() as ctx:
        raw_gates = ctx.enter_context(nc.sbuf_tensor("raw_gates", [P, 2 * B], F32))
        gates_in = ctx.enter_context(nc.semaphore("gates_in"))
        zeroed = ctx.enter_context(nc.semaphore("zeroed"))
        block = ctx.enter_context(nc.Block())

        @block.sync
        def _(sp):
            sp.dma_start(raw_gates[:, 0:B], dram["g_xattn"].partition_broadcast(P)).then_inc(gates_in, 16)
            sp.dma_start(raw_gates[:, B:], dram["g_ffn"].partition_broadcast(P)).then_inc(gates_in, 16)
            sp.dma_start(chip.ctxT[:], dram["ctxT"]).then_inc(chip.loaded, 16)
            sp.dma_start(chip.headmask[:], dram["headmask"]).then_inc(chip.loaded, 16)
            sp.dma_start(chip.rowmask[:], dram["rowmask"]).then_inc(chip.loaded, 16)
            for n, name in enumerate(VEC):
                sp.dma_start(chip.vecs[:, n * D:(n + 1) * D], dram[name].partition_broadcast(P)).then_inc(chip.loaded, 16)
            for n, name in enumerate(COL):
                sp.dma_start(chip.cols[:, 2 * n:2 * n + 2], dram[name]).then_inc(chip.loaded, 16)
            sp.dma_start(chip.x[:, 0:TB * D].rearrange("p (t d) -> p t d", d=D),
                         dram["x"][:, 0:TB, :]).then_inc(chip.loaded, 16)
            chip.load(sp, WEIGHTS["L0"], dram)
            for b in range(1, B):
                sp.dma_start(chip.x[:, b * TB * D:(b + 1) * TB * D].rearrange("p (t d) -> p t d", d=D),
                             dram["x"][:, b * TB:(b + 1) * TB, :]).then_inc(chip.loaded, 16)
            chip.load(sp, WEIGHTS["L0F"] + WEIGHTS["L1"], dram)

        @block.gpsimd
        def _(pool):
            nc.gpsimd.memset(chip.ident[:], 0.0).then_inc(zeroed, 1)
            nc.gpsimd.memset(chip.neghalf[:], -0.5)
            nc.gpsimd.memset(chip.half[:], 0.5)
            nc.gpsimd.memset(chip.ones[:], 1.0)
            pool.wait_ge(zeroed, 1)
            nc.gpsimd.affine_select(out=chip.ident[:], in_=chip.ident[:], compare_op=ALU.not_equal, fill=1.0,
                                    base=0, pattern=[[-1, P]], channel_multiplier=1)
            nc.gpsimd.iota(chip.iota[:], [[1, 32]], base=0, channel_multiplier=0,
                           allow_small_or_imprecise_dtypes=True)

        @block.scalar
        def _(act):
            act.wait_ge(gates_in, 32)
            nc.scalar.activation(chip.gates[:], raw_gates[:], ACT.Tanh)


def walk(front, unit, turn, out, lag=2):
    front(0)
    for j in range(2):
        for u in range(UN):
            unit(j, u)
            if u >= lag:
                turn(j, u - lag)
            elif j:
                turn(j - 1, u - lag + UN)
            if (j, u) == (0, 4):
                front(1)
            if j and u >= 2:
                out(0, u - 2)
    for u in range(UN - lag, UN):
        turn(1, u)
    for piece in range(6):
        out(1, piece)


def context_stage(chip, dram, kind):
    nc = chip.nc
    w = chip.w
    L = {"L0": 0, "L1": 1, "L2": 2}[kind]
    scale = {"L0": 0.25, "L1": 0.125, "L2": 1.0 / np.sqrt(np.float32(NC))}[kind]
    scale = float(np.float32(scale))
    gate = chip.gates[:, L:L + 1]
    fold = kind == "L1"
    with ExitStack() as ctx:
        def sb(name, shape, dt=F32):
            return ctx.enter_context(nc.sbuf_tensor(f"{kind}_{name}", shape, dt))

        def sem(name):
            return ctx.enter_context(nc.semaphore(f"{kind}_{name}"))

        S_ps = [ctx.enter_context(nc.psum_tensor(f"{kind}_scores{i}", [P, 2, 512], F32)) for i in range(2)]
        T_ps = ctx.enter_context(nc.psum_tensor(f"{kind}_turned", [P, 1024], F32))
        R_ps = [ctx.enter_context(nc.psum_tensor(f"{kind}_ring{i}", [P, 512], F32)) for i in range(2)]
        ctx_rep = sb("ctx_rep", [P, KD, HK])
        xn = sb("xn", [P, CH, D])
        xT = sb("xT", [P, 2 if fold else 1, KD, CT])
        prob = sb("prob", [P, PBUF, HK])
        probT = sb("probT", [P, 2, 2, KCH, CT])
        oT = sb("oT", [P, 2, CT])
        res = sb("res", [P, CH, D])
        mx = sb("mx", [P, 2, HH])
        sm = sb("sm", [P, 4, HH])
        rc = sb("rc", [P, 4, HH])
        stat = sb("stat", [P, 2, CH, 6])
        mv = sb("mv", [P, 2, CH, 2])
        rs = sb("rs", [P, 2, CH])
        ve = sb("ve", [P, 2, CH])
        if fold:
            kfold = sb("kfold", [P, KD, 2 * HK])
            vrow = sb("vrow", [P, 2 * KCH, D])
            stat2 = sb("stat2", [P, CH, 6])
            mv2 = sb("mv2", [P, CH, 2])
            rs2 = sb("rs2", [P, CH])
            ve2 = sb("ve2", [P, CH])
        else:
            kT = sb("kT", [P, 2, NC])
            kblk = sb("kblk", [P, 2, HH, NC])
            vrow = sb("vrow", [P, 2, KCH, P])
            qT = sb("qT", [P, 2, KD, CT])
        spare = probT[:].rearrange("p j f c t -> p (j f c t)")
        if fold:
            kpair, vpair = (spare[:, n * 2 * HK:(n + 1) * 2 * HK].rearrange("p (m a k) -> p m a k", a=2, k=NC) for n in range(2))
            kT, vT = (spare[:, (8 + n) * HK:(9 + n) * HK].rearrange("p (m k) -> p m k", k=NC) for n in range(2))
            vfoldT = spare[:, 4 * HK:4 * HK + KD * 2 * HK].rearrange("p (c r) -> p c r", c=KD)
        else:
            vraw = spare[:, 0:2 * KCH * P].rearrange("p (f c d) -> p f c d", f=2, c=KCH)
        gvec = sb("gvec", [P, 2 * D])
        if kind == "L0":
            mask_i = sb("mask_i", [P, TB, NC], I32)
            unmask = sb("unmask", [P, TB, NC], U32)
            floor = sb("floor", [P, 1])
        if kind == "L2":
            stat2 = sb("stat2", [P, CH, 6])
            mv2 = sb("mv2", [P, CH, 2])
            rs2 = sb("rs2", [P, CH])
            ve2 = sb("ve2", [P, CH])
            cT = oT
            cn, fo = (chip.arena[:, ZONE_B + (6 + 4 * n) * D:ZONE_B + (10 + 4 * n) * D].rearrange("p (i d) -> p i d", d=D) for n in range(2))

        mask_in, mask_used, unmasked = sem("mask_in"), sem("mask_used"), sem("unmasked")
        rep_done, rep_free = sem("rep_done"), sem("rep_free")
        blocks_done, blocks_free = sem("blocks_done"), sem("blocks_free")
        pairs_done = sem("pairs_done")
        stats_done, rstd_done, xn_done, xn_free = sem("stats_done"), sem("rstd_done"), sem("xn_done"), sem("xn_free")
        ring_full, ring_free = sem("ring_full"), sem("ring_free")
        s_full = sem("s_full")
        shifted, exp_done, inv_done, p_done = sem("shifted"), sem("exp_done"), sem("inv_done"), sem("p_done")
        t_full, t_free = sem("t_full"), sem("t_free")
        stats2_done, rstd2_done, norm2_done = sem("stats2_done"), sem("rstd2_done"), sem("norm2_done")
        c_done, f_sum = sem("c_done"), sem("f_sum")
        relu_done = sem("relu_done")
        x_done = sem("x_done")
        dve_step, pool_step, const_done = sem("dve_step"), sem("pool_step"), sem("const_done")
        block = ctx.enter_context(nc.Block())

        def s_view(U):
            return S_ps[U % 2][:, :, 0:BK].rearrange("p a (h k) -> p a h k", k=NC)

        def p_view(u):
            return prob[:, u % PBUF, :].rearrange("p (a h k) -> p a h k", a=2, k=NC)

        def rows(c):
            return P if c < KCH - 1 else KLAST

        at = {}
        RINGS = {"L0": 6, "L1": 22, "L2": 6}[kind] + 2 * (2 + (0 if fold else 2) + 6) + (2 * 6 if kind == "L2" else 0)

        if kind == "L1":
            @block.sync
            def _(sp):
                chip.load(sp, WEIGHTS["L1F"], dram)

        if kind == "L2":
            @block.sync
            def _(sp):
                with sp.Fori(0, B) as b:
                    for j in range(2):
                        sp.wait_ge(xn_free, 2 * b + j + 1)
                        sp.dma_start(xn[:], dram["a"][:, bass.ds((2 * b + j) * CH, CH), :]).then_inc(xn_done, 16)

        if kind == "L0":
            @block.sync
            def _(sp):
                with sp.Fori(0, B) as b:
                    sp.wait_ge(mask_used, b + 1)
                    sp.dma_start(mask_i[:], dram["mask"][:, bass.ts(b, TB), :]).then_inc(mask_in, 16)

        @block.tensor
        def _(pe):
            ring = Count(ring_full)
            stepfree = Count(ring_free)

            def bank():
                pe.wait_ge(ring_free, stepfree.up())
                return R_ps[(stepfree.k - 1) % 2]

            def drained():
                pe.wait_ge(ring_free, stepfree.base + 2 + stepfree.k)

            pe.sem_inc(rep_free, 1)
            pe.sem_inc(blocks_free, 1)
            pe.sem_inc(xn_free, 1)
            pe.sem_inc(t_full, PBUF)
            if L == 0:
                pe.wait_ge(chip.loaded, N_LOADED)
            for name in WEIGHTS[kind]:
                pe.wait_ge(chip.w_in[name], 16)
            with pe.Fori(0, B) as b:
                stepfree.enter(b * RINGS)

                def setup():
                    pe.wait_ge(rep_done, b + 1)
                    if not fold:
                        for m in range(2):
                            o = bank()
                            for k in range(KD):
                                mm = nc.tensor.matmul(o[:, 0:NC], w[f"{kind}_Wk"][:, k, m * P:(m + 1) * P], ctx_rep[:, k, 0:NC],
                                                      start=(k == 0), stop=(k == KD - 1))
                            mm.then_inc(ring_full, 1)
                        for hf in range(2):
                            for group in (range(KCH - 1), range(KCH - 1, KCH)):
                                o = bank()
                                for n, c in enumerate(group):
                                    for k in range(KD):
                                        mm = nc.tensor.matmul(o[0:rows(c), n * P:(n + 1) * P], ctx_rep[:, k, c * P:c * P + rows(c)],
                                                              w[f"{kind}_Wv"][:, k, hf * P:(hf + 1) * P],
                                                              start=(k == 0), stop=(k == KD - 1))
                                mm.then_inc(ring_full, 1)
                        mm = None
                        pe.sem_inc(rep_free, 1)
                        pe.wait_ge(blocks_done, b + 1)
                        return
                    for name in ("L1_Wk", "L1_Wv"):
                        for q in range(2):
                            o = bank()
                            for n in range(4):
                                for k in range(KD):
                                    m = 4 * q + n
                                    mm = nc.tensor.matmul(o[:, n * NC:(n + 1) * NC], w[name][:, k, m * P:(m + 1) * P],
                                                          ctx_rep[:, k, 0:NC], start=(k == 0), stop=(k == KD - 1))
                            mm.then_inc(ring_full, 1)
                    pe.sem_inc(rep_free, 1)
                    pe.wait_ge(pairs_done, b + 1)
                    for name, pair in (("L1_WqT", kpair), ("L1_Wo1", vpair)):
                        for dh in range(KD):
                            for group in ((0, 1, 2), (3, 4, 5), (6, 7)):
                                o = bank()
                                for n, m in enumerate(group):
                                    mm = nc.tensor.matmul(o[:, n * 2 * NC:(n + 1) * 2 * NC], w[name][:, m, dh * P:(dh + 1) * P],
                                                          pair[:, m, :, :].rearrange("p a k -> p (a k)"), start=True, stop=True)
                                mm.then_inc(ring_full, 1)
                    drained()
                    for hf in range(2):
                        for group in ((0, 1), (2, 3), (4,)):
                            o = bank()
                            for n, c in enumerate(group):
                                for dh in range(KD):
                                    mm = nc.tensor.transpose(o[0:rows(c), n * D + dh * P:n * D + (dh + 1) * P],
                                                             vfoldT[:, dh, hf * HK + c * P:hf * HK + c * P + rows(c)], chip.ident[:])
                            mm.then_inc(ring_full, 1)
                    drained()

                def front(j):
                    g = 2 * b + j
                    pe.wait_ge(xn_done, (16 if kind == "L2" else 4) * (g + 1))
                    for dh in range(KD):
                        o = bank()
                        for i in range(CH):
                            mm = nc.tensor.transpose(o[:, i * P:(i + 1) * P], xn[:, i, dh * P:(dh + 1) * P], chip.ident[:])
                        mm.then_inc(ring_full, 1)
                    drained()
                    pe.sem_inc(xn_free, 1)
                    if fold:
                        return
                    for m in range(2):
                        o = bank()
                        for k in range(KD):
                            mm = nc.tensor.matmul(o[:], w[f"{kind}_Wq"][:, k, m * P:(m + 1) * P], xT[:, j if fold else 0, k, :],
                                                  start=(k == 0), stop=(k == KD - 1))
                        mm.then_inc(ring_full, 1)
                    at["front", j] = stepfree.k

                def scores(j, u):
                    U = 2 * UN * b + UN * j + u
                    i, hf = u // 2, u % 2
                    if not fold and u == 0:
                        pe.wait_ge(ring_free, stepfree.base + 2 + at["front", j])
                    pe.wait_ge(shifted, U + 1)
                    for a in range(2):
                        if fold:
                            for k in range(KD):
                                mm = nc.tensor.matmul(S_ps[u % 2][:, a, 0:BK], xT[:, j if fold else 0, k, i * P:(i + 1) * P],
                                                      kfold[:, k, hf * HK + a * BK:hf * HK + (a + 1) * BK],
                                                      start=(k == 0), stop=(k == KD - 1))
                        else:
                            mm = nc.tensor.matmul(S_ps[u % 2][:, a, 0:BK], qT[:, j, hf, i * P:(i + 1) * P],
                                                  kblk[:, hf, 4 * a:4 * a + 4, :].rearrange("p h k -> p (h k)"),
                                                  start=True, stop=True)
                    mm.then_inc(s_full, 1)

                def turn(j, u):
                    U = 2 * UN * b + UN * j + u
                    pe.wait_ge(p_done, U + 1)
                    pe.wait_ge(t_free, U + 1)
                    for c in range(KCH):
                        mm = nc.tensor.transpose(T_ps[0:rows(c), c * P:(c + 1) * P], prob[:, u % PBUF, c * P:c * P + rows(c)],
                                                 chip.ident[:])
                    mm.then_inc(t_full, 1)

                def out(j, piece):
                    g = 2 * b + j
                    if piece == 2:
                        drained()
                    o = bank()
                    if piece < 2:
                        pe.wait_ge(t_free, 1 + UN * (g + 1))
                        if fold:
                            for r in range(2 * KCH):
                                hf, c = r // KCH, r % KCH
                                mm = nc.tensor.matmul(o[:], vrow[0:rows(c), r, piece * P:(piece + 1) * P],
                                                      probT[0:rows(c), j, hf, c, :], start=(r == 0), stop=(r == 2 * KCH - 1))
                        else:
                            for c in range(KCH):
                                mm = nc.tensor.matmul(o[:], vrow[0:rows(c), piece, c, :], probT[0:rows(c), j, piece, c, :],
                                                      start=(c == 0), stop=(c == KCH - 1))
                        mm.then_inc(ring_full, 1)
                        return
                    i = piece - 2
                    for k in range(KD):
                        mm = nc.tensor.matmul(o[:, 0:D], oT[:, k, i * P:(i + 1) * P], w[f"{kind}_Wo"][:, k, :],
                                              start=(k == 0), stop=(k == KD - 1))
                    mm.then_inc(ring_full, 1)
                    at["res", j] = stepfree.k
                    if kind == "L2" and piece == 5:
                        pe.wait_ge(c_done, g + 1)
                        for dh in range(KD):
                            o = bank()
                            for i in range(CH):
                                mm = nc.tensor.transpose(o[:, i * P:(i + 1) * P], cn[:, i, dh * P:(dh + 1) * P], chip.ident[:])
                            mm.then_inc(ring_full, 1)
                        drained()
                        for i in range(CH):
                            o = bank()
                            for k in range(KD):
                                mm = nc.tensor.matmul(o[:, 0:D], cT[:, k, i * P:(i + 1) * P], w["L2_Wf"][:, k, :],
                                                      start=(k == 0), stop=(k == KD - 1))
                            mm.then_inc(ring_full, 1)
                        at["f", j] = stepfree.k

                setup()
                walk(front, scores, turn, out)
                pe.sem_inc(blocks_free, 1)
                assert stepfree.k == RINGS, stepfree.k

        @block.scalar
        def _(act):
            full = Count(ring_full)
            act.sem_inc(ring_free, 2)
            act.sem_inc(t_free, 1)

            def filled():
                act.wait_ge(ring_full, full.up())
                return R_ps[(full.k - 1) % 2]

            with act.Fori(0, B) as b:
                full.enter(b * RINGS)

                def setup():
                    if not fold:
                        for m in range(2):
                            o = filled()
                            if L == 0:
                                nc.scalar.activation(kT[:, m, :], o[:, 0:NC], ACT.Identity,
                                                     bias=chip.col("L0_xattn_bk")[:, m:m + 1]).then_inc(ring_free, 1)
                            else:
                                nc.scalar.activation(kT[:, m, :], o[:, 0:NC], ACT.Copy).then_inc(ring_free, 1)
                        for hf in range(2):
                            o = filled()
                            nc.scalar.activation(vraw[:, hf, 0:KCH - 1, :].rearrange("p c d -> p (c d)"), o[:],
                                                 ACT.Copy).then_inc(ring_free, 1)
                            o = filled()
                            nc.scalar.activation(vraw[0:KLAST, hf, KCH - 1, :], o[0:KLAST, 0:P],
                                                 ACT.Copy).then_inc(ring_free, 1)
                        return

                    def copy(dst, src):
                        nc.scalar.activation(dst, src, ACT.Copy).then_inc(ring_free, 1)

                    for dst in (kT, vT):
                        for q in range(2):
                            o = filled()
                            copy(dst[:, 4 * q:4 * q + 4, :].rearrange("p m k -> p (m k)"), o[:, 0:4 * NC])
                    for dst in (kfold, vfoldT):
                        for dh in range(KD):
                            for group in ((0, 1, 2), (3, 4, 5), (6, 7)):
                                o = filled()
                                copy(dst[:, dh, group[0] * 2 * NC:(group[-1] + 1) * 2 * NC], o[:, 0:len(group) * 2 * NC])
                    for hf in range(2):
                        for group in ((0, 1), (2, 3), (4,)):
                            o = filled()
                            r = rows(group[-1])
                            copy(vrow[0:r, hf * KCH + group[0]:hf * KCH + group[-1] + 1, :].rearrange("p c d -> p (c d)"),
                                 o[0:r, 0:len(group) * D])

                def evacuate(dst, o, func=ACT.Copy, **kw):
                    nc.scalar.activation(dst, o, func, **kw).then_inc(ring_free, 1)

                def front(j):
                    for dh in range(KD):
                        evacuate(xT[:, j if fold else 0, dh, :], filled()[:])
                    if not fold:
                        for m in range(2):
                            if L == 0:
                                evacuate(qT[:, j, m, :], filled()[:], ACT.Identity, bias=chip.col("L0_xattn_bq")[:, m:m + 1])
                            else:
                                evacuate(qT[:, j, m, :], filled()[:])

                def unit(j, u):
                    U = 2 * UN * b + UN * j + u
                    act.wait_ge(shifted, U + 3)
                    nc.scalar.activation(prob[:, u % PBUF, :], prob[:, u % PBUF, :], ACT.Exp, scale=scale).then_inc(exp_done, 1)

                def turn(j, u):
                    U = 2 * UN * b + UN * j + u
                    i, hf = u // 2, u % 2
                    act.wait_ge(t_full, U + 1 + PBUF)
                    nc.scalar.activation(probT[:, j, hf, 0:KCH - 1, i * P:(i + 1) * P],
                                         T_ps[:, 0:(KCH - 1) * P].rearrange("p (c t) -> p c t", t=P), ACT.Copy)
                    nc.scalar.activation(probT[0:KLAST, j, hf, KCH - 1, i * P:(i + 1) * P],
                                         T_ps[0:KLAST, (KCH - 1) * P:KCH * P], ACT.Copy).then_inc(t_free, 1)

                def out(j, piece):
                    g = 2 * b + j
                    if piece < 2:
                        evacuate(oT[:, piece, :], filled()[:], ACT.Relu if fold else ACT.Copy)
                        return
                    if piece == 2:
                        act.wait_ge(x_done, g + 1)
                    evacuate(res[:, piece - 2, :], filled()[:, 0:D])
                    if kind == "L2" and piece == 5:
                        for dh in range(KD):
                            evacuate(cT[:, dh, :], filled()[:])
                        for i in range(CH):
                            evacuate(fo[:, i, :], filled()[:, 0:D])

                setup()
                walk(front, unit, turn, out)
                assert full.k == RINGS, full.k

        @block.vector
        def _(dve):
            step = Count(dve_step)

            def link(ins):
                ins.then_inc(dve_step, 1)
                dve.wait_ge(dve_step, step.up())

            dve.sem_inc(shifted, 2)
            if L == 0:
                dve.sem_inc(mask_used, 1)
                link(nc.vector.memset(floor[:], -1e9 / scale))
                dve.wait_ge(chip.loaded, N_LOADED)
            first = step.k
            per = {"L0": 51, "L1": 36, "L2": 38}[kind]
            with dve.Fori(0, B) as b:
                step.enter(b * per + first)

                def stats(j):
                    g = 2 * b + j
                    for i in range(CH):
                        ins = nc.vector.bn_stats(stat[:, j, i, :], chip.x[:, bass.ds((4 * g + i) * D, D)])
                    link(ins)
                    chip.settle(dve)
                    for i in range(CH):
                        ins = nc.vector.bn_aggr(mv[:, j, i, :], stat[:, j, i, :])
                    ins.then_inc(stats_done, 1)

                def front(j):
                    g = 2 * b + j
                    if kind == "L2":
                        return
                    dve.wait_ge(rstd_done, g + 1)
                    for i in range(CH):
                        nc.vector.tensor_scalar(xn[:, i, :], chip.x[:, bass.ds((4 * g + i) * D, D)], mv[:, j, i, 0:1],
                                                rs[:, j, i:i + 1], ALU.subtract, ALU.mult).then_inc(xn_done, 1)

                def unit(j, u):
                    U = 2 * UN * b + UN * j + u
                    dve.wait_ge(s_full, U + 1)
                    s = s_view(u)
                    shape = [P, 2, 4, NC]
                    if L == 0:
                        i = CH * j + u // 2
                        chip.settle(dve)
                        link(nc.vector.copy_predicated(s, wide(unmask[:, i, :].unsqueeze(1).unsqueeze(1), shape),
                                                       wide(floor[:].unsqueeze(1).unsqueeze(1), shape)))
                    m = mx[:, u % 2, :].rearrange("p (a h) -> p a h", a=2)
                    link(nc.vector.tensor_reduce(m, s, AX.X, ALU.max))
                    dve.wait_ge(t_full, U + 1)
                    nc.vector.tensor_tensor(p_view(u), s, wide(m.unsqueeze(3), shape), ALU.subtract).then_inc(shifted, 1)

                def total(j, u):
                    U = 2 * UN * b + UN * j + u
                    dve.wait_ge(exp_done, U + 1)
                    link(nc.vector.tensor_reduce(sm[:, u % 4, :], prob[:, u % PBUF, :].rearrange("p (h k) -> p h k", k=NC),
                                                 AX.X, ALU.add))
                    nc.vector.reciprocal(rc[:, u % 4, :], sm[:, u % 4, :]).then_inc(inv_done, 1)

                def norm2(j, n, src):
                    g = 2 * b + j
                    for i in range(CH):
                        ins = nc.vector.bn_stats(stat2[:, i, :], src[:, i, :])
                    link(ins)
                    chip.settle(dve)
                    for i in range(CH):
                        ins = nc.vector.bn_aggr(mv2[:, i, :], stat2[:, i, :])
                    ins.then_inc(stats2_done, 1)
                    k = (2 if kind == "L2" else 1) * g + n + 1
                    dve.wait_ge(rstd2_done, k)
                    for i in range(CH):
                        ins = nc.vector.tensor_scalar(src[:, i, :], src[:, i, :], mv2[:, i, 0:1], rs2[:, i:i + 1],
                                                      ALU.subtract, ALU.mult)
                    ins.then_inc(norm2_done, 1)

                def out(j, piece):
                    g = 2 * b + j
                    if kind == "L1" and piece == 5:
                        dve.wait_ge(ring_free, b * RINGS + 2 + at["res", j])
                        norm2(j, 0, res)
                    if kind == "L2" and piece == 5:
                        dve.wait_ge(relu_done, g + 1)
                        norm2(j, 0, res)
                        dve.wait_ge(f_sum, g + 1)
                        link(nc.vector.scalar_tensor_tensor(out=fo[:], in0=fo[:], scalar=0.0, in1=cn[:], op0=ALU.max, op1=ALU.add))
                        norm2(j, 1, fo)

                if L == 0:
                    dve.wait_ge(mask_in, 16 * (b + 1))
                    link(nc.vector.tensor_scalar(unmask[:], mask_i[:], 0.0, None, ALU.is_equal))
                    dve.sem_inc(mask_used, 1)
                if kind != "L2":
                    stats(0)
                    stats(1)
                walk(front, unit, total, out, lag=1)
                assert step.k == per, (kind, step.k)

        @block.gpsimd
        def _(pool):
            step = Count(pool_step)

            def link(ins):
                ins.then_inc(pool_step, 1)
                pool.wait_ge(pool_step, step.up())

            pool.sem_inc(x_done, 1)
            if L == 0:
                pool.wait_ge(chip.loaded, N_LOADED)
                link(nc.gpsimd.tensor_scalar(gvec[:, 0:D], chip.vec("L0_xattn_bo"), 1.0, gate, ALU.mult, ALU.mult))
            elif L == 1:
                link(nc.gpsimd.tensor_scalar(gvec[:, 0:D], chip.vec("L1_xattn_gamma"), 1.0, gate, ALU.mult, ALU.mult))
            else:
                link(nc.gpsimd.tensor_scalar(gvec[:, 0:D], chip.vec("L2_xattn_g3"), 1.0, gate, ALU.mult, ALU.mult))
                link(nc.gpsimd.tensor_scalar(gvec[:, D:], chip.vec("L2_xattn_b3"), 1.0, gate, ALU.mult, ALU.mult))
            first = step.k
            per = {"L0": 10, "L1": 6, "L2": 12}[kind]
            with pool.Fori(0, B) as b:
                step.enter(b * per + first)

                def rstd(j):
                    g = 2 * b + j
                    pool.wait_ge(stats_done, g + 1)
                    chip.settle(pool)
                    link(nc.gpsimd.tensor_scalar(ve[:, j, :], mv[:, j, :, 1], 1e-5, None, ALU.add))
                    nc.gpsimd.tensor_tensor(rs[:, j, :], ve[:, j, :], chip.neghalf[:, 0:CH], ALU.pow).then_inc(rstd_done, 1)

                def rstd2(k, eps):
                    pool.wait_ge(stats2_done, k)
                    chip.settle(pool)
                    link(nc.gpsimd.tensor_scalar(ve2[:], mv2[:, :, 1], eps, None, ALU.add))
                    nc.gpsimd.tensor_tensor(rs2[:], ve2[:], chip.neghalf[:, 0:CH], ALU.pow).then_inc(rstd2_done, 1)

                def setup():
                    pool.wait_ge(rep_free, b + 1)
                    ins = nc.gpsimd.tensor_copy(ctx_rep[:].rearrange("p c (h k) -> p c h k", k=NC),
                                                wide(chip.ctxT[:, :, bass.ds(b * NC, NC)].unsqueeze(2), [P, KD, HH, NC]))
                    ins.then_inc(rep_done, 1)
                    if fold:
                        pool.wait_ge(ring_free, b * RINGS + 6)
                        for n, (pair, t) in enumerate(((kpair, kT), (vpair, vT))):
                            ins = nc.gpsimd.tensor_tensor(pair[:], wide(t.unsqueeze(2), [P, HH, 2, NC]),
                                                          wide(chip.headmask[:, 8:10].unsqueeze(1).unsqueeze(3), [P, HH, 2, NC]),
                                                          ALU.mult)
                        ins.then_inc(pairs_done, 1)
                        return
                    pool.wait_ge(ring_free, b * RINGS + 8)
                    pool.wait_ge(blocks_free, b + 1)
                    for m in range(2):
                        nc.gpsimd.tensor_tensor(kblk[:, m], wide(kT[:, m, :].unsqueeze(1), [P, HH, NC]),
                                                wide(chip.headmask[:, 0:HH].unsqueeze(2), [P, HH, NC]), ALU.mult)
                    for hf in range(2):
                        for r, cs in ((P, slice(0, KCH - 1)), (KLAST, slice(KCH - 1, KCH))):
                            n = cs.stop - cs.start
                            src = vraw[0:r, hf, cs, :]
                            if L == 0:
                                link(nc.gpsimd.tensor_tensor(src, src, wide(chip.vec("L0_xattn_bv")[0:r, hf * P:(hf + 1) * P].unsqueeze(1),
                                                                            [r, n, P]), ALU.add))
                            ins = nc.gpsimd.tensor_tensor(vrow[0:r, hf, cs, :], src, chip.rowmask[0:r, cs, :], ALU.mult)
                    ins.then_inc(blocks_done, 1)

                def front(j):
                    pass

                def nothing(j, u):
                    pass

                def divide(j, u):
                    U = 2 * UN * b + UN * j + u
                    pool.wait_ge(inv_done, U + 1)
                    nc.gpsimd.tensor_tensor(prob[:, u % PBUF, :].rearrange("p (h k) -> p h k", k=NC),
                                            prob[:, u % PBUF, :].rearrange("p (h k) -> p h k", k=NC),
                                            wide(rc[:, u % 4, :].unsqueeze(2), [P, HH, NC]), ALU.mult).then_inc(p_done, 1)

                def out(j, piece):
                    if piece != 5:
                        return
                    g = 2 * b + j
                    r = res[:]
                    x = chip.x[:, bass.ds(4 * g * D, CH * D)].rearrange("p (i d) -> p i d", d=D)
                    full = [P, CH, D]

                    def bc(v):
                        return wide(v.unsqueeze(1), full)

                    if kind == "L0":
                        pool.wait_ge(ring_free, b * RINGS + 2 + at["res", j])
                        chip.settle(pool)
                        link(nc.gpsimd.tensor_scalar(r, r, 1.0, gate, ALU.mult, ALU.mult))
                        link(nc.gpsimd.tensor_tensor(r, r, bc(gvec[:, 0:D]), ALU.add))
                    if kind == "L1":
                        rstd2(g + 1, 1e-5)
                        pool.wait_ge(norm2_done, g + 1)
                        link(nc.gpsimd.tensor_tensor(r, r, bc(gvec[:, 0:D]), ALU.mult))
                    if kind == "L2":
                        pool.wait_ge(ring_free, b * RINGS + 2 + at["res", j])
                        link(nc.gpsimd.tensor_tensor(r, r, bc(chip.vec("L2_xattn_bo2")), ALU.add))
                        chip.settle(pool)
                        nc.gpsimd.tensor_scalar(r, r, 0.0, 2.0, ALU.max, ALU.mult).then_inc(relu_done, 1)
                        rstd2(2 * g + 1, 1e-6)
                        pool.wait_ge(norm2_done, 2 * g + 1)
                        link(nc.gpsimd.tensor_tensor(r, r, bc(chip.vec("L2_xattn_g2")), ALU.mult))
                        nc.gpsimd.tensor_tensor(cn[:], r, bc(chip.vec("L2_xattn_b2")), ALU.add).then_inc(c_done, 1)
                        pool.wait_ge(ring_free, b * RINGS + 2 + at["f", j])
                        pool.wait_ge(c_done, g + 1)
                        nc.gpsimd.tensor_tensor(fo[:], fo[:], bc(chip.vec("L2_xattn_bf")), ALU.add).then_inc(f_sum, 1)
                        rstd2(2 * g + 2, 1e-6)
                        pool.wait_ge(norm2_done, 2 * g + 2)
                        link(nc.gpsimd.tensor_tensor(r, fo[:], bc(gvec[:, 0:D]), ALU.mult))
                        link(nc.gpsimd.tensor_tensor(r, r, bc(gvec[:, D:]), ALU.add))
                    nc.gpsimd.tensor_tensor(x, x, r, ALU.add).then_inc(x_done, 1)
                    pool.wait_ge(x_done, g + 2)

                if kind != "L2":
                    rstd(0)
                    rstd(1)
                setup()
                walk(front, nothing, divide, out, lag=1)
                assert step.k == per, (kind, step.k)


def pipelined(eng, phases, n=T, unroll=2):
    depth = len(phases) - 1
    lead = depth + (-depth) % unroll

    def step(s, static):
        for k, phase in enumerate(phases):
            t = s - k
            if static:
                if 0 <= t < n:
                    phase(t, t % unroll)
            else:
                phase(t, (static_of[0] - k) % unroll)

    for s in range(lead):
        step(s, True)
    loops = (n - lead) // unroll
    static_of = [0]
    with eng.Fori(0, loops) as it:
        for r in range(unroll):
            static_of[0] = r + lead
            step(it * unroll + (lead + r), False)
    for s in range(lead + loops * unroll, n + depth):
        step(s, True)


class Links:

    def __init__(self, eng, sem, per, n=T, start=0):
        self.eng, self.sem, self.per, self.n, self.start = eng, sem, per, n, start
        self.value = start

    def enter(self, phase, t):
        clamp = (lambda v: max(0, min(v, self.n))) if isinstance(t, int) else (lambda v: v)
        done = sum(m * clamp(t + (phase - i) + (1 if i < phase else 0)) for i, m in enumerate(self.per) if m)
        self.value, self.k, self.expect = done + self.start, 0, self.per[phase]

    def __call__(self, ins):
        self.k += 1
        ins.then_inc(self.sem, 1)
        self.eng.wait_ge(self.sem, self.value + self.k)

    def leave(self):
        assert self.k == self.expect, (self.k, self.expect)


def tile_of(chip, t):
    return chip.x[:, bass.ds(t * D, D)]


def experts_stage(chip, dram):
    nc, w = chip.nc, chip.w
    NE, R = 32, 512
    RK = R // P
    gate = chip.gates[:, B:B + 1]
    with ExitStack() as ctx:
        def sb(name, shape, dt=F32):
            return ctx.enter_context(nc.sbuf_tensor(f"L0F_{name}", shape, dt))

        def sem(name):
            return ctx.enter_context(nc.semaphore(f"L0F_{name}"))

        def ps(name, shape):
            return ctx.enter_context(nc.psum_tensor(f"L0F_{name}", shape, F32))

        xT_ps, d_ps, o_ps = ps("xT_ps", [P, 512]), ps("d_ps", [P, 512]), ps("o_ps", [P, 512])
        h_ps = [ps(f"h_ps{i}", [P, R]) for i in range(2)]
        hT_ps, gT_ps = ps("hT_ps", [P, 512]), ps("gT_ps", [NE, 512])
        stat, mv, ve, rs = sb("stat", [P, 2, 6]), sb("mv", [P, 2, 2]), sb("ve", [P, 2]), sb("rs", [P, 2])
        xn, xT = sb("xn", [P, 2, D]), sb("xT", [P, 2, KD, P])
        square, x2 = sb("square", [P, 2, D]), sb("x2", [P, 2])
        protosq, p2, tinv = sb("protosq", [P, KD, NE]), sb("p2", [P, NE]), sb("tinv", [P, 1])
        dist = sb("dist", [P, 2, NE])
        top, idx, idxf = sb("top", [P, 2, 8]), sb("idx", [P, 2, 8], U32), sb("idxf", [P, 2, 2])
        e2, g1, g2 = sb("e2", [P, 2]), sb("g1", [P, 2]), sb("g2", [P, 2])
        near = sb("near", [P, 2, 2])
        G, Gb = sb("G", [P, 2, NE]), sb("Gb", [P, 2, NE])
        hg, hT, gT, res = sb("hg", [P, 2, R]), sb("hT", [P, 2, RK, P]), sb("gT", [NE, 2, P]), sb("res", [P, 2, D])
        names = """stats_done rstd_done xn_done xT_full xT_free d_full d_free h_full hg_done hT_full hT_free
            gT_full gT_free o_full o_free sc_done top_done near_done e2_done G_done x_done x2_done dve_step pool_step act_step pe_pre pre temp_in""".split()
        s = {n: sem(n) for n in names}
        block = ctx.enter_context(nc.Block())

        @block.sync
        def _(sp):
            sp.dma_start(tinv[:], dram["L0F_temp"].partition_broadcast(P)).then_inc(s["temp_in"], 16)

        @block.tensor
        def _(pe):
            for name in WEIGHTS["L0F"]:
                pe.wait_ge(chip.w_in[name], 16)
            pe.wait_ge(s["pre"], 1)
            for k in range(KD):
                mm = nc.tensor.matmul(d_ps[:, 0:NE], chip.ones[:], protosq[:, k, :], start=(k == 0), stop=(k == KD - 1))
            mm.then_inc(s["pe_pre"], 1)

            def turn_x(t, p):
                pe.wait_ge(s["xn_done"], t + 1)
                pe.wait_ge(s["xT_free"], t + 1)
                for k in range(KD):
                    mm = nc.tensor.transpose(xT_ps[:, k * P:(k + 1) * P], xn[:, p, k * P:(k + 1) * P], chip.ident[:])
                mm.then_inc(s["xT_full"], 1)

            def project(t, p):
                pe.wait_ge(s["xT_free"], t + 2)
                pe.wait_ge(s["d_free"], t + 1)
                for k in range(KD):
                    mm = nc.tensor.matmul(d_ps[:, 0:NE], xT[:, p, k, :], w["L0F_protoT"][:, k, :], start=(k == 0), stop=(k == KD - 1))
                mm.then_inc(s["d_full"], 1)
                pe.wait_ge(s["hg_done"], t + 1)
                for k in range(KD):
                    mm = nc.tensor.matmul(h_ps[p][:], xT[:, p, k, :], w["L0F_BT"][:, k, :], start=(k == 0), stop=(k == KD - 1))
                mm.then_inc(s["h_full"], 1)

            def turn_h(t, p):
                pe.wait_ge(s["hg_done"], t + 3)
                pe.wait_ge(s["hT_free"], t + 1)
                for k in range(RK):
                    mm = nc.tensor.transpose(hT_ps[:, k * P:(k + 1) * P], hg[:, p, k * P:(k + 1) * P], chip.ident[:])
                mm.then_inc(s["hT_full"], 1)
                pe.wait_ge(s["gT_free"], t + 1)
                nc.tensor.transpose(gT_ps[:, 0:P], G[:, p, :], chip.ident[:]).then_inc(s["gT_full"], 1)

            def expand(t, p):
                pe.wait_ge(s["hT_free"], t + 2)
                pe.wait_ge(s["gT_free"], t + 2)
                pe.wait_ge(s["o_free"], t + 1)
                for k in range(RK):
                    nc.tensor.matmul(o_ps[:, 0:D], hT[:, p, k, :], w["L0F_A"][:, k, :], start=(k == 0), stop=False)
                nc.tensor.matmul(o_ps[:, 0:D], gT[:, p, :], w["L0F_bias"], start=False, stop=True).then_inc(s["o_full"], 1)

            none = lambda t, p: None
            pipelined(pe, [none, turn_x, project, none, turn_h, expand])

        @block.scalar
        def _(act):
            for n in ("xT_free", "d_free", "hT_free", "gT_free", "o_free"):
                act.sem_inc(s[n], 1)

            def copy_x(t, p):
                act.wait_ge(s["xn_done"], t + 1)
                act.wait_ge(s["sc_done"], t + 1)
                nc.scalar.activation(square[:, p, :], xn[:, p, :], ACT.Square, accum_out=x2[:, p:p + 1])
                act.wait_ge(s["xT_full"], t + 1)
                nc.scalar.activation(xT[:, p, :, :].rearrange("p k t -> p (k t)"), xT_ps[:, 0:D], ACT.Copy).then_inc(s["xT_free"], 1)

            def distance(t, p):
                act.wait_ge(s["d_full"], t + 1)
                act.wait_ge(s["G_done"], t + 1)
                nc.scalar.activation(dist[:, p, :], d_ps[:, 0:NE], ACT.Copy, scale=2.0).then_inc(s["d_free"], 1)

            def ratio(t, p):
                act.wait_ge(s["near_done"], t + 1)
                nc.scalar.activation(e2[:, p:p + 1], near[:, p, 0:1], ACT.Exp, bias=near[:, p, 1:2], scale=-1.0).then_inc(s["e2_done"], 1)

            def copy_h(t, p):
                act.wait_ge(s["hT_full"], t + 1)
                nc.scalar.activation(hT[:, p, :, :].rearrange("p k t -> p (k t)"), hT_ps[:], ACT.Copy).then_inc(s["hT_free"], 1)
                act.wait_ge(s["gT_full"], t + 1)
                nc.scalar.activation(gT[:, p, :], gT_ps[:, 0:P], ACT.Copy).then_inc(s["gT_free"], 1)

            def result(t, p):
                act.wait_ge(s["o_full"], t + 1)
                act.wait_ge(s["x_done"], t + 1)
                nc.scalar.activation(res[:, p, :], o_ps[:, 0:D], ACT.Identity, scale=gate).then_inc(s["o_free"], 1)

            none = lambda t, p: None
            pipelined(act, [none, copy_x, distance, ratio, copy_h, result])

        @block.vector
        def _(dve):
            link = Links(dve, s["dve_step"], [1, 0, 2, 5, 0, 0])
            link.start, link.k, link.value = 4, 0, 0
            dve.wait_ge(chip.w_in["L0F_protoT"], 16)
            nc.vector.tensor_tensor(protosq[:], w["L0F_protoT"], w["L0F_protoT"], ALU.mult).then_inc(s["pre"], 1)
            dve.wait_ge(s["temp_in"], 16)
            link(nc.vector.tensor_scalar(p2[:, 0:1], tinv[:], -1.0, 0.1, ALU.mult, ALU.max))
            link(nc.vector.tensor_tensor(tinv[:], tinv[:], p2[:, 0:1], ALU.max))
            link(nc.vector.reciprocal(tinv[:], tinv[:]))
            link(nc.vector.tensor_scalar(tinv[:], tinv[:], -1.0, None, ALU.mult))
            dve.wait_ge(s["pe_pre"], 1)
            nc.vector.tensor_copy(p2[:], d_ps[:, 0:NE]).then_inc(s["pre"], 1)
            dve.sem_inc(s["hg_done"], 2)
            dve.sem_inc(s["G_done"], 2)

            def stats(t, p):
                link.enter(0, t)
                link(nc.vector.bn_stats(stat[:, p, :], tile_of(chip, t)))
                chip.settle(dve)
                nc.vector.bn_aggr(mv[:, p, :], stat[:, p, :]).then_inc(s["stats_done"], 1)
                link.leave()

            def normalise(t, p):
                dve.wait_ge(s["rstd_done"], t + 1)
                nc.vector.tensor_scalar(xn[:, p, :], tile_of(chip, t), mv[:, p, 0:1], rs[:, p:p + 1],
                                        ALU.subtract, ALU.mult).then_inc(s["xn_done"], 1)

            def pick(t, p):
                link.enter(2, t)
                dve.wait_ge(s["sc_done"], t + 3)
                chip.settle(dve)
                link(nc.vector.max(top[:, p, :], dist[:, p, :]))
                chip.settle(dve)
                link(nc.vector.max_index(idx[:, p, :], top[:, p, :], dist[:, p, :]))
                nc.vector.tensor_copy(idxf[:, p, :], idx[:, p, 0:2]).then_inc(s["top_done"], 1)
                link.leave()

            def weigh(t, p):
                link.enter(3, t)
                dve.wait_ge(s["top_done"], t + 1)
                dve.wait_ge(s["e2_done"], t + 1)
                link(nc.vector.tensor_scalar(g1[:, p:p + 1], e2[:, p:p + 1], 1.0, None, ALU.add))
                link(nc.vector.reciprocal(g1[:, p:p + 1], g1[:, p:p + 1]))
                link(nc.vector.tensor_tensor(g2[:, p:p + 1], g1[:, p:p + 1], e2[:, p:p + 1], ALU.mult))
                nc.vector.tensor_scalar(G[:, p, :], chip.iota[:], idxf[:, p, 0:1], g1[:, p:p + 1], ALU.is_equal, ALU.mult)
                link(nc.vector.tensor_scalar(Gb[:, p, :], chip.iota[:], idxf[:, p, 1:2], g2[:, p:p + 1], ALU.is_equal, ALU.mult))
                link(nc.vector.tensor_tensor(G[:, p, :], G[:, p, :], Gb[:, p, :], ALU.add))
                dve.sem_inc(s["G_done"], 1)
                dve.wait_ge(s["h_full"], t + 1)
                nc.vector.tensor_tensor(hg[:, p, :].rearrange("p (e r) -> p e r", e=NE), h_ps[p][:].rearrange("p (e r) -> p e r", e=NE),
                                        wide(G[:, p, :].unsqueeze(2), [P, NE, R // NE]), ALU.mult).then_inc(s["hg_done"], 1)
                link.leave()

            none = lambda t, p: None
            pipelined(dve, [stats, normalise, pick, weigh, none, none])

        @block.gpsimd
        def _(pool):
            link = Links(pool, s["pool_step"], [1, 0, 2, 2, 0, 0])
            pool.sem_inc(s["x_done"], 2)
            pool.sem_inc(s["sc_done"], 2)
            pool.wait_ge(s["pre"], 2)

            def rstd(t, p):
                link.enter(0, t)
                pool.wait_ge(s["stats_done"], t + 1)
                chip.settle(pool)
                link(nc.gpsimd.tensor_scalar(ve[:, p:p + 1], mv[:, p, 1:2], 1e-5, None, ALU.add))
                nc.gpsimd.tensor_tensor(rs[:, p:p + 1], ve[:, p:p + 1], chip.neghalf[:, 0:1], ALU.pow).then_inc(s["rstd_done"], 1)
                link.leave()

            def score(t, p):
                link.enter(2, t)
                d = dist[:, p, :]
                pool.wait_ge(s["d_free"], t + 2)
                chip.settle(pool)
                link(nc.gpsimd.tensor_scalar(d, d, x2[:, p:p + 1], None, ALU.subtract))
                link(nc.gpsimd.tensor_tensor(d, d, p2[:], ALU.subtract))
                chip.settle(pool)
                nc.gpsimd.tensor_scalar(d, d, 0.0, None, ALU.min).then_inc(s["sc_done"], 1)
                link.leave()

            def root(t, p):
                link.enter(3, t)
                pool.wait_ge(s["top_done"], t + 1)
                chip.settle(pool)
                link(nc.gpsimd.tensor_scalar(near[:, p, :], top[:, p, 0:2], -1.0, None, ALU.mult))
                link(nc.gpsimd.tensor_tensor(near[:, p, :], near[:, p, :], chip.half[:, 0:2], ALU.pow))
                nc.gpsimd.tensor_tensor(near[:, p, :], near[:, p, :], wide(tinv[:], [P, 2]), ALU.mult).then_inc(s["near_done"], 1)
                link.leave()

            def add(t, p):
                pool.wait_ge(s["o_free"], t + 2)
                nc.gpsimd.tensor_tensor(tile_of(chip, t), tile_of(chip, t), res[:, p, :], ALU.add).then_inc(s["x_done"], 1)

            none = lambda t, p: None
            pipelined(pool, [rstd, none, score, root, none, add])


ROUND = 1.5 * 2.0 ** 23


def ternary_stage(chip, dram):
    nc, w = chip.nc, chip.w
    INNER = 1024
    IK = INNER // P
    COUNT = float(D * INNER)
    gate = chip.gates[:, B + 1:B + 2]
    with ExitStack() as ctx:
        def sb(name, shape, dt=F32):
            return ctx.enter_context(nc.sbuf_tensor(f"L1F_{name}", shape, dt))

        def sem(name):
            return ctx.enter_context(nc.semaphore(f"L1F_{name}"))

        def ps(name, shape, dt=F32):
            return ctx.enter_context(nc.psum_tensor(f"L1F_{name}", shape, dt))

        g_ps, u_ps = ps("gate_ps", [P, INNER]), ps("up_ps", [P, INNER])
        xT_ps, hT_ps, o_ps = ps("xT_ps", [P, 1024], BF16), ps("hT_ps", [P, INNER], BF16), ps("o_ps", [P, 512])
        m_ps = ps("m_ps", [P, 512])
        identb = sb("identb", [P, P], BF16)
        tern = {"gate": sb("t_gate", [P, KD, INNER], BF16), "up": sb("t_up", [P, KD, INNER], BF16), "down": sb("t_down", [P, IK, D], BF16)}
        absw, rowsum = sb("absw", [P, 2048]), sb("rowsum", [P, 3])
        wmean, wscale = sb("wmean", [P, 3]), sb("wscale", [P, 3])
        stat, mv, ve, rs = sb("stat", [P, 2, 6]), sb("mv", [P, 2, 2]), sb("ve", [P, 2]), sb("rs", [P, 2])
        xn, xq, xqb, xT = sb("xn", [P, 2, D]), sb("xq", [P, 2, D]), sb("xqb", [P, 2, D], BF16), sb("xT", [P, 2, KD, P], BF16)
        am, ax, ix = sb("am", [P, 2]), sb("ax", [P, 4]), sb("ix", [P, 2])
        gs, us = sb("gs", [P, 4]), sb("us", [P, 4])
        h, hq, hqb, hT = sb("h", [P, 2, INNER]), sb("hq", [P, 2, INNER]), sb("hqb", [P, 2, INNER], BF16), sb("hT", [P, 2, IK, P], BF16)
        ah, ai, s2, ev = sb("ah", [P, 2]), sb("ai", [P, 2]), sb("s2", [P, 2]), sb("ev", [P, 4])
        minus1, res = sb("minus1", [P, 1]), sb("res", [P, 2, D])
        names = """pre abs_done mean_done tern_done stats_done rstd_done xn_done ix_done xq_done xT_full xT_free gu_full silu_done
            h_done ah_done s2_done hq_done hqb_done hT_full hT_free o_full o_free x_done dve_step pool_step act_step wmean_done""".split()
        s = {n: sem(n) for n in names}
        block = ctx.enter_context(nc.Block())
        order = ("gate", "up", "down")

        @block.sync
        def _(sp):
            chip.load(sp, WEIGHTS["L2S"] + WEIGHTS["L2"], dram)

        @block.tensor
        def _(pe):
            pe.sem_inc(s["xT_full"], 2)
            pe.sem_inc(s["hT_full"], 2)
            pe.wait_ge(s["abs_done"], 3)
            nc.tensor.matmul(m_ps[:, 0:3], chip.ones[:], rowsum[:], start=True, stop=True).then_inc(s["mean_done"], 1)
            pe.wait_ge(s["tern_done"], 4)

            def turn_x(t, q):
                p = q % 2
                pe.wait_ge(s["xq_done"], t + 1)
                pe.wait_ge(s["xT_free"], t + 1)
                for k in range(KD):
                    mm = nc.tensor.transpose(xT_ps[:, k * P:(k + 1) * P], xqb[:, p, k * P:(k + 1) * P], identb[:])
                mm.then_inc(s["xT_full"], 1)

            def widen(t, q):
                p = q % 2
                pe.wait_ge(s["xT_free"], t + 2)
                pe.wait_ge(s["h_done"], t + 1)
                for o, n in ((g_ps, "gate"), (u_ps, "up")):
                    for c in range(INNER // 512):
                        for k in range(KD):
                            mm = nc.tensor.matmul(o[:, c * 512:(c + 1) * 512], xT[:, p, k, :], tern[n][:, k, c * 512:(c + 1) * 512],
                                                  start=(k == 0), stop=(k == KD - 1))
                mm.then_inc(s["gu_full"], 1)

            def turn_h(t, q):
                p = q % 2
                pe.wait_ge(s["hqb_done"], t + 3)
                pe.wait_ge(s["hT_free"], t + 1)
                for k in range(IK):
                    mm = nc.tensor.transpose(hT_ps[:, k * P:(k + 1) * P], hqb[:, p, k * P:(k + 1) * P], identb[:])
                mm.then_inc(s["hT_full"], 1)

            def narrow(t, q):
                p = q % 2
                pe.wait_ge(s["hT_free"], t + 2)
                pe.wait_ge(s["o_free"], t + 1)
                for k in range(IK):
                    mm = nc.tensor.matmul(o_ps[:, 0:D], hT[:, p, k, :], tern["down"][:, k, :], start=(k == 0), stop=(k == IK - 1))
                mm.then_inc(s["o_full"], 1)

            none = lambda t, p: None
            pipelined(pe, [none, none, turn_x, widen, none, none, turn_h, narrow], unroll=4)

        @block.scalar
        def _(act):
            for n in ("xT_free", "hT_free", "o_free"):
                act.sem_inc(s[n], 1)
            act.sem_inc(s["hq_done"], 2)
            for n, name in enumerate(order):
                act.wait_ge(chip.w_in["L1F_" + name], 16)
                if n:
                    act.wait_ge(s["abs_done"], n)
                nc.scalar.activation(absw[:], w["L1F_" + name].rearrange("p a n -> p (a n)"), ACT.Abs,
                                     accum_out=rowsum[:, n:n + 1]).then_inc(s["abs_done"], 1)

            def copy_x(t, q):
                p = q % 2
                act.wait_ge(s["xT_full"], t + 3)
                nc.scalar.activation(xT[:, p, :, :].rearrange("p k t -> p (k t)"), xT_ps[:, 0:D], ACT.Copy).then_inc(s["xT_free"], 1)

            def silu(t, q):
                p = q % 2
                act.wait_ge(s["gu_full"], t + 1)
                act.wait_ge(s["ix_done"], t + 3)
                act.wait_ge(s["hq_done"], t + 1)
                nc.scalar.activation(h[:, p, :], g_ps[:], ACT.Silu, scale=gs[:, q:q + 1]).then_inc(s["silu_done"], 1)

            def quantise(t, q):
                p = q % 2
                act.wait_ge(s["s2_done"], t + 1)
                act.wait_ge(s["hqb_done"], t + 1)
                nc.scalar.activation(hq[:, p, :], h[:, p, :], ACT.Copy, scale=s2[:, p:p + 1], bias=ROUND).then_inc(s["hq_done"], 1)

            def copy_h(t, q):
                p = q % 2
                act.wait_ge(s["hT_full"], t + 3)
                nc.scalar.activation(hT[:, p, :, :].rearrange("p k t -> p (k t)"), hT_ps[:], ACT.Copy).then_inc(s["hT_free"], 1)

            def result(t, q):
                p = q % 2
                act.wait_ge(s["o_full"], t + 1)
                act.wait_ge(s["x_done"], t + 1)
                nc.scalar.activation(res[:, p, :], o_ps[:, 0:D], ACT.Identity, scale=ev[:, q:q + 1]).then_inc(s["o_free"], 1)

            none = lambda t, p: None
            pipelined(act, [none, none, copy_x, none, silu, quantise, copy_h, result], unroll=4)

        @block.vector
        def _(dve):
            link = Links(dve, s["dve_step"], [1, 1, 1, 0, 1, 0, 0, 0])
            link.k = 0
            link(nc.vector.tensor_copy(identb[:], chip.ident[:]))
            dve.wait_ge(s["mean_done"], 1)
            link(nc.vector.tensor_scalar(wmean[:], m_ps[:, 0:3], 1.0 / COUNT, 1e-5, ALU.mult, ALU.max))
            nc.vector.reciprocal(wscale[:], wmean[:]).then_inc(s["wmean_done"], 1)
            dve.wait_ge(s["wmean_done"], 1)
            for n, name in enumerate(order):
                dst = tern[name][:].rearrange("p a n -> p (a n)")
                link(nc.vector.tensor_scalar(absw[:], w["L1F_" + name].rearrange("p a n -> p (a n)"), wscale[:, n:n + 1], ROUND,
                                             ALU.mult, ALU.add))
                link(nc.vector.tensor_scalar(absw[:], absw[:], ROUND - 1.0, ROUND + 1.0, ALU.max, ALU.min))
                nc.vector.tensor_scalar(dst, absw[:], -ROUND, None, ALU.add).then_inc(s["tern_done"], 1)
                dve.wait_ge(s["tern_done"], n + 1)
            dve.sem_inc(s["tern_done"], 1)
            dve.sem_inc(s["h_done"], 1)
            dve.sem_inc(s["hqb_done"], 2)
            link.start = link.k

            def stats(t, q):
                p = q % 2
                link.enter(0, t)
                link(nc.vector.bn_stats(stat[:, p, :], tile_of(chip, t)))
                chip.settle(dve)
                nc.vector.bn_aggr(mv[:, p, :], stat[:, p, :]).then_inc(s["stats_done"], 1)
                link.leave()

            def normalise(t, q):
                p = q % 2
                link.enter(1, t)
                dve.wait_ge(s["rstd_done"], t + 1)
                link(nc.vector.tensor_scalar(xn[:, p, :], tile_of(chip, t), mv[:, p, 0:1], rs[:, p:p + 1], ALU.subtract, ALU.mult))
                nc.vector.tensor_reduce(am[:, p:p + 1], xn[:, p, :], AX.X, ALU.max, apply_absolute_value=True).then_inc(s["xn_done"], 1)
                link.leave()

            def quantise(t, q):
                p = q % 2
                link.enter(2, t)
                dve.wait_ge(s["ix_done"], t + 3)
                dve.wait_ge(s["xT_full"], t + 1)
                link(nc.vector.tensor_scalar(xq[:, p, :], xn[:, p, :], ix[:, p:p + 1], ROUND, ALU.mult, ALU.add))
                nc.vector.tensor_scalar(xqb[:, p, :], xq[:, p, :], ROUND + 127.0, -ROUND, ALU.min, ALU.add).then_inc(s["xq_done"], 1)
                link.leave()

            def multiply(t, q):
                p = q % 2
                link.enter(4, t)
                dve.wait_ge(s["silu_done"], t + 1)
                nc.vector.tensor_tensor(h[:, p, :], h[:, p, :], u_ps[:], ALU.mult).then_inc(s["h_done"], 1)
                dve.wait_ge(s["h_done"], t + 2)
                link(nc.vector.tensor_reduce(ah[:, p:p + 1], h[:, p, :], AX.X, ALU.max, apply_absolute_value=True))
                dve.sem_inc(s["ah_done"], 1)
                link.leave()

            def shift(t, q):
                p = q % 2
                dve.wait_ge(s["hq_done"], t + 3)
                dve.wait_ge(s["hT_full"], t + 1)
                nc.vector.tensor_scalar(hqb[:, p, :], hq[:, p, :], ROUND + 127.0, -ROUND, ALU.min, ALU.add).then_inc(s["hqb_done"], 1)

            none = lambda t, p: None
            pipelined(dve, [stats, normalise, quantise, none, multiply, shift, none, none], unroll=4)

        @block.gpsimd
        def _(pool):
            link = Links(pool, s["pool_step"], [1, 3, 0, 0, 5, 0, 0, 0])
            link.k = 0
            link(nc.gpsimd.memset(minus1[:], -1.0))
            pool.sem_inc(s["x_done"], 2)
            pool.sem_inc(s["ix_done"], 2)
            pool.wait_ge(s["wmean_done"], 1)
            link(nc.gpsimd.tensor_tensor(wmean[:, 2:3], wmean[:, 2:3], gate, ALU.mult))
            link.start = link.k

            def rstd(t, q):
                p = q % 2
                link.enter(0, t)
                pool.wait_ge(s["stats_done"], t + 1)
                chip.settle(pool)
                link(nc.gpsimd.tensor_scalar(ve[:, p:p + 1], mv[:, p, 1:2], 1e-5, None, ALU.add))
                nc.gpsimd.tensor_tensor(rs[:, p:p + 1], ve[:, p:p + 1], chip.neghalf[:, 0:1], ALU.pow).then_inc(s["rstd_done"], 1)
                link.leave()

            def scale_x(t, q):
                p = q % 2
                link.enter(1, t)
                pool.wait_ge(s["xn_done"], t + 1)
                chip.settle(pool)
                link(nc.gpsimd.tensor_scalar(ax[:, q:q + 1], am[:, p:p + 1], 1e-5, 1.0 / 127.0, ALU.max, ALU.mult))
                link(nc.gpsimd.tensor_tensor(gs[:, q:q + 1], ax[:, q:q + 1], wmean[:, 0:1], ALU.mult))
                link(nc.gpsimd.tensor_tensor(us[:, q:q + 1], ax[:, q:q + 1], wmean[:, 1:2], ALU.mult))
                nc.gpsimd.tensor_tensor(ix[:, p:p + 1], ax[:, q:q + 1], minus1[:], ALU.pow).then_inc(s["ix_done"], 1)
                link.leave()

            def scale_h(t, q):
                p = q % 2
                link.enter(4, t)
                pool.wait_ge(s["ah_done"], t + 1)
                link(nc.gpsimd.tensor_tensor(ah[:, p:p + 1], ah[:, p:p + 1], us[:, q:q + 1], ALU.mult))
                chip.settle(pool)
                link(nc.gpsimd.tensor_scalar(ah[:, p:p + 1], ah[:, p:p + 1], 1e-5, 1.0 / 127.0, ALU.max, ALU.mult))
                link(nc.gpsimd.tensor_tensor(ai[:, p:p + 1], ah[:, p:p + 1], minus1[:], ALU.pow))
                link(nc.gpsimd.tensor_tensor(ev[:, q:q + 1], ah[:, p:p + 1], wmean[:, 2:3], ALU.mult))
                link(nc.gpsimd.tensor_tensor(s2[:, p:p + 1], ai[:, p:p + 1], us[:, q:q + 1], ALU.mult))
                pool.sem_inc(s["s2_done"], 1)
                link.leave()

            def add(t, q):
                p = q % 2
                pool.wait_ge(s["o_free"], t + 2)
                nc.gpsimd.tensor_tensor(tile_of(chip, t), tile_of(chip, t), res[:, p, :], ALU.add).then_inc(s["x_done"], 1)

            none = lambda t, p: None
            pipelined(pool, [rstd, scale_x, none, none, scale_h, none, none, add], unroll=4)


def routed_stage(chip, dram):
    nc = chip.nc
    E, F, SEQ = 8, 256, 512
    NT = SEQ // P
    N = NT * E
    gate = chip.gates[:, B + 2:B + 3]
    with ExitStack() as ctx:
        def sb(name, shape, dt=F32):
            return ctx.enter_context(nc.sbuf_tensor(f"L2F_{name}", shape, dt))

        def ps(name, shape):
            return ctx.enter_context(nc.psum_tensor(f"L2F_{name}", shape, F32))

        acc = [ps(f"acc{i}", [P, 512]) for i in range(NT)]
        gu_ps = [ps(f"gu_ps{i}", [P, 512]) for i in range(2)]
        hT_ps = [ps(f"hT_ps{i}", [P, 512]) for i in range(2)]
        wgu, wdn, gub = sb("wgu", [P, KD, E * 2 * F]), sb("wdn", [P, KD, E * D]), sb("gub", [P, E * 2 * F])
        bdn, rw, ri = sb("bdn", [E, D]), sb("rw", [P, NT, E]), sb("ri", [P, NT, 2], I32)
        rif, hot, we, wrow, wT = sb("rif", [P, NT, 2]), sb("hot", [P, NT, E]), sb("we", [P, E, NT]), sb("wrow", [P, NT, E]), sb("wT", [E, SEQ])
        stat, mv, ve, rs = sb("stat", [P, NT, 6]), sb("mv", [P, NT, 2]), sb("ve", [P, NT]), sb("rs", [P, NT])
        xn, xT = sb("xn", [P, NT, D]), sb("xT", [P, NT, KD, P])
        gu, sig, glu, h, hT = sb("gu", [P, 2, 2 * F]), sb("sig", [P, 2, F]), sb("glu", [P, 2, F]), sb("h", [P, 2, F]), sb("hT", [P, 2, KD, P])
        res = sb("res", [P, NT, D])
        names = """router_in small_in weights_in ready stats_done rstd_done xn_done xT_full xT_copied w_done wT_full wT_copied acc_done
            gu_full added clipped sig_done h_done hT_full hT_free res_done dve_step pool_step x_done""".split()
        s = {n: ctx.enter_context(nc.semaphore(f"L2F_{n}")) for n in names}
        expert_in = [ctx.enter_context(nc.semaphore(f"L2F_expert_in{e}")) for e in range(E)]
        block = ctx.enter_context(nc.Block())

        @block.sync
        def _(sp):
            sp.dma_start(rw[:], dram["L2_rw"]).then_inc(s["router_in"], 16)
            sp.dma_start(ri[:], dram["L2_ri"]).then_inc(s["router_in"], 16)
            sp.dma_start(bdn[:], dram["L2_dn_bias"]).then_inc(s["small_in"], 16)
            for e in range(E):
                cols = slice(e * 2 * F, (e + 1) * 2 * F)
                sp.dma_start(wgu[:, :, cols], dram["L2_gu"][:, :, cols]).then_inc(expert_in[e], 16)
                sp.dma_start(gub[:, cols], dram["L2_gu_bias"][cols].partition_broadcast(P)).then_inc(expert_in[e], 16)
                sp.dma_start(wdn[:, :, e * D:(e + 1) * D], dram["L2_dn"][:, :, e * D:(e + 1) * D]).then_inc(expert_in[e], 16)
            for e in range(E):
                sp.wait_ge(expert_in[e], 48)
                sp.sem_inc(s["ready"], NT)

        @block.tensor
        def _(pe):
            pe.sem_inc(s["gu_full"], 2)
            for i in range(NT):
                pe.wait_ge(s["xn_done"], i + 1)
                if i >= 2:
                    pe.wait_ge(s["xT_copied"], i - 1)
                for k in range(KD):
                    mm = nc.tensor.transpose(hT_ps[i % 2][:, k * P:(k + 1) * P], xn[:, i, k * P:(k + 1) * P], chip.ident[:])
                mm.then_inc(s["xT_full"], 1)
            pe.wait_ge(s["w_done"], 1)
            for i in range(NT):
                mm = nc.tensor.transpose(gu_ps[0][0:E, i * P:(i + 1) * P], wrow[:, i, :], chip.ident[:])
            mm.then_inc(s["wT_full"], 1)
            pe.wait_ge(s["wT_copied"], 1)
            pe.wait_ge(s["small_in"], 16)
            pe.wait_ge(s["xT_copied"], NT)
            for i in range(NT):
                nc.tensor.matmul(acc[i][:, 0:D], wT[:, i * P:(i + 1) * P], bdn[:], start=True, stop=True, skip_group_check=True)

            def up(t, q):
                pe.wait_ge(s["ready"], t - q + NT)
                pe.wait_ge(s["added"], t + 1)
                for k in range(KD):
                    mm = nc.tensor.matmul(gu_ps[q % 2][:], xT[:, q, k, :], wgu[:, k, bass.ds((t - q) * P, 2 * F)],
                                          start=(k == 0), stop=(k == KD - 1))
                mm.then_inc(s["gu_full"], 1)

            def turn_h(t, q):
                pe.wait_ge(s["h_done"], t + 1)
                pe.wait_ge(s["hT_free"], t + 1)
                for k in range(KD):
                    mm = nc.tensor.transpose(hT_ps[q % 2][:, k * P:(k + 1) * P], h[:, q % 2, k * P:(k + 1) * P], chip.ident[:])
                mm.then_inc(s["hT_full"], 1)

            def down(t, q):
                pe.wait_ge(s["hT_free"], t + 3)
                for k in range(KD):
                    mm = nc.tensor.matmul(acc[q][:, 0:D], hT[:, q % 2, k, :], wdn[:, k, bass.ds((t - q) * (D // NT), D)],
                                          start=False, stop=True, skip_group_check=True)
                mm.then_inc(s["acc_done"], 1)

            none = lambda t, q: None
            pipelined(pe, [up, none, none, turn_h, down], n=N, unroll=NT)

        @block.scalar
        def _(act):
            act.sem_inc(s["hT_free"], 2)
            for i in range(NT):
                act.wait_ge(s["xT_full"], i + 1)
                nc.scalar.activation(xT[:, i, :, :].rearrange("p k t -> p (k t)"), hT_ps[i % 2][:, 0:D], ACT.Copy).then_inc(s["xT_copied"], 1)
            act.wait_ge(s["wT_full"], 1)
            nc.scalar.activation(wT[:], gu_ps[0][0:E, :], ACT.Copy).then_inc(s["wT_copied"], 1)

            def sigmoid(t, q):
                act.wait_ge(s["clipped"], t + 1)
                nc.scalar.activation(sig[:, q % 2, :], gu[:, q % 2, 0:F], ACT.Sigmoid, scale=1.702).then_inc(s["sig_done"], 1)

            def copy_h(t, q):
                act.wait_ge(s["hT_full"], t + 1)
                nc.scalar.activation(hT[:, q % 2, :, :].rearrange("p k t -> p (k t)"), hT_ps[q % 2][:, 0:D], ACT.Copy).then_inc(s["hT_free"], 1)

            none = lambda t, q: None
            pipelined(act, [none, sigmoid, none, copy_h, none], n=N, unroll=NT)
            act.wait_ge(s["acc_done"], N)
            for i in range(NT):
                nc.scalar.activation(res[:, i, :], acc[i][:, 0:D], ACT.Identity, scale=gate).then_inc(s["res_done"], 1)

        @block.vector
        def _(dve):
            link = Links(dve, s["dve_step"], [0, 3, 1, 0, 0], n=N)
            link.k = 0
            for i in range(NT):
                ins = nc.vector.bn_stats(stat[:, i, :], chip.x[:, i * D:(i + 1) * D])
            link(ins)
            for i in range(NT):
                ins = nc.vector.bn_aggr(mv[:, i, :], stat[:, i, :])
            ins.then_inc(s["stats_done"], 1)
            dve.wait_ge(s["router_in"], 32)
            link(nc.vector.tensor_copy(rif[:], ri[:]))
            for i in range(NT):
                link(nc.vector.tensor_scalar(hot[:, i, :], chip.iota[:, 0:E], rif[:, i, 0:1], None, ALU.is_equal))
                link(nc.vector.scalar_tensor_tensor(out=hot[:, i, :], in0=chip.iota[:, 0:E], scalar=rif[:, i, 1:2], in1=hot[:, i, :],
                                                    op0=ALU.is_equal, op1=ALU.add))
                nc.vector.tensor_tensor(we[:, :, i], hot[:, i, :], rw[:, i, :], ALU.mult)
                link(nc.vector.tensor_tensor(wrow[:, i, :], hot[:, i, :], rw[:, i, :], ALU.mult))
            dve.sem_inc(s["w_done"], 1)
            dve.wait_ge(s["rstd_done"], 1)
            for i in range(NT):
                nc.vector.tensor_scalar(xn[:, i, :], chip.x[:, i * D:(i + 1) * D], mv[:, i, 0:1], rs[:, i:i + 1],
                                        ALU.subtract, ALU.mult).then_inc(s["xn_done"], 1)
            dve.wait_ge(s["wT_copied"], 1)
            dve.sem_inc(s["added"], 2)
            link.start = link.k

            def clip(t, q):
                link.enter(1, t)
                p = q % 2
                dve.wait_ge(s["ready"], t - q + NT)
                dve.wait_ge(s["gu_full"], t + 3)
                if not (isinstance(t, int) and t < 2):
                    dve.wait_ge(s["h_done"], t - 1)
                nc.vector.tensor_tensor(gu[:, p, :], gu_ps[p][:], gub[:, bass.ds((t - q) * P, 2 * F)], ALU.add).then_inc(s["added"], 1)
                dve.wait_ge(s["added"], t + 3)
                link(nc.vector.tensor_scalar(gu[:, p, 0:F], gu[:, p, 0:F], 7.0, None, ALU.min))
                dve.sem_inc(s["clipped"], 1)
                link(nc.vector.tensor_scalar(gu[:, p, F:], gu[:, p, F:], -7.0, 7.0, ALU.max, ALU.min))
                link(nc.vector.tensor_scalar(gu[:, p, F:], gu[:, p, F:], 1.0, None, ALU.add))
                link.leave()

            def swiglu(t, q):
                link.enter(2, t)
                p = q % 2
                dve.wait_ge(s["sig_done"], t + 1)
                link(nc.vector.scalar_tensor_tensor(out=glu[:, p, :], in0=sig[:, p, :], scalar=we[:].rearrange("p e i -> p (e i)")[:, bass.ds(t, 1)],
                                                    in1=gu[:, p, 0:F], op0=ALU.mult, op1=ALU.mult))
                if not (isinstance(t, int) and t < 2):
                    dve.wait_ge(s["hT_full"], t - 1)
                nc.vector.tensor_tensor(h[:, p, :], glu[:, p, :], gu[:, p, F:], ALU.mult).then_inc(s["h_done"], 1)
                link.leave()

            none = lambda t, q: None
            pipelined(dve, [none, clip, swiglu, none, none], n=N, unroll=NT)

        @block.gpsimd
        def _(pool):
            pool.wait_ge(s["stats_done"], 1)
            nc.gpsimd.tensor_scalar(ve[:], mv[:, :, 1], 1e-5, None, ALU.add).then_inc(s["pool_step"], 1)
            pool.wait_ge(s["pool_step"], 1)
            nc.gpsimd.tensor_tensor(rs[:], ve[:], chip.neghalf[:, 0:NT], ALU.pow).then_inc(s["rstd_done"], 1)
            for i in range(NT):
                pool.wait_ge(s["res_done"], i + 1)
                nc.gpsimd.tensor_tensor(chip.x[:, i * D:(i + 1) * D], chip.x[:, i * D:(i + 1) * D], res[:, i, :], ALU.add)


def single_stage(chip, dram):
    nc, w = chip.nc, chip.w
    NCP = 80
    gate = chip.gates[:, 3:4]
    with ExitStack() as ctx:
        def sb(name, shape, dt=F32):
            return ctx.enter_context(nc.sbuf_tensor(f"L3_{name}", shape, dt))

        def ps(name, shape):
            return ctx.enter_context(nc.psum_tensor(f"L3_{name}", shape, F32))

        xT_ps, s_ps, pT_ps, o_ps = ps("xT_ps", [P, 512]), ps("s_ps", [P, 512]), ps("pT_ps", [P, 512]), ps("o_ps", [P, 512])
        pre_ps = [ps(f"pre_ps{i}", [P, 512]) for i in range(4)]
        kT, fold, fbias, v = sb("kT", [P, KD, B * NC]), sb("fold", [P, KD, B * NCP]), sb("fbias", [1, B * NCP]), sb("v", [NC, B, D])
        stat, mv, ve, rs = sb("stat", [P, 2, 6]), sb("mv", [P, 2, 2]), sb("ve", [P, 2]), sb("rs", [P, 2])
        xn, xT = sb("xn", [P, 2, D]), sb("xT", [P, 2, KD, P])
        mx, sm, rc = sb("mx", [P, 2]), sb("sm", [P, 4]), sb("rc", [P, 4])
        pr, pT, res = sb("pr", [P, 2, NC]), sb("pT", [NC, 2, P]), sb("res", [P, 2, D])
        names = """pre_full pre_copied v_done stats_done rstd_done xn_done xT_full xT_free s_full shifted exp_done pT_full pT_free
            o_full o_free x_done dve_step pool_step""".split()
        s = {n: ctx.enter_context(nc.semaphore(f"L3_{n}")) for n in names}
        block = ctx.enter_context(nc.Block())
        NU = 8

        @block.tensor
        def _(pe):
            for name in WEIGHTS["L3"]:
                pe.wait_ge(chip.w_in[name], 16)
            for m in range(KD):
                for k in range(KD):
                    mm = nc.tensor.matmul(pre_ps[m][:, 0:B * NC], w["L3_Wk"][:, k, m * P:(m + 1) * P], chip.ctxT[:, k, :],
                                          start=(k == 0), stop=(k == KD - 1))
                mm.then_inc(s["pre_full"], 1)
            for half in range(2):
                for n in range(2):
                    b = 2 * half + n
                    for k in range(KD):
                        mm = nc.tensor.matmul(pre_ps[2 + half][0:NC, n * D:(n + 1) * D], chip.ctxT[:, k, b * NC:(b + 1) * NC],
                                              w["L3_Wv"][:, k, :], start=(k == 0), stop=(k == KD - 1))
                mm.then_inc(s["pre_full"], 1)
            pe.wait_ge(s["pre_copied"], 2)
            for m in range(KD):
                for k in range(KD):
                    mm = nc.tensor.matmul(pre_ps[m][:, 0:B * NC], w["L3_WqT"][:, k, m * P:(m + 1) * P], kT[:, k, :],
                                          start=(k == 0), stop=(k == KD - 1))
                mm.then_inc(s["pre_full"], 1)
            for k in range(KD):
                mm = nc.tensor.matmul(s_ps[0:1, 0:B * NC], chip.col("L3_xattn_bq")[:, k:k + 1], kT[:, k, :],
                                      start=(k == 0), stop=(k == KD - 1))
            mm.then_inc(s["pre_full"], 1)
            pe.wait_ge(s["pre_copied"], 5)
            pe.wait_ge(s["v_done"], 4)

            def turn_x(t, q):
                pe.wait_ge(s["xn_done"], t + 1)
                pe.wait_ge(s["xT_free"], t + 1)
                for k in range(KD):
                    mm = nc.tensor.transpose(xT_ps[:, k * P:(k + 1) * P], xn[:, q % 2, k * P:(k + 1) * P], chip.ident[:])
                mm.then_inc(s["xT_full"], 1)

            def scores(t, q):
                cols = bass.ds((t - q) * (NCP // NU), NC)
                pe.wait_ge(s["xT_free"], t + 2)
                pe.wait_ge(s["shifted"], t + 1)
                for k in range(KD):
                    nc.tensor.matmul(s_ps[:, 0:NC], xT[:, q % 2, k, :], fold[:, k, cols], start=(k == 0), stop=False)
                nc.tensor.matmul(s_ps[:, 0:NC], chip.ones[0:1, :], fbias[:, cols], start=False, stop=True).then_inc(s["s_full"], 1)

            def turn_p(t, q):
                pe.wait_ge(s["exp_done"], t + 1)
                pe.wait_ge(s["pT_free"], t + 1)
                nc.tensor.transpose(pT_ps[0:NC, 0:P], pr[:, q % 2, :], chip.ident[:]).then_inc(s["pT_full"], 1)

            def values(t, q):
                pe.wait_ge(s["pT_free"], t + 2)
                pe.wait_ge(s["o_free"], t + 4)
                nc.tensor.matmul(o_ps[:, 0:D], pT[:, q % 2, :], v[:].rearrange("k b d -> k (b d)")[:, bass.ds((t - q) * (D // NU), D)],
                                 start=True, stop=True).then_inc(s["o_full"], 1)

            none = lambda t, q: None
            pipelined(pe, [none, turn_x, scores, none, turn_p, values], unroll=NU)

        @block.scalar
        def _(act):
            act.sem_inc(s["xT_free"], 1)
            act.sem_inc(s["pT_free"], 1)
            for m in range(KD):
                act.wait_ge(s["pre_full"], m + 1)
                nc.scalar.activation(kT[:, m, :], pre_ps[m][:, 0:B * NC], ACT.Identity,
                                     bias=chip.col("L3_xattn_bk")[:, m:m + 1]).then_inc(s["pre_copied"], 1)
            for m in range(KD):
                act.wait_ge(s["pre_full"], 5 + m)
                nc.scalar.activation(fold[:, m, :].rearrange("p (b c) -> p b c", c=NCP)[:, :, 0:NC],
                                     pre_ps[m][:, 0:B * NC].rearrange("p (b c) -> p b c", c=NC), ACT.Copy).then_inc(s["pre_copied"], 1)
            act.wait_ge(s["pre_full"], 7)
            nc.scalar.activation(fbias[:].rearrange("p (b c) -> p b c", c=NCP)[:, :, 0:NC],
                                 s_ps[0:1, 0:B * NC].rearrange("p (b c) -> p b c", c=NC), ACT.Copy).then_inc(s["pre_copied"], 1)

            def copy_x(t, q):
                act.wait_ge(s["xT_full"], t + 1)
                nc.scalar.activation(xT[:, q % 2, :, :].rearrange("p k t -> p (k t)"), xT_ps[:, 0:D], ACT.Copy).then_inc(s["xT_free"], 1)

            def exp(t, q):
                act.wait_ge(s["shifted"], t + 2)
                act.wait_ge(s["o_free"], t + 1)
                nc.scalar.activation(pr[:, q % 2, :], pr[:, q % 2, :], ACT.Exp, scale=1.0 / 16.0, accum_out=sm[:, q % 4:q % 4 + 1]).then_inc(s["exp_done"], 1)

            def copy_p(t, q):
                act.wait_ge(s["pT_full"], t + 1)
                nc.scalar.activation(pT[:, q % 2, :], pT_ps[0:NC, 0:P], ACT.Copy).then_inc(s["pT_free"], 1)

            none = lambda t, q: None
            pipelined(act, [none, copy_x, none, exp, copy_p, none], unroll=NU)

        @block.vector
        def _(dve):
            link = Links(dve, s["dve_step"], [1, 0, 1, 0, 0, 1])
            link.k = 0
            for half in range(2):
                dve.wait_ge(s["pre_full"], 3 + half)
                for n in range(2):
                    nc.vector.tensor_tensor(v[:, 2 * half + n, :], pre_ps[2 + half][0:NC, n * D:(n + 1) * D],
                                            chip.vec("L3_xattn_bv")[0:NC, :], ALU.add).then_inc(s["v_done"], 1)
            dve.sem_inc(s["shifted"], 1)
            dve.sem_inc(s["o_free"], 4)

            def stats(t, q):
                p = q % 2
                link.enter(0, t)
                link(nc.vector.bn_stats(stat[:, p, :], tile_of(chip, t)))
                chip.settle(dve)
                nc.vector.bn_aggr(mv[:, p, :], stat[:, p, :]).then_inc(s["stats_done"], 1)
                link.leave()

            def normalise(t, q):
                p = q % 2
                dve.wait_ge(s["rstd_done"], t + 1)
                nc.vector.tensor_scalar(xn[:, p, :], tile_of(chip, t), mv[:, p, 0:1], rs[:, p:p + 1],
                                        ALU.subtract, ALU.mult).then_inc(s["xn_done"], 1)

            def shift(t, q):
                p = q % 2
                link.enter(2, t)
                dve.wait_ge(s["s_full"], t + 1)
                link(nc.vector.tensor_reduce(mx[:, p:p + 1], s_ps[:, 0:NC], AX.X, ALU.max))
                if not (isinstance(t, int) and t < 2):
                    dve.wait_ge(s["pT_full"], t - 1)
                nc.vector.tensor_scalar(pr[:, p, :], s_ps[:, 0:NC], mx[:, p:p + 1], None, ALU.subtract).then_inc(s["shifted"], 1)
                link.leave()

            def result(t, q):
                p = q % 2
                link.enter(5, t)
                dve.wait_ge(s["exp_done"], t + 1)
                link(nc.vector.reciprocal(rc[:, q % 4:q % 4 + 1], sm[:, q % 4:q % 4 + 1]))
                dve.wait_ge(s["o_full"], t + 1)
                dve.wait_ge(s["x_done"], t + 1)
                nc.vector.tensor_scalar(res[:, p, :], o_ps[:, 0:D], rc[:, q % 4:q % 4 + 1], gate, ALU.mult, ALU.mult).then_inc(s["o_free"], 1)
                link.leave()

            none = lambda t, q: None
            pipelined(dve, [stats, normalise, shift, none, none, result], unroll=NU)

        @block.gpsimd
        def _(pool):
            link = Links(pool, s["pool_step"], [1, 0, 0, 0, 0, 0])
            pool.sem_inc(s["x_done"], 2)

            def rstd(t, q):
                p = q % 2
                link.enter(0, t)
                pool.wait_ge(s["stats_done"], t + 1)
                chip.settle(pool)
                link(nc.gpsimd.tensor_scalar(ve[:, p:p + 1], mv[:, p, 1:2], 1e-5, None, ALU.add))
                nc.gpsimd.tensor_tensor(rs[:, p:p + 1], ve[:, p:p + 1], chip.neghalf[:, 0:1], ALU.pow).then_inc(s["rstd_done"], 1)
                link.leave()

            def add(t, q):
                pool.wait_ge(s["o_free"], t + 5)
                nc.gpsimd.tensor_tensor(tile_of(chip, t), tile_of(chip, t), res[:, q % 2, :], ALU.add).then_inc(s["x_done"], 1)

            none = lambda t, q: None
            pipelined(pool, [rstd, none, none, none, none, add], unroll=NU)


def self_stage(chip, dram):
    nc, w = chip.nc, chip.w
    BIG = -1e30
    SK = 1.0 / 32.0
    HD = D // H
    KR = 6 * HD
    MR = KR + 2
    QUADS = H // 4
    VC = HD + 1
    STEPS = [(0, kt) for kt in range(TB // 2)] + [(1, kt) for kt in range(TB)]
    NS = len(STEPS)
    PEAKS = [(i, hs) for i in range(TB) for hs in (((0, 1), (2, 3)) if i < TB // 2 else ((0,), (1,), (2,), (3,)))]
    NP = len(PEAKS)
    SHARE = (5, 2, 1, 1, 4, 3, 3, 3, 2, 0, 0, 0)
    TURN_AT = 9
    with ExitStack() as ctx:
        def sb(name, shape, dt=F32):
            return ctx.enter_context(nc.sbuf_tensor(f"L2S_{name}", shape, dt))

        def ps(name, shape, dt=F32):
            return ctx.enter_context(nc.psum_tensor(f"L2S_{name}", shape, dt))

        s_ps = [ps(f"s_ps{i}", [P, S]) for i in range(2)]
        t_ps = [ps(f"t_ps{i}", [P, 512]) for i in range(2)]
        o_ps = ps("o_ps", [P, 512])
        r_ps = ps("r_ps", [P, 512])
        stat, mv, ve, rs = sb("stat", [P, TB, 6]), sb("mv", [P, TB, 2]), sb("ve", [P, TB]), sb("rs", [P, TB])
        xn = sb("xn", [P, TB, D])
        xT = sb("xT", [P, KD, S])
        part = sb("part", [P, 2, 3, S], BF16)
        q6 = sb("q6", [MR, 2, 4, S], BF16)
        k6 = sb("k6", [MR, 2, 4, S], BF16)
        v = sb("v", [P, TB, H * VC + 32 - VC])
        pT = sb("pT", [P, 2, 4, 512])
        rest = pT[:, 0, :, :].rearrange("p j t -> p (j t)").rearrange("p (r t) -> p r t", r=2)
        cmask, cmaskT, identb = sb("cmask", [P, P], BF16), sb("cmaskT", [P, P], BF16), sb("identb", [P, P], BF16)
        mx = sb("mx", [P, 2, 4, TB])
        mrow = sb("mrow", [4 * TB, 2, P], BF16)
        oT = sb("oT", [P, 512])
        rc = sb("rc", [P, 4, 4])
        att = sb("att", [P, TB, D])
        names = """const_done ones_done stats_done rstd_done xn_done pre_full act_pre rest_done split_done written0 written1 loaded_low0 loaded_low1
            loaded_high0 loaded_high1 s_full mx_done r_full r_free mrow_in t_full exp_done pv_done o_copied att_free y_done
            rstd2_done stats2_done norm_done a_done a_out pool_step dve_step""".split()
        s = {n: ctx.enter_context(nc.semaphore(f"L2S_{n}")) for n in names}
        block = ctx.enter_context(nc.Block())

        R_USES = 3 * QUADS
        R_AT, order = {}, []
        for q in range(QUADS):
            order += [("m", 0)] if q == 0 else [("o", q - 1, 1)]
            order += [("o", q, 0)] + ([("m", q + 1)] if q + 1 < QUADS else [])
        order += [("o", QUADS - 1, 1)]
        R_AT = {use: n + 1 for n, use in enumerate(order)}

        def nothing(*a):
            pass

        def self_walk(setup=nothing, peak=nothing, turn_max=nothing, unit=nothing, values=nothing, copy_out=nothing,
                      turn_out=nothing, finish=nothing):
            setup()
            for n in range(NP):
                peak(0, n)
            turn_max(0)
            for q in range(QUADS):
                pending = list(range(NP)) if q + 1 < QUADS else []
                for st in range(NS):
                    share = pending[:SHARE[st]]
                    pending = pending[SHARE[st]:]
                    for j in range(4):
                        unit(q, st, j)
                        for n in share[j:j + 1]:
                            peak(q + 1, n)
                    for n in share[4:]:
                        peak(q + 1, n)
                    before = (q, st - 1) if st else (q - 1, NS - 1)
                    if before[0] >= 0:
                        values(*before)
                        if before[1] in (TB // 2 - 1, NS - 1):
                            copy_out(before[0], STEPS[before[1]][0])
                    if st == TB // 2 + 1:
                        turn_out(q, 0)
                    if st == 1 and q:
                        turn_out(q - 1, 1)
                    if st == TURN_AT and q + 1 < QUADS:
                        turn_max(q + 1)
            values(QUADS - 1, NS - 1)
            copy_out(QUADS - 1, 1)
            turn_out(QUADS - 1, 1)
            finish()

        def low(st):
            c, kt = STEPS[st]
            return max(0, (kt - 4 * c) * P)

        @block.sync
        def _(sp):
            chip.load(sp, WEIGHTS["L3"], dram)

            def load(b, q, which, cols, sem):
                t = {"q": q6, "k": k6}[which]
                chip.settle(sp)
                src = dram["parts"][bass.ds(b * 2 + (0 if which == "q" else 1), 1)]
                for slot, p in enumerate({"q": (0, 0, 0, 1, 1, 2), "k": (0, 1, 2, 0, 1, 0)}[which]):
                    sp.dma_start(t[slot * HD:(slot + 1) * HD, q % 2, :, cols],
                                 src[:, q, p, :, :, cols].rearrange("o h d s -> (o d) h s")).then_inc(sem, 16)

            lowc, highc = slice(0, S // 2), slice(S // 2, S)
            sp.sem_inc(s["att_free"], 1)
            with sp.Fori(0, B) as b:
                def write(f):
                    which, m = f % 2, f // 2
                    sp.wait_ge(s["split_done"], 4 * b + f + 2)
                    chip.settle(sp)
                    for p in range(3):
                        for qq in range(2):
                            sp.dma_start(dram["parts"][bass.ds(b * 2 + which, 1), 2 * m + qq, p, :, :, :].rearrange("o h d s -> (o h d) s"),
                                         part[64 * qq:64 * qq + 64, f % 2, p, :]).then_inc(s[f"written{which}"], 16)

                write(0)
                write(1)
                for which in range(2):
                    sp.wait_ge(s[f"written{which}"], (2 * b + 1) * 96)
                    chip.settle(sp)
                for q in range(2):
                    for cols, n in ((lowc, "low"), (highc, "high")):
                        for which in "qk":
                            load(b, q, which, cols, s[f"loaded_{n}{q % 2}"])
                write(2)
                write(3)
                for which in range(2):
                    sp.wait_ge(s[f"written{which}"], (2 * b + 2) * 96)
                    chip.settle(sp)
                for q in range(2, QUADS):
                    done = b * QUADS * NS * 4 + (q - 2) * NS * 4
                    sp.wait_ge(s["t_full"], done + 4 * (TB // 2))
                    load(b, q, "q", lowc, s[f"loaded_low{q % 2}"])
                    sp.wait_ge(s["t_full"], done + 4 * TB)
                    load(b, q, "k", lowc, s[f"loaded_low{q % 2}"])
                    sp.wait_ge(s["t_full"], done + 4 * NS)
                    load(b, q, "q", highc, s[f"loaded_high{q % 2}"])
                    load(b, q, "k", highc, s[f"loaded_high{q % 2}"])
                sp.wait_ge(s["a_done"], b + 1)
                chip.settle(sp)
                sp.dma_start(dram["a"][:, bass.ts(b, TB), :], att[:]).then_inc(s["a_out"], 16)
                sp.wait_ge(s["a_out"], 16 * b + 16)
                sp.sem_inc(s["att_free"], 1)

        @block.tensor
        def _(pe):
            for name in WEIGHTS["L2S"]:
                pe.wait_ge(chip.w_in[name], 16)
            pe.wait_ge(s["const_done"], 1)
            pe.wait_ge(s["ones_done"], 1)
            pe.sem_inc(s["pv_done"], 1)
            pe.sem_inc(s["r_full"], 1)
            with pe.Fori(0, B) as b:
                def setup():
                    pe.wait_ge(s["y_done"], 2 * b + 1)
                    pe.wait_ge(s["xn_done"], TB * b + TB)
                    for dh in range(KD):
                        for i in range(TB):
                            mm = nc.tensor.transpose(s_ps[dh][:, i * P:(i + 1) * P], xn[:, i, dh * P:(dh + 1) * P], chip.ident[:])
                        mm.then_inc(s["pre_full"], 1)
                    pe.wait_ge(s["act_pre"], 10 * b + 2)
                    for half in range(2):
                        for i in range(4):
                            t = 4 * half + i
                            for k in range(KD):
                                mm = nc.tensor.matmul(s_ps[half][:, i * D:(i + 1) * D], xT[:, k, t * P:(t + 1) * P], w["L2S_Wv"][:, k, :],
                                                      start=(k == 0), stop=(k == KD - 1))
                        mm.then_inc(s["pre_full"], 1)
                    for f in range(4):
                        if f < 2:
                            pe.wait_ge(s["act_pre"], 10 * b + 3 + f)
                        else:
                            pe.wait_ge(s["rest_done"], 4 * b + f - 1)
                        m = f // 2
                        for c in range(2):
                            for k in range(KD):
                                mm = nc.tensor.matmul(s_ps[f % 2][:, c * 512:(c + 1) * 512], w[("L2S_Wq", "L2S_Wk")[f % 2]][:, k, m * P:(m + 1) * P],
                                                      xT[:, k, c * 512:(c + 1) * 512], start=(k == 0), stop=(k == KD - 1))
                        mm.then_inc(s["pre_full"], 1)
                    pe.wait_ge(s["rest_done"], 4 * b + 4)

                def peak(q, n):
                    i, hs = PEAKS[n]
                    number = NP * (QUADS * b + q) + n
                    if n == 0:
                        pe.wait_ge(s[f"loaded_low{q % 2}"], 192 * (2 * b + q // 2 + 1))
                    if n == TB:
                        pe.wait_ge(s[f"loaded_high{q % 2}"], 192 * (2 * b + q // 2 + 1))
                    pe.wait_ge(s["mx_done"], number + 1)
                    o = s_ps[n % 2]
                    for z, h in enumerate(hs):
                        lhs = q6[0:KR, q % 2, h, i * P:(i + 1) * P]
                        end = (i + 1) * P
                        for c in range(0, end, 512):
                            e = min(end, c + 512)
                            nc.tensor.matmul(o[:, z * 512 + c:z * 512 + e], lhs, k6[0:KR, q % 2, h, c:e], start=True, stop=(e < end))
                        mm = nc.tensor.matmul(o[:, z * 512 + end - P:z * 512 + end], identb[:], cmask[:], start=False, stop=True)
                    mm.then_inc(s["s_full"], 1)

                def turn_max(q):
                    k = R_USES * b + R_AT["m", q]
                    pe.wait_ge(s["r_free"], k)
                    pe.wait_ge(s["mx_done"], NP * (QUADS * b + q + 1) + 2)
                    nc.tensor.transpose(r_ps[0:4 * TB, 0:P], mx[:, q % 2, :, :].rearrange("p h i -> p (h i)"), chip.ident[:]).then_inc(s["r_full"], 1)

                def unit(q, st, j):
                    c, kt = STEPS[st]
                    number = ((QUADS * b + q) * NS + st) * 4 + j
                    if st == 0 and j == 0:
                        pe.wait_ge(s["mrow_in"], 32 * (QUADS * b + q + 1))
                    pe.wait_ge(s["exp_done"], number + 1)
                    o, lo = t_ps[j % 2], low(st)
                    diagonal = kt >= 4 * c
                    mm = nc.tensor.matmul(o[:, lo:512], k6[:, q % 2, j, kt * P:(kt + 1) * P], q6[:, q % 2, j, c * 512 + lo:(c + 1) * 512],
                                          start=True, stop=not diagonal)
                    if diagonal:
                        mm = nc.tensor.matmul(o[:, lo:lo + P], identb[:], cmaskT[:], start=False, stop=True)
                    mm.then_inc(s["t_full"], 1)

                def values(q, st):
                    c, kt = STEPS[st]
                    step = (QUADS * b + q) * NS + st
                    last = 3 if c == 0 else TB - 1
                    pe.wait_ge(s["exp_done"], 4 * step + 4 + 2)
                    if kt == 0:
                        pe.wait_ge(s["o_copied"], 2 * (QUADS * b + q) + c + 1)
                    lo = low(st)
                    for j in range(4):
                        h = 4 * q + j
                        mm = nc.tensor.matmul(o_ps[32 * j:32 * j + 32, lo:512], v[:, kt, h * VC:h * VC + 32], pT[:, st % 2, j, lo:512],
                                              start=(kt == 0), stop=(kt == last))
                    mm.then_inc(s["pv_done"], 1)

                def turn_out(q, c):
                    k = R_USES * b + R_AT["o", q, c]
                    pe.wait_ge(s["r_free"], k)
                    pe.wait_ge(s["o_copied"], 2 * (QUADS * b + q) + c + 2)
                    for i in range(4):
                        mm = nc.tensor.transpose(r_ps[:, i * P:(i + 1) * P], oT[:, i * P:(i + 1) * P], chip.ident[:])
                    mm.then_inc(s["r_full"], 1)

                def finish():
                    pe.wait_ge(s["r_free"], R_USES * b + R_USES + 1)
                    for dh in range(KD):
                        for i in range(TB):
                            mm = nc.tensor.transpose(s_ps[dh][:, i * P:(i + 1) * P], att[:, i, dh * P:(dh + 1) * P], chip.ident[:])
                        mm.then_inc(s["pre_full"], 1)
                    pe.wait_ge(s["act_pre"], 10 * b + 10)
                    for half in range(2):
                        for i in range(4):
                            t = 4 * half + i
                            for k in range(KD):
                                mm = nc.tensor.matmul(s_ps[half][:, i * D:(i + 1) * D], xT[:, k, t * P:(t + 1) * P], w["L2S_Wo"][:, k, :],
                                                      start=(k == 0), stop=(k == KD - 1))
                        mm.then_inc(s["pre_full"], 1)

                self_walk(setup, peak, turn_max, unit, values, nothing, turn_out, finish)

        @block.scalar
        def _(act):
            act.sem_inc(s["exp_done"], 2)
            act.sem_inc(s["o_copied"], 1)
            with act.Fori(0, B) as b:
                def copy(dst, src):
                    nc.scalar.activation(dst, src, ACT.Copy).then_inc(s["act_pre"], 1)

                def setup():
                    for f in range(2):
                        act.wait_ge(s["pre_full"], 12 * b + f + 1)
                        copy(xT[:, f, :], s_ps[f][:])
                    act.wait_ge(s["ones_done"], 1)
                    for f in range(2):
                        act.wait_ge(s["pre_full"], 12 * b + f + 3)
                        copy(v[:, 4 * f:4 * f + 4, 0:H * VC].rearrange("p t (h c) -> p t h c", c=VC)[:, :, :, 0:HD],
                             s_ps[f][:].rearrange("p (t h d) -> p t h d", t=4, d=HD))
                    for f in range(4):
                        act.wait_ge(s["pre_full"], 12 * b + f + 5)
                        if f >= 2:
                            act.wait_ge(s[f"written{f % 2}"], (2 * b + 1) * 96)
                        copy(part[:, f % 2, 0, :], s_ps[f % 2][:])

                def unit(q, st, j):
                    step = (QUADS * b + q) * NS + st
                    act.wait_ge(s["t_full"], 4 * step + j + 1)
                    if q == 0 and st == 0 and j == 0:
                        act.wait_ge(s["split_done"], 4 * b + 5)
                    if j == 0:
                        if st < 2 and q == 0:
                            act.wait_ge(s["pv_done"], QUADS * NS * b + 1)
                        else:
                            act.wait_ge(s["pv_done"], step)
                    lo = low(st)
                    nc.scalar.activation(pT[:, st % 2, j, lo:512], t_ps[j % 2][:, lo:512], ACT.Exp, scale=SK).then_inc(s["exp_done"], 1)

                def copy_out(q, c):
                    act.wait_ge(s["pv_done"], (QUADS * b + q) * NS + (TB // 2 if c == 0 else NS) + 1)
                    k = R_AT["o", q, 0] if c else (R_AT["o", q - 1, 1] if q else 0)
                    act.wait_ge(s["r_full"], R_USES * b + k + 1)
                    nc.scalar.activation(oT[:], o_ps[:], ACT.Copy).then_inc(s["o_copied"], 1)

                def finish():
                    for f in range(2):
                        act.wait_ge(s["pre_full"], 12 * b + f + 9)
                        copy(xT[:, f, :], s_ps[f][:])

                self_walk(setup=setup, unit=unit, copy_out=copy_out, finish=finish)

        @block.vector
        def _(dve):
            step = Count(s["dve_step"])

            def link(ins):
                ins.then_inc(s["dve_step"], 1)
                dve.wait_ge(s["dve_step"], step.up())

            nc.vector.memset(v[:], 1.0)
            nc.vector.memset(k6[KR:MR], 1.0).then_inc(s["ones_done"], 1)
            dve.sem_inc(s["mx_done"], 2)
            dve.sem_inc(s["r_free"], 1)
            dve.sem_inc(s["y_done"], 1)
            PER = 1 + QUADS + 2 * QUADS + 5
            with dve.Fori(0, B) as b:
                step.enter(PER * b)

                def setup():
                    for i in range(TB):
                        ins = nc.vector.bn_stats(stat[:, i, :], chip.x[:, bass.ds((TB * b + i) * D, D)])
                    link(ins)
                    chip.settle(dve)
                    for i in range(TB):
                        ins = nc.vector.bn_aggr(mv[:, i, :], stat[:, i, :])
                    ins.then_inc(s["stats_done"], 1)
                    dve.wait_ge(s["rstd_done"], b + 1)
                    for i in range(TB):
                        nc.vector.tensor_scalar(xn[:, i, :], chip.x[:, bass.ds((TB * b + i) * D, D)], mv[:, i, 0:1], rs[:, i:i + 1],
                                                ALU.subtract, ALU.mult).then_inc(s["xn_done"], 1)
                    for f in range(4):
                        dve.wait_ge(s["act_pre"], 10 * b + 5 + f)
                        dve.wait_ge(s["split_done"], 4 * b + max(f - 1, 0) + 1)
                        nc.vector.tensor_tensor(rest[:, f % 2, :], s_ps[f % 2][:], part[:, f % 2, 0, :], ALU.subtract).then_inc(s["rest_done"], 1)

                def peak(q, n):
                    i, hs = PEAKS[n]
                    dve.wait_ge(s["s_full"], NP * (QUADS * b + q) + n + 1)
                    if len(hs) == 2:
                        src = s_ps[n % 2][:].rearrange("p (h k) -> p h k", h=2)[:, :, 0:(i + 1) * P]
                        dst = mx[:, q % 2, hs[0]:hs[0] + 2, i]
                    else:
                        src, dst = s_ps[n % 2][:, 0:(i + 1) * P], mx[:, q % 2, hs[0], i:i + 1]
                    nc.vector.tensor_reduce(dst, src, AX.X, ALU.max).then_inc(s["mx_done"], 1)

                def turn_max(q):
                    dve.wait_ge(s["r_full"], R_USES * b + R_AT["m", q] + 1)
                    if q:
                        dve.wait_ge(s["mrow_in"], 32 * (QUADS * b + q))
                    link(nc.vector.tensor_scalar(mrow[:, 0, :], r_ps[0:4 * TB, 0:P], -1.0, None, ALU.mult))
                    nc.vector.scalar_tensor_tensor(out=mrow[:, 1, :], in0=r_ps[0:4 * TB, 0:P], scalar=-1.0, in1=mrow[:, 0, :],
                                                   op0=ALU.mult, op1=ALU.subtract).then_inc(s["r_free"], 1)

                def turn_out(q, c):
                    dve.wait_ge(s["r_full"], R_USES * b + R_AT["o", q, c] + 1)
                    dve.wait_ge(s["att_free"], b + 1)
                    o = r_ps[:].rearrange("p (i h d) -> p i h d", i=4, h=4)
                    link(nc.vector.reciprocal(rc[:], o[:, :, :, HD]))
                    dst = att[:, 4 * c:4 * c + 4, 4 * q * HD:4 * (q + 1) * HD].rearrange("p i (h d) -> p i h d", h=4)
                    nc.vector.tensor_tensor(dst, o[:, :, :, 0:HD], wide(rc[:].unsqueeze(3), [P, 4, 4, HD]), ALU.mult).then_inc(s["r_free"], 1)

                def finish():
                    for half in range(2):
                        y = att[:, 4 * half:4 * half + 4, :]
                        dve.wait_ge(s["pre_full"], 12 * b + 11 + half)
                        ins = nc.vector.tensor_tensor(y, s_ps[half][:].rearrange("p (i d) -> p i d", d=D),
                                                      wide(chip.vec("L2_xattn_bo1").unsqueeze(1), [P, 4, D]), ALU.add)
                        ins.then_inc(s["y_done"], 1)
                        dve.wait_ge(s["y_done"], 2 * b + half + 2)
                        link(nc.vector.scalar_tensor_tensor(out=y, in0=y, scalar=0.0, in1=xn[:, 4 * half:4 * half + 4, :],
                                                            op0=ALU.max, op1=ALU.add))
                    for i in range(TB):
                        ins = nc.vector.bn_stats(stat[:, i, :], att[:, i, :])
                    link(ins)
                    chip.settle(dve)
                    for i in range(TB):
                        ins = nc.vector.bn_aggr(mv[:, i, :], stat[:, i, :])
                    ins.then_inc(s["stats2_done"], 1)
                    dve.wait_ge(s["rstd2_done"], b + 1)
                    for i in range(TB):
                        ins = nc.vector.tensor_scalar(att[:, i, :], att[:, i, :], mv[:, i, 0:1], rs[:, i:i + 1], ALU.subtract, ALU.mult)
                    link(ins)
                    link(nc.vector.tensor_tensor(att[:], att[:], wide(chip.vec("L2_xattn_g1").unsqueeze(1), [P, TB, D]), ALU.mult))
                    nc.vector.tensor_tensor(att[:], att[:], wide(chip.vec("L2_xattn_b1").unsqueeze(1), [P, TB, D]), ALU.add).then_inc(s["a_done"], 1)

                self_walk(setup, peak, turn_max, nothing, nothing, nothing, turn_out, finish)
                assert step.k == PER, step.k

        @block.gpsimd
        def _(pool):
            nc.gpsimd.memset(cmask[:], 0.0)
            nc.gpsimd.memset(cmaskT[:], 0.0)
            nc.gpsimd.tensor_copy(identb[:], chip.ident[:]).then_inc(s["pool_step"], 1)
            pool.wait_ge(s["pool_step"], 1)
            nc.gpsimd.affine_select(out=cmask[:], in_=cmask[:], compare_op=ALU.is_ge, fill=BIG, base=0,
                                    pattern=[[-1, P]], channel_multiplier=1)
            nc.gpsimd.affine_select(out=cmaskT[:], in_=cmaskT[:], compare_op=ALU.is_ge, fill=BIG, base=0,
                                    pattern=[[1, P]], channel_multiplier=-1).then_inc(s["const_done"], 1)
            pool.sem_inc(s["split_done"], 1)
            first = 1
            PER = 6
            with pool.Fori(0, B) as b:
                def rstd(sem_in, sem_out, k, eps):
                    pool.wait_ge(s[sem_in], b + 1)
                    chip.settle(pool)
                    nc.gpsimd.tensor_scalar(ve[:], mv[:, :, 1], eps, None, ALU.add).then_inc(s["pool_step"], 1)
                    pool.wait_ge(s["pool_step"], first + PER * b + k)
                    nc.gpsimd.tensor_tensor(rs[:], ve[:], chip.neghalf[:, 0:TB], ALU.pow).then_inc(s[sem_out], 1)

                def setup():
                    rstd("stats_done", "rstd_done", 1, 1e-5)
                    for f in range(4):
                        pool.wait_ge(s["rest_done"], 4 * b + f + 1)
                        if f >= 2:
                            pool.wait_ge(s[f"written{f % 2}"], (2 * b + 1) * 96)
                        chip.settle(pool)
                        nc.gpsimd.tensor_scalar(part[:, f % 2, 1, :], rest[:, f % 2, :], 1.0, None, ALU.mult).then_inc(s["pool_step"], 1)
                        pool.wait_ge(s["pool_step"], first + PER * b + 2 + f)
                        nc.gpsimd.tensor_tensor(part[:, f % 2, 2, :], rest[:, f % 2, :], part[:, f % 2, 1, :], ALU.subtract).then_inc(s["split_done"], 1)

                def turn_max(q):
                    pool.wait_ge(s["r_free"], R_USES * b + R_AT["m", q] + 1)
                    chip.settle(pool)
                    for p in range(2):
                        nc.gpsimd.dma_start(q6[KR + p:KR + p + 1, q % 2, :, :].rearrange("o h (i t) -> o (h i) t", t=P),
                                            mrow[:, p, :]).then_inc(s["mrow_in"], 16)

                def finish():
                    rstd("stats2_done", "rstd2_done", 6, 1e-6)

                self_walk(setup=setup, turn_max=turn_max, finish=finish)


def mixture_stage(chip, dram):
    nc = chip.nc
    E, F = 8, 512
    FK = F // P
    N = T * E
    UR = 2 * E
    gate = chip.gates[:, B + 3:B + 4]
    with ExitStack() as ctx:
        def sb(name, shape, dt=F32):
            return ctx.enter_context(nc.sbuf_tensor(f"L3F_{name}", shape, dt))

        def ps(name, shape):
            return ctx.enter_context(nc.psum_tensor(f"L3F_{name}", shape, F32))

        g_ps, u_ps = [ps(f"g_ps{i}", [P, F]) for i in range(2)], [ps(f"u_ps{i}", [P, F]) for i in range(2)]
        hT_ps, o_ps = ps("hT_ps", [P, 512]), ps("o_ps", [P, 512])
        xT_ps, l_ps = ps("xT_ps", [P, 512]), ps("l_ps", [P, 512])
        w0 = chip.arena[:, 0:KD * E * F].rearrange("p (k n) -> p k n", k=KD)
        w1, wo, wg = sb("w1", [P, KD, E * F]), sb("wo", [P, FK, E * D]), sb("wg", [P, KD, E])
        stat, mv, ve, rs = sb("stat", [P, 2, 6]), sb("mv", [P, 2, 2]), sb("ve", [P, 2]), sb("rs", [P, 2])
        xn, xT = sb("xn", [P, 2, D]), sb("xT", [P, 2, KD, P])
        lg, top, idx, idxf = sb("lg", [P, 2, E]), sb("top", [P, 2, 8]), sb("idx", [P, 2, 8], U32), sb("idxf", [P, 2, 2])
        d12, e2, g1, g2, Ga, Gb = sb("d12", [P, 2]), sb("e2", [P, 2]), sb("g1", [P, 2]), sb("g2", [P, 2]), sb("Ga", [P, 2, E]), sb("Gb", [P, 2, E])
        si, h, hT, res = sb("si", [P, 2, F]), sb("h", [P, 2, F]), sb("hT", [P, 2, FK, P]), sb("res", [P, 2, D])
        names = """gates_in stats_done rstd_done xn_done xT_full xT_free l_full top_done e2_done G_done g_full u_full si_done h_done
            hT_full hT_free o_full o_free x_done dve_step pool_step weights_in""".split()
        s = {n: ctx.enter_context(nc.semaphore(f"L3F_{n}")) for n in names}
        block = ctx.enter_context(nc.Block())

        @block.sync
        def _(sp):
            sp.dma_start(wg[:], dram["L3_wg"]).then_inc(s["gates_in"], 16)
            for e in range(E):
                a, c = slice(e * F, (e + 1) * F), slice(e * D, (e + 1) * D)
                sp.dma_start(w0[:, :, a], dram["L3_w0"][:, :, a]).then_inc(s["weights_in"], 16)
                sp.dma_start(w1[:, :, a], dram["L3_w1"][:, :, a]).then_inc(s["weights_in"], 16)
                sp.dma_start(wo[:, :, c], dram["L3_wo"][:, :, c]).then_inc(s["weights_in"], 16)

        def tile_no(u, q):
            return (u - q) // E + q // E if isinstance(u, int) else None

        @block.tensor
        def _(pe):
            pe.wait_ge(s["gates_in"], 16)

            def turn_x(t, p):
                pe.wait_ge(s["xn_done"], t + 1)
                pe.wait_ge(s["xT_free"], t + 1)
                for k in range(KD):
                    mm = nc.tensor.transpose(xT_ps[:, k * P:(k + 1) * P], xn[:, p, k * P:(k + 1) * P], chip.ident[:])
                mm.then_inc(s["xT_full"], 1)

            def logits(t, p):
                pe.wait_ge(s["xT_free"], t + 2)
                pe.wait_ge(s["top_done"], t + 1)
                for k in range(KD):
                    mm = nc.tensor.matmul(l_ps[:, 0:E], xT[:, p, k, :], wg[:, k, :], start=(k == 0), stop=(k == KD - 1))
                mm.then_inc(s["l_full"], 1)

            def up(u, p, e, r):
                if isinstance(u, int) and u == 0:
                    pe.wait_ge(s["weights_in"], 48 * E)
                pe.wait_ge(s["h_done"], u + 1)
                for o, wt, sm_ in ((g_ps, w0, "g_full"), (u_ps, w1, "u_full")):
                    for k in range(KD):
                        mm = nc.tensor.matmul(o[r][:], xT[:, p, k, :], wt[:, k, e * F:(e + 1) * F], start=(k == 0), stop=(k == KD - 1))
                    mm.then_inc(s[sm_], 1)

            def turn_h(u, p, e, r):
                pe.wait_ge(s["h_done"], u + 3)
                pe.wait_ge(s["hT_free"], u + 1)
                for k in range(FK):
                    mm = nc.tensor.transpose(hT_ps[:, k * P:(k + 1) * P], h[:, r, k * P:(k + 1) * P], chip.ident[:])
                mm.then_inc(s["hT_full"], 1)

            def down(u, p, e, r, t):
                pe.wait_ge(s["hT_free"], u + 2)
                if e == 0:
                    pe.wait_ge(s["o_free"], t + 1)
                for k in range(FK):
                    mm = nc.tensor.matmul(o_ps[:, 0:D], hT[:, r, k, :], wo[:, k, e * D:(e + 1) * D],
                                          start=(e == 0 and k == 0), stop=(e == E - 1 and k == FK - 1))
                if e == E - 1:
                    mm.then_inc(s["o_full"], 1)

            mixture_walk(pe, turn_x=turn_x, logits=logits, up=up, turn_h=turn_h, down=down)

        @block.scalar
        def _(act):
            for n in ("xT_free", "hT_free", "o_free"):
                act.sem_inc(s[n], 1)

            def turn_x(t, p):
                act.wait_ge(s["xT_full"], t + 1)
                if not (isinstance(t, int) and t < 2):
                    act.wait_ge(s["u_full"], E * (t - 1))
                nc.scalar.activation(xT[:, p, :, :].rearrange("p k t -> p (k t)"), xT_ps[:, 0:D], ACT.Copy).then_inc(s["xT_free"], 1)

            def ratio(t, p):
                act.wait_ge(s["top_done"], t + 2)
                nc.scalar.activation(e2[:, p:p + 1], d12[:, p:p + 1], ACT.Exp).then_inc(s["e2_done"], 1)

            def mul(u, p, e, r):
                act.wait_ge(s["g_full"], u + 1)
                act.wait_ge(s["h_done"], u + 1)
                nc.scalar.activation(si[:, r, :], g_ps[r][:], ACT.Silu).then_inc(s["si_done"], 1)

            def turn_h(u, p, e, r):
                act.wait_ge(s["hT_full"], u + 1)
                nc.scalar.activation(hT[:, r, :, :].rearrange("p k t -> p (k t)"), hT_ps[:], ACT.Copy).then_inc(s["hT_free"], 1)

            def down(u, p, e, r, t):
                if e == E - 1:
                    act.wait_ge(s["o_full"], t + 1)
                    act.wait_ge(s["x_done"], t + 1)
                    nc.scalar.activation(res[:, p, :], o_ps[:, 0:D], ACT.Identity, scale=gate).then_inc(s["o_free"], 1)

            mixture_walk(act, turn_x=turn_x, ratio=ratio, mul=mul, turn_h=turn_h, down=down)

        @block.vector
        def _(dve):
            step = Count(s["dve_step"])

            def link(ins):
                ins.then_inc(s["dve_step"], 1)
                dve.wait_ge(s["dve_step"], step.up())

            dve.sem_inc(s["top_done"], 1)
            dve.sem_inc(s["h_done"], 2)

            def stats(t, p):
                step.enter(12 * t)
                link(nc.vector.bn_stats(stat[:, p, :], tile_of(chip, t)))
                chip.settle(dve)
                nc.vector.bn_aggr(mv[:, p, :], stat[:, p, :]).then_inc(s["stats_done"], 1)

            def normalise(t, p):
                dve.wait_ge(s["rstd_done"], t + 1)
                nc.vector.tensor_scalar(xn[:, p, :], tile_of(chip, t), mv[:, p, 0:1], rs[:, p:p + 1],
                                        ALU.subtract, ALU.mult).then_inc(s["xn_done"], 1)

            def pick(t, p):
                step.enter(12 * t + 1)
                dve.wait_ge(s["l_full"], t + 1)
                link(nc.vector.tensor_copy(lg[:, p, :], l_ps[:, 0:E]))
                chip.settle(dve)
                link(nc.vector.max(top[:, p, :], lg[:, p, :]))
                chip.settle(dve)
                link(nc.vector.max_index(idx[:, p, :], top[:, p, :], lg[:, p, :]))
                link(nc.vector.tensor_copy(idxf[:, p, :], idx[:, p, 0:2]))
                link(nc.vector.tensor_tensor(d12[:, p:p + 1], top[:, p, 1:2], top[:, p, 0:1], ALU.subtract))
                dve.sem_inc(s["top_done"], 1)

            def weigh(t, p):
                step.enter(12 * t + 6)
                dve.wait_ge(s["e2_done"], t + 1)
                link(nc.vector.tensor_scalar(g1[:, p:p + 1], e2[:, p:p + 1], 1.0, None, ALU.add))
                link(nc.vector.reciprocal(g1[:, p:p + 1], g1[:, p:p + 1]))
                link(nc.vector.tensor_tensor(g2[:, p:p + 1], g1[:, p:p + 1], e2[:, p:p + 1], ALU.mult))
                link(nc.vector.tensor_scalar(Ga[:, p, :], chip.iota[:, 0:E], idxf[:, p, 0:1], g1[:, p:p + 1], ALU.is_equal, ALU.mult))
                link(nc.vector.tensor_scalar(Gb[:, p, :], chip.iota[:, 0:E], idxf[:, p, 1:2], g2[:, p:p + 1], ALU.is_equal, ALU.mult))
                link(nc.vector.tensor_tensor(Ga[:, p, :], Ga[:, p, :], Gb[:, p, :], ALU.add))

            def mul(u, p, e, r):
                dve.wait_ge(s["si_done"], u + 1)
                dve.wait_ge(s["u_full"], u + 1)
                if not (isinstance(u, int) and u < 2):
                    dve.wait_ge(s["hT_full"], u - 1)
                nc.vector.scalar_tensor_tensor(out=h[:, r, :], in0=si[:, r, :], scalar=Ga[:, p, e:e + 1], in1=u_ps[r][:],
                                               op0=ALU.mult, op1=ALU.mult).then_inc(s["h_done"], 1)

            mixture_walk(dve, stats=stats, normalise=normalise, pick=pick, weigh=weigh, mul=mul)

        @block.gpsimd
        def _(pool):
            pool.sem_inc(s["x_done"], 2)

            def rstd(t, p):
                pool.wait_ge(s["stats_done"], t + 1)
                chip.settle(pool)
                nc.gpsimd.tensor_scalar(ve[:, p:p + 1], mv[:, p, 1:2], 1e-5, None, ALU.add).then_inc(s["pool_step"], 1)
                pool.wait_ge(s["pool_step"], t + 1)
                nc.gpsimd.tensor_tensor(rs[:, p:p + 1], ve[:, p:p + 1], chip.neghalf[:, 0:1], ALU.pow).then_inc(s["rstd_done"], 1)

            def down(u, p, e, r, t):
                if e == E - 1:
                    pool.wait_ge(s["o_free"], t + 2)
                    nc.gpsimd.tensor_tensor(tile_of(chip, t), tile_of(chip, t), res[:, p, :], ALU.add).then_inc(s["x_done"], 1)

            mixture_walk(pool, stats=rstd, down=down)


def mixture_walk(eng, stats=None, normalise=None, turn_x=None, logits=None, pick=None, ratio=None, weigh=None,
                 up=None, mul=None, turn_h=None, down=None):
    E = 8
    heads = {0: stats, 1: normalise, 2: turn_x, 3: logits, 4: pick, 5: ratio, 6: weigh}

    def head(e, t, p):
        if heads.get(e):
            heads[e](t, p)

    def unit(t, p, e, more):
        u = t * E + e
        if up:
            up(u, p, e, u_par(e))
        if more:
            head(e, t + 1, 1 - p)
        if mul:
            mul(u, p, e, u_par(e))
        for lag, f in ((1, turn_h), (2, down)):
            if f is None:
                continue
            ee, tt, pp = e - lag, t, p
            if ee < 0:
                ee, tt, pp = ee + E, t - 1, 1 - p
            if isinstance(tt, int) and tt < 0:
                continue
            args = (tt * E + ee, pp, ee, u_par(ee))
            f(*args, tt) if f is down else f(*args)

    def u_par(e):
        return e % 2

    for e in range(7):
        head(e, 0, 0)
    for t in range(2):
        for e in range(E):
            unit(t, t % 2, e, True)
    with eng.Fori(1, T // 2 - 1) as it:
        for p in range(2):
            for e in range(E):
                unit(it * 2 + p, p, e, True)
    for t in range(T - 2, T):
        for e in range(E):
            unit(t, t % 2, e, t < T - 1)
    u = T * E
    if turn_h:
        turn_h(u - 1, 1, E - 1, 1)
    if down:
        down(u - 2, 1, E - 2, 0, T - 1)
        down(u - 1, 1, E - 1, 1, T - 1)


def clear_semaphores(nc):
    with nc.Block() as block:
        @block.gpsimd
        def _(pool):
            for number in sorted(set(nc.released_uncleared_semaphores)):
                pool.sem_clear(range(number, number + 1))


def build(nc, dram):
    ctx = ExitStack()
    with ctx:
        chip = Chip(nc, ctx)
        chip.x = chip.keep("x_sb", [P, T * D])
        chip.ident = chip.keep("ident", [P, P])
        chip.ones = chip.keep("ones", [P, P])
        chip.neghalf = chip.keep("neghalf", [P, 32])
        chip.half = chip.keep("half", [P, 32])
        chip.iota = chip.keep("iota", [P, 32])
        chip.gates = chip.keep("gates", [P, 2 * B])
        chip.vecs = chip.keep("vecs", [P, len(VEC) * D])
        chip.cols = chip.keep("cols", [P, 2 * len(COL)])
        chip.ctxT = chip.keep("ctxT_sb", [P, KD, B * NC])
        chip.headmask = chip.keep("headmask_sb", [P, HH + 2])
        chip.rowmask = chip.keep("rowmask_sb", [P, KCH, P])
        chip.loaded = ctx.enter_context(nc.semaphore("loaded"))
        chip.arena = chip.keep("weights", [P, ARENA])
        chip.w, chip.w_in = {}, {}
        chip.zone(WEIGHTS["L1"], dram, 0)
        chip.zone(WEIGHTS["L2S"] + WEIGHTS["L2"], dram, 0)
        chip.zone(WEIGHTS["L0"] + WEIGHTS["L0F"], dram, ZONE_B)
        chip.zone(WEIGHTS["L1F"], dram, ZONE_B)
        chip.zone(WEIGHTS["L3"], dram, ZONE_B)
        for name in chip.w:
            chip.w_in[name] = ctx.enter_context(nc.semaphore("in_" + name))
        chip.settled = {str(e.engine): ctx.enter_context(nc.semaphore(f"settled{i}")) for i, e in enumerate((nc.vector, nc.gpsimd, nc.scalar, nc.sync))}
        dram = dict(dram)
        dram["a"] = nc.dram_tensor("self_attended", (P, T, D), F32, kind="Internal").ap()
        dram["parts"] = nc.dram_tensor("qk_parts", (2 * B, H // 4, 3, 4, D // H, S), BF16, kind="Internal").ap()
        load_stage(chip, dram)
        stages = [lambda: context_stage(chip, dram, "L0"),
                  lambda: experts_stage(chip, dram),
                  lambda: context_stage(chip, dram, "L1"),
                  lambda: ternary_stage(chip, dram),
                  lambda: (self_stage(chip, dram), clear_semaphores(nc), context_stage(chip, dram, "L2")),
                  lambda: routed_stage(chip, dram),
                  lambda: single_stage(chip, dram),
                  lambda: mixture_stage(chip, dram)]
        for stage in stages:
            stage()
            clear_semaphores(nc)
        with nc.semaphore("stored") as stored, nc.Block() as block:
            @block.sync
            def _(sp):
                sp.dma_start(dram["out"], chip.x[:].rearrange("p (t d) -> p t d", d=D)).then_inc(stored, 16)
                sp.wait_ge(stored, 16)


def rows_first(w):
    k, n = w.shape
    return w.reshape(k // P, P, n).transpose(1, 0, 2)


def by_head(w):
    h, e, d = w.shape
    return w.transpose(1, 0, 2).reshape(e, h * d)


def lay_out(a):
    tiles = lambda m: m.reshape(T, P, m.shape[-1]).transpose(1, 0, 2)
    ins = {"x": tiles(a["x"]), "mask": tiles(a["mask_BxSxS2_ik1"]), "g_xattn": a["g_xattn"], "g_ffn": a["g_ffn"],
           "ctxT": rows_first(a["ctx_1024"].reshape(B * NC, D).T)}
    p = np.arange(P)
    head = (p[:, None] // 16 == np.arange(HH)[None]).astype(np.float32)
    pair = (p[:, None] // 64 == np.arange(2)[None]).astype(np.float32)
    ins["headmask"] = np.concatenate([head, pair], 1)
    row = np.arange(KCH)[None, :, None] * P + p[:, None, None]
    ins["rowmask"] = (row // NC == p[None, None, :] // 16).astype(np.float32)
    for n in VEC:
        ins[n] = a[n]
    for n in COL:
        ins[n] = a[n].reshape(KD, P).T
    ins["L0_Wq"] = rows_first(a["L0_xattn_Wq"].T)
    ins["L0_Wk"] = rows_first(a["L0_xattn_Wk"].T)
    ins["L0_Wv"] = rows_first(a["L0_xattn_Wv"].T)
    ins["L0_Wo"] = rows_first(a["L0_xattn_Wo"].T)
    ins["L0F_protoT"] = rows_first(a["L0_ffn_prototypes"].T)
    ins["L0F_BT"] = rows_first(a["L0_ffn_B"].reshape(512, D).T)
    ins["L0F_A"] = rows_first(a["L0_ffn_A"].transpose(0, 2, 1).reshape(512, D))
    ins["L0F_bias"] = a["L0_ffn_bias"]
    ins["L0F_temp"] = a["L0_ffn_temp"].reshape(1)
    ins["L1F_gate"] = rows_first(a["L1_ffn_w_gate"].T)
    ins["L1F_up"] = rows_first(a["L1_ffn_w_up"].T)
    ins["L1F_down"] = rows_first(a["L1_ffn_w_down"].T)
    ins["L1_Wk"] = rows_first(a["L1_xattn_w_kv"][:, :1024])
    ins["L1_Wv"] = rows_first(a["L1_xattn_w_kv"][:, 1024:])
    ins["L1_WqT"] = rows_first(a["L1_xattn_w_q"].T)
    ins["L1_Wo1"] = rows_first(a["L1_xattn_w_out1"])
    ins["L1_Wo"] = rows_first(a["L1_xattn_w_out2"])
    ins["L2S_Wq"] = rows_first(by_head(a["L2_xattn_Wq1"]))
    ins["L2S_Wk"] = rows_first(by_head(a["L2_xattn_Wk1"]))
    ins["L2S_Wv"] = rows_first(by_head(a["L2_xattn_Wv1"]))
    ins["L2S_Wo"] = rows_first(a["L2_xattn_Wo1"])
    ins["L2_rw"] = a["L2_ffn_routing_weights"].reshape(4, P, 8).transpose(1, 0, 2)
    ins["L2_ri"] = a["L2_ffn_router_indices"].reshape(4, P, 2).transpose(1, 0, 2)
    gu = a["L2_ffn_gate_up_proj"]
    gu = np.concatenate([gu[:, :, 0::2], gu[:, :, 1::2]], 2)
    ins["L2_gu"] = rows_first(by_head(gu))
    gb = a["L2_ffn_gate_up_proj_bias"]
    ins["L2_gu_bias"] = np.concatenate([gb[:, 0::2], gb[:, 1::2]], 1).reshape(-1)
    ins["L2_dn"] = rows_first(by_head(a["L2_ffn_down_proj"]))
    ins["L2_dn_bias"] = a["L2_ffn_down_proj_bias"]
    ins["L3_wg"] = rows_first(a["L3_ffn_gate_kernel"])
    ins["L3_w0"] = rows_first(by_head(a["L3_ffn_w0_kernel"]))
    ins["L3_w1"] = rows_first(by_head(a["L3_ffn_w1_kernel"]))
    ins["L3_wo"] = rows_first(by_head(a["L3_ffn_wo_kernel"]))
    ins["L3_WqT"] = rows_first(a["L3_xattn_Wq"].T)
    ins["L3_Wk"] = rows_first(a["L3_xattn_Wk"])
    ins["L3_Wv"] = rows_first(a["L3_xattn_Wv"])
    ins["L2_Wq"] = rows_first(by_head(a["L2_xattn_Wq2"]))
    ins["L2_Wk"] = rows_first(by_head(a["L2_xattn_Wk2"]))
    ins["L2_Wv"] = rows_first(by_head(a["L2_xattn_Wv2"]))
    ins["L2_Wo"] = rows_first(a["L2_xattn_Wo2"])
    ins["L2_Wf"] = rows_first(a["L2_xattn_Wf"])
    return {k: np.ascontiguousarray(v) for k, v in ins.items()}


def kernel(**inputs):
    import concourse.bacc as bacc
    from concourse.bass_utils import run_bass_kernel_spmd

    arrays = lay_out({k: np.asarray(v) for k, v in inputs.items()})
    nc = bacc.Bacc("TRN2", target_bir_lowering=False, num_devices=1)
    dram = {k: nc.dram_tensor("in_" + k, v.shape, mybir.dt.from_np(v.dtype), kind="ExternalInput").ap()
            for k, v in arrays.items()}
    dram["out"] = nc.dram_tensor("out", (P, T, D), F32, kind="ExternalOutput").ap()
    build(nc, dram)
    got = run_bass_kernel_spmd(nc, [{"in_" + k: v for k, v in arrays.items()}], core_ids=[0]).results[0]["out"]
    return got.transpose(1, 0, 2).reshape(B, S, D)
```

```python
from contextlib import ExitStack

import concourse.bass as bass
from concourse import mybir
import numpy as np

P = 128
D = 256
KD = D // P
B, S = 4, 1024
T = B * S // P
TB = S // P
CH = 4
CT = CH * P
NC = 77
H = 16
HH = 8
HK = HH * NC
BK = HK // 2
KCH = -(-HK // P)
KLAST = HK - (KCH - 1) * P
UN = 2 * CH
PBUF = 4

F32 = mybir.dt.float32
BF16 = mybir.dt.bfloat16
I32 = mybir.dt.int32
U32 = mybir.dt.uint32
ACT = mybir.ActivationFunctionType
ALU = mybir.AluOpType
AX = mybir.AxisListType

VEC = ["L0_xattn_bo", "L1_xattn_gamma", "L2_xattn_bo1", "L2_xattn_bo2", "L2_xattn_bf",
       "L2_xattn_g1", "L2_xattn_b1", "L2_xattn_g2", "L2_xattn_b2", "L2_xattn_g3", "L2_xattn_b3", "L3_xattn_bv"]
WEIGHTS = {"L0": ["L0_Wq", "L0_Wk", "L0_Wv", "L0_Wo"],
           "L0F": ["L0F_protoT", "L0F_BT", "L0F_A", "L0F_bias"],
           "L1": ["L1_Wk", "L1_Wv", "L1_WqT", "L1_Wo1", "L1_Wo"],
           "L1F": ["L1F_gate", "L1F_up", "L1F_down"],
           "L2S": ["L2S_Wq", "L2S_Wk", "L2S_Wv", "L2S_Wo"],
           "L2": ["L2_Wq", "L2_Wk", "L2_Wv", "L2_Wo", "L2_Wf"],
           "L3": ["L3_WqT", "L3_Wk", "L3_Wv"]}
ZONE_B = 34 * 256
ARENA = ZONE_B + 24 * 256
COL = ["L0_xattn_bq", "L0_xattn_bk", "L0_xattn_bv", "L3_xattn_bq", "L3_xattn_bk"]


class Count:

    def __init__(self, sem, start=0):
        self.sem, self.base, self.k = sem, start, 0

    def enter(self, base):
        self.base, self.k = base, 0

    def up(self, n=1):
        self.k += n
        return self.base + self.k


class Chip:

    def __init__(self, nc, ctx):
        self.nc, self.ctx = nc, ctx

    def keep(self, name, shape, dt=F32):
        return self.ctx.enter_context(self.nc.sbuf_tensor(name, shape, dt))

    def zone(self, names, dram, offset):
        for name in names:
            shape = dram[name].shape
            n = int(np.prod(shape[1:]))
            v = self.arena[0:shape[0], offset:offset + n]
            if len(shape) == 3:
                v = v.rearrange("p (a n) -> p a n", a=shape[1])
            self.w[name] = v
            offset += n

    def load(self, sp, names, dram):
        for name in names:
            sp.dma_start(self.w[name], dram[name]).then_inc(self.w_in[name], 16)

    def settle(self, eng):
        eng.sem_inc(self.settled[str(eng.engine)], 1)

    def col(self, name):
        n = COL.index(name)
        return self.cols[:, 2 * n:2 * n + 2]

    def vec(self, name):
        n = VEC.index(name)
        return self.vecs[:, n * D:(n + 1) * D]


def wide(ap, shape):
    return ap.to_broadcast(shape)


N_LOADED = 16 * (3 + len(VEC) + len(COL) + B)


def load_stage(chip, dram):
    nc = chip.nc
    with ExitStack() as ctx:
        raw_gates = ctx.enter_context(nc.sbuf_tensor("raw_gates", [P, 2 * B], F32))
        gates_in = ctx.enter_context(nc.semaphore("gates_in"))
        zeroed = ctx.enter_context(nc.semaphore("zeroed"))
        block = ctx.enter_context(nc.Block())

        @block.sync
        def _(sp):
            sp.dma_start(raw_gates[:, 0:B], dram["g_xattn"].partition_broadcast(P)).then_inc(gates_in, 16)
            sp.dma_start(raw_gates[:, B:], dram["g_ffn"].partition_broadcast(P)).then_inc(gates_in, 16)
            sp.dma_start(chip.ctxT[:], dram["ctxT"]).then_inc(chip.loaded, 16)
            sp.dma_start(chip.headmask[:], dram["headmask"]).then_inc(chip.loaded, 16)
            sp.dma_start(chip.rowmask[:], dram["rowmask"]).then_inc(chip.loaded, 16)
            for n, name in enumerate(VEC):
                sp.dma_start(chip.vecs[:, n * D:(n + 1) * D], dram[name].partition_broadcast(P)).then_inc(chip.loaded, 16)
            for n, name in enumerate(COL):
                sp.dma_start(chip.cols[:, 2 * n:2 * n + 2], dram[name]).then_inc(chip.loaded, 16)
            sp.dma_start(chip.x[:, 0:TB * D].rearrange("p (t d) -> p t d", d=D),
                         dram["x"][:, 0:TB, :]).then_inc(chip.loaded, 16)
            chip.load(sp, WEIGHTS["L0"], dram)
            for b in range(1, B):
                sp.dma_start(chip.x[:, b * TB * D:(b + 1) * TB * D].rearrange("p (t d) -> p t d", d=D),
                             dram["x"][:, b * TB:(b + 1) * TB, :]).then_inc(chip.loaded, 16)
            chip.load(sp, WEIGHTS["L0F"] + WEIGHTS["L1"], dram)

        @block.gpsimd
        def _(pool):
            nc.gpsimd.memset(chip.ident[:], 0.0).then_inc(zeroed, 1)
            nc.gpsimd.memset(chip.neghalf[:], -0.5)
            nc.gpsimd.memset(chip.half[:], 0.5)
            nc.gpsimd.memset(chip.ones[:], 1.0)
            pool.wait_ge(zeroed, 1)
            nc.gpsimd.affine_select(out=chip.ident[:], in_=chip.ident[:], compare_op=ALU.not_equal, fill=1.0,
                                    base=0, pattern=[[-1, P]], channel_multiplier=1)
            nc.gpsimd.iota(chip.iota[:], [[1, 32]], base=0, channel_multiplier=0,
                           allow_small_or_imprecise_dtypes=True)

        @block.scalar
        def _(act):
            act.wait_ge(gates_in, 32)
            nc.scalar.activation(chip.gates[:], raw_gates[:], ACT.Tanh)


def walk(more, early, front, unit, tail, turn, out, last, lag=2):
    for j in range(2):
        for u in range(UN):
            unit(j, u)
            if u >= lag:
                turn(j, u - lag)
            elif j:
                turn(j - 1, u - lag + UN)
            if u == 2 and (more or not j):
                early(j)
            if u == 4 and (more or not j):
                front(j)
            if j and u >= 2:
                out(0, u - 2)
    if more:
        tail()
    for u in range(UN - lag, UN):
        turn(1, u)
    for piece in range(6):
        out(1, piece)
    if more:
        last()


def context_stage(chip, dram, kind):
    nc = chip.nc
    w = chip.w
    L = {"L0": 0, "L1": 1, "L2": 2}[kind]
    scale = {"L0": 0.25, "L1": 0.125, "L2": 1.0 / np.sqrt(np.float32(NC))}[kind]
    scale = float(np.float32(scale))
    gate = chip.gates[:, L:L + 1]
    fold = kind == "L1"
    with ExitStack() as ctx:
        def sb(name, shape, dt=F32):
            return ctx.enter_context(nc.sbuf_tensor(f"{kind}_{name}", shape, dt))

        def sem(name):
            return ctx.enter_context(nc.semaphore(f"{kind}_{name}"))

        S_ps = [ctx.enter_context(nc.psum_tensor(f"{kind}_scores{i}", [P, 2, 512], F32)) for i in range(2)]
        T_ps = ctx.enter_context(nc.psum_tensor(f"{kind}_turned", [P, 1024], F32))
        R_ps = [ctx.enter_context(nc.psum_tensor(f"{kind}_ring{i}", [P, 512], F32)) for i in range(2)]
        ctx_rep = sb("ctx_rep", [P, KD, HK])
        xn = sb("xn", [P, CH, D])
        xT = sb("xT", [P, 2 if fold else 1, KD, CT])
        prob = sb("prob", [P, PBUF, HK])
        probT = sb("probT", [P, 2, 2, KCH, CT])
        oT = sb("oT", [P, 2, CT])
        res = sb("res", [P, CH, D])
        mx = sb("mx", [P, 2, HH])
        sm = sb("sm", [P, 4, HH])
        rc = sb("rc", [P, 4, HH])
        stat = sb("stat", [P, 2, CH, 6])
        mv = sb("mv", [P, 2, CH, 2])
        rs = sb("rs", [P, 2, CH])
        ve = sb("ve", [P, 2, CH])
        if fold:
            kfold = sb("kfold", [P, KD, 2 * HK])
            vrow = sb("vrow", [P, 2 * KCH, D])
            stat2 = sb("stat2", [P, CH, 6])
            mv2 = sb("mv2", [P, CH, 2])
            rs2 = sb("rs2", [P, CH])
            ve2 = sb("ve2", [P, CH])
        else:
            kT = sb("kT", [P, 2, NC])
            kblk = sb("kblk", [P, 2, HH, NC])
            vrow = sb("vrow", [P, 2, KCH, P])
            qT = sb("qT", [P, 2, KD, CT])
        spare = probT[:].rearrange("p j f c t -> p (j f c t)")
        if fold:
            kpair, vpair = (spare[:, n * 2 * HK:(n + 1) * 2 * HK].rearrange("p (m a k) -> p m a k", a=2, k=NC) for n in range(2))
            kT, vT = (spare[:, (8 + n) * HK:(9 + n) * HK].rearrange("p (m k) -> p m k", k=NC) for n in range(2))
            vfoldT = spare[:, 4 * HK:4 * HK + KD * 2 * HK].rearrange("p (c r) -> p c r", c=KD)
        else:
            vraw = spare[:, 0:2 * KCH * P].rearrange("p (f c d) -> p f c d", f=2, c=KCH)
        gvec = sb("gvec", [P, 2 * D])
        if kind == "L0":
            mask_i = sb("mask_i", [P, TB, NC], I32)
            unmask = sb("unmask", [P, TB, NC], U32)
            floor = sb("floor", [P, 1])
        mask_in, mask_used, unmasked = sem("mask_in"), sem("mask_used"), sem("unmasked")
        rep_done, rep_free = sem("rep_done"), sem("rep_free")
        blocks_done = sem("blocks_done")
        pairs_done = sem("pairs_done")
        stats_done, rstd_done, xn_done, xn_free = sem("stats_done"), sem("rstd_done"), sem("xn_done"), sem("xn_free")
        ring_full, ring_free = sem("ring_full"), sem("ring_free")
        s_full = sem("s_full")
        shifted, exp_done, inv_done, p_done = sem("shifted"), sem("exp_done"), sem("inv_done"), sem("p_done")
        t_full, t_free = sem("t_full"), sem("t_free")
        stats2_done, rstd2_done, norm2_done = sem("stats2_done"), sem("rstd2_done"), sem("norm2_done")
        stored = sem("stored")
        x_done = sem("x_done")
        dve_step, pool_step, const_done = sem("dve_step"), sem("pool_step"), sem("const_done")
        block = ctx.enter_context(nc.Block())

        def s_view(U):
            return S_ps[U % 2][:, :, 0:BK].rearrange("p a (h k) -> p a h k", k=NC)

        def p_view(u):
            return prob[:, u % PBUF, :].rearrange("p (a h k) -> p a h k", a=2, k=NC)

        def rows(c):
            return P if c < KCH - 1 else KLAST

        at = {}
        AHEAD = {"L0": 6, "L1": 22, "L2": 6}[kind] + 2 + (0 if fold else 2)
        RINGS = AHEAD + 2 + (0 if fold else 2) + 2 * 6

        def nothing(*a):
            pass

        if kind == "L1":
            @block.sync
            def _(sp):
                chip.load(sp, WEIGHTS["L1F"], dram)

        if kind == "L0":
            @block.sync
            def _(sp):
                with sp.Fori(0, B) as b:
                    sp.wait_ge(mask_used, b + 1)
                    sp.dma_start(mask_i[:], dram["mask"][:, bass.ts(b, TB), :]).then_inc(mask_in, 16)

        @block.tensor
        def _(pe):
            ring = Count(ring_full)
            stepfree = Count(ring_free)

            def bank():
                pe.wait_ge(ring_free, stepfree.up())
                return R_ps[(stepfree.k - 1) % 2]

            def drained():
                pe.wait_ge(ring_free, stepfree.base + 2 + stepfree.k)

            pe.sem_inc(rep_free, 1)
            pe.sem_inc(xn_free, 1)
            pe.sem_inc(t_full, PBUF)
            if L == 0:
                pe.wait_ge(chip.loaded, N_LOADED)
            for name in WEIGHTS[kind]:
                pe.wait_ge(chip.w_in[name], 16)

            def batch(b, more):
                stepfree.enter(0 if b is None else AHEAD + b * RINGS)
                nb = 0 if b is None else b + 1

                def setup():
                    pe.wait_ge(rep_done, nb + 1)
                    if not fold:
                        for m in range(2):
                            o = bank()
                            for k in range(KD):
                                mm = nc.tensor.matmul(o[:, 0:NC], w[f"{kind}_Wk"][:, k, m * P:(m + 1) * P], ctx_rep[:, k, 0:NC],
                                                      start=(k == 0), stop=(k == KD - 1))
                            mm.then_inc(ring_full, 1)
                        for hf in range(2):
                            for group in (range(KCH - 1), range(KCH - 1, KCH)):
                                o = bank()
                                for n, c in enumerate(group):
                                    for k in range(KD):
                                        mm = nc.tensor.matmul(o[0:rows(c), n * P:(n + 1) * P], ctx_rep[:, k, c * P:c * P + rows(c)],
                                                              w[f"{kind}_Wv"][:, k, hf * P:(hf + 1) * P],
                                                              start=(k == 0), stop=(k == KD - 1))
                                mm.then_inc(ring_full, 1)
                        at["setup", b is None] = stepfree.k
                        pe.sem_inc(rep_free, 1)
                        return
                    for name in ("L1_Wk", "L1_Wv"):
                        for q in range(2):
                            o = bank()
                            for n in range(4):
                                for k in range(KD):
                                    m = 4 * q + n
                                    mm = nc.tensor.matmul(o[:, n * NC:(n + 1) * NC], w[name][:, k, m * P:(m + 1) * P],
                                                          ctx_rep[:, k, 0:NC], start=(k == 0), stop=(k == KD - 1))
                            mm.then_inc(ring_full, 1)
                    at["pairs", b is None] = stepfree.k
                    pe.sem_inc(rep_free, 1)
                    pe.wait_ge(pairs_done, nb + 1)
                    for name, pair in (("L1_WqT", kpair), ("L1_Wo1", vpair)):
                        for dh in range(KD):
                            for group in ((0, 1, 2), (3, 4, 5), (6, 7)):
                                o = bank()
                                for n, m in enumerate(group):
                                    mm = nc.tensor.matmul(o[:, n * 2 * NC:(n + 1) * 2 * NC], w[name][:, m, dh * P:(dh + 1) * P],
                                                          pair[:, m, :, :].rearrange("p a k -> p (a k)"), start=True, stop=True)
                                mm.then_inc(ring_full, 1)
                    drained()
                    for hf in range(2):
                        for group in ((0, 1), (2, 3), (4,)):
                            o = bank()
                            for n, c in enumerate(group):
                                for dh in range(KD):
                                    mm = nc.tensor.transpose(o[0:rows(c), n * D + dh * P:n * D + (dh + 1) * P],
                                                             vfoldT[:, dh, hf * HK + c * P:hf * HK + c * P + rows(c)], chip.ident[:])
                            mm.then_inc(ring_full, 1)
                    drained()

                def front(j):
                    g = 0 if b is None else 2 * b + j + 1
                    j = 1 - j
                    pe.wait_ge(xn_done, (16 if kind == "L2" else 4) * (g + 1))
                    for dh in range(KD):
                        o = bank()
                        for i in range(CH):
                            mm = nc.tensor.transpose(o[:, i * P:(i + 1) * P], xn[:, i, dh * P:(dh + 1) * P], chip.ident[:])
                        mm.then_inc(ring_full, 1)
                    drained()
                    pe.sem_inc(xn_free, 1)
                    at["front", j, more] = stepfree.k
                    if fold:
                        return
                    for m in range(2):
                        o = bank()
                        for k in range(KD):
                            mm = nc.tensor.matmul(o[:], w[f"{kind}_Wq"][:, k, m * P:(m + 1) * P], xT[:, j if fold else 0, k, :],
                                                  start=(k == 0), stop=(k == KD - 1))
                        mm.then_inc(ring_full, 1)
                    at["front", j, more] = stepfree.k

                def scores(j, u):
                    U = 2 * UN * b + UN * j + u
                    i, hf = u // 2, u % 2
                    if u == 0:
                        pe.wait_ge(ring_free, stepfree.base + 2 + (at["front", j, more] if j else 0))
                    if not fold and u == 0 and j == 0:
                        pe.wait_ge(blocks_done, b + 1)
                    pe.wait_ge(shifted, U + 1)
                    for a in range(2):
                        if fold:
                            for k in range(KD):
                                mm = nc.tensor.matmul(S_ps[u % 2][:, a, 0:BK], xT[:, j if fold else 0, k, i * P:(i + 1) * P],
                                                      kfold[:, k, hf * HK + a * BK:hf * HK + (a + 1) * BK],
                                                      start=(k == 0), stop=(k == KD - 1))
                        else:
                            mm = nc.tensor.matmul(S_ps[u % 2][:, a, 0:BK], qT[:, j, hf, i * P:(i + 1) * P],
                                                  kblk[:, hf, 4 * a:4 * a + 4, :].rearrange("p h k -> p (h k)"),
                                                  start=True, stop=True)
                    mm.then_inc(s_full, 1)

                def turn(j, u):
                    U = 2 * UN * b + UN * j + u
                    pe.wait_ge(p_done, U + 1)
                    pe.wait_ge(t_free, U + 1)
                    for c in range(KCH):
                        mm = nc.tensor.transpose(T_ps[0:rows(c), c * P:(c + 1) * P], prob[:, u % PBUF, c * P:c * P + rows(c)],
                                                 chip.ident[:])
                    mm.then_inc(t_full, 1)

                def out(j, piece):
                    g = 2 * b + j
                    if piece == 2:
                        drained()
                    o = bank()
                    if piece < 2:
                        pe.wait_ge(t_free, 1 + UN * (g + 1))
                        if fold:
                            for r in range(2 * KCH):
                                hf, c = r // KCH, r % KCH
                                mm = nc.tensor.matmul(o[:], vrow[0:rows(c), r, piece * P:(piece + 1) * P],
                                                      probT[0:rows(c), j, hf, c, :], start=(r == 0), stop=(r == 2 * KCH - 1))
                        else:
                            for c in range(KCH):
                                mm = nc.tensor.matmul(o[:], vrow[0:rows(c), piece, c, :], probT[0:rows(c), j, piece, c, :],
                                                      start=(c == 0), stop=(c == KCH - 1))
                        mm.then_inc(ring_full, 1)
                        if more:
                            at["out"] = stepfree.k
                        return
                    i = piece - 2
                    for k in range(KD):
                        mm = nc.tensor.matmul(o[:, 0:D], oT[:, k, i * P:(i + 1) * P], w[f"{kind}_Wo"][:, k, :],
                                              start=(k == 0), stop=(k == KD - 1))
                    mm.then_inc(ring_full, 1)
                    at["res", j, more] = stepfree.k
                if b is None:
                    setup()
                    front(1)
                    assert stepfree.k == AHEAD, stepfree.k
                    return
                walk(more, nothing, front, scores, nothing if fold else setup, turn, out, setup if fold else nothing)
                assert stepfree.k == (RINGS if more else RINGS - AHEAD), stepfree.k

            batch(None, True)
            with pe.Fori(0, B - 1) as b:
                batch(b, True)
            batch(B - 1, False)

        @block.scalar
        def _(act):
            full = Count(ring_full)
            act.sem_inc(ring_free, 2)
            act.sem_inc(t_free, 1)

            def filled():
                act.wait_ge(ring_full, full.up())
                return R_ps[(full.k - 1) % 2]

            def batch(b, more):
                full.enter(0 if b is None else AHEAD + b * RINGS)

                def setup():
                    if not fold:
                        for m in range(2):
                            o = filled()
                            if L == 0:
                                nc.scalar.activation(kT[:, m, :], o[:, 0:NC], ACT.Identity,
                                                     bias=chip.col("L0_xattn_bk")[:, m:m + 1]).then_inc(ring_free, 1)
                            else:
                                nc.scalar.activation(kT[:, m, :], o[:, 0:NC], ACT.Copy).then_inc(ring_free, 1)
                        for hf in range(2):
                            o = filled()
                            nc.scalar.activation(vraw[:, hf, 0:KCH - 1, :].rearrange("p c d -> p (c d)"), o[:],
                                                 ACT.Copy).then_inc(ring_free, 1)
                            o = filled()
                            nc.scalar.activation(vraw[0:KLAST, hf, KCH - 1, :], o[0:KLAST, 0:P],
                                                 ACT.Copy).then_inc(ring_free, 1)
                        return

                    def copy(dst, src):
                        nc.scalar.activation(dst, src, ACT.Copy).then_inc(ring_free, 1)

                    for dst in (kT, vT):
                        for q in range(2):
                            o = filled()
                            copy(dst[:, 4 * q:4 * q + 4, :].rearrange("p m k -> p (m k)"), o[:, 0:4 * NC])
                    for dst in (kfold, vfoldT):
                        for dh in range(KD):
                            for group in ((0, 1, 2), (3, 4, 5), (6, 7)):
                                o = filled()
                                copy(dst[:, dh, group[0] * 2 * NC:(group[-1] + 1) * 2 * NC], o[:, 0:len(group) * 2 * NC])
                    for hf in range(2):
                        for group in ((0, 1), (2, 3), (4,)):
                            o = filled()
                            r = rows(group[-1])
                            copy(vrow[0:r, hf * KCH + group[0]:hf * KCH + group[-1] + 1, :].rearrange("p c d -> p (c d)"),
                                 o[0:r, 0:len(group) * D])

                def evacuate(dst, o, func=ACT.Copy, **kw):
                    nc.scalar.activation(dst, o, func, **kw).then_inc(ring_free, 1)

                def front(j):
                    j = 1 - j
                    for dh in range(KD):
                        evacuate(xT[:, j if fold else 0, dh, :], filled()[:])
                    if not fold:
                        for m in range(2):
                            if L == 0:
                                evacuate(qT[:, j, m, :], filled()[:], ACT.Identity, bias=chip.col("L0_xattn_bq")[:, m:m + 1])
                            else:
                                evacuate(qT[:, j, m, :], filled()[:])

                def unit(j, u):
                    U = 2 * UN * b + UN * j + u
                    act.wait_ge(shifted, U + 3)
                    nc.scalar.activation(prob[:, u % PBUF, :], prob[:, u % PBUF, :], ACT.Exp, scale=scale).then_inc(exp_done, 1)

                def turn(j, u):
                    U = 2 * UN * b + UN * j + u
                    i, hf = u // 2, u % 2
                    act.wait_ge(t_full, U + 1 + PBUF)
                    nc.scalar.activation(probT[:, j, hf, 0:KCH - 1, i * P:(i + 1) * P],
                                         T_ps[:, 0:(KCH - 1) * P].rearrange("p (c t) -> p c t", t=P), ACT.Copy)
                    nc.scalar.activation(probT[0:KLAST, j, hf, KCH - 1, i * P:(i + 1) * P],
                                         T_ps[0:KLAST, (KCH - 1) * P:KCH * P], ACT.Copy).then_inc(t_free, 1)

                def out(j, piece):
                    g = 2 * b + j
                    if piece < 2:
                        if L == 0:
                            evacuate(oT[:, piece, :], filled()[:], ACT.Identity, bias=chip.col("L0_xattn_bv")[:, piece:piece + 1])
                        else:
                            evacuate(oT[:, piece, :], filled()[:], ACT.Relu if fold else ACT.Copy)
                        return
                    if piece == 2:
                        act.wait_ge(x_done, g + 1)
                    evacuate(res[:, piece - 2, :], filled()[:, 0:D])
                if b is None:
                    setup()
                    front(1)
                    return
                walk(more, nothing, front, unit, nothing if fold else setup, turn, out, setup if fold else nothing)
                assert full.k == (RINGS if more else RINGS - AHEAD), full.k

            batch(None, True)
            with act.Fori(0, B - 1) as b:
                batch(b, True)
            batch(B - 1, False)

        @block.vector
        def _(dve):
            step = Count(dve_step)

            def link(ins):
                ins.then_inc(dve_step, 1)
                dve.wait_ge(dve_step, step.up())

            dve.sem_inc(shifted, 2)
            if L == 0:
                dve.sem_inc(mask_used, 1)
                link(nc.vector.memset(floor[:], -1e9 / scale))
                dve.wait_ge(chip.loaded, N_LOADED)
            first = step.k
            PER = {"L0": 51, "L1": 36, "L2": 32}[kind]
            BEFORE = 0 if kind == "L2" else 1

            def batch(b, more):
                step.enter(first if b is None else b * PER + first + BEFORE)
                nb = 0 if b is None else b + 1

                def replicate():
                    dve.wait_ge(rep_free, nb + 1)
                    nc.vector.tensor_copy(ctx_rep[:].rearrange("p c (h k) -> p c h k", k=NC),
                                          wide(chip.ctxT[:, :, bass.ds(nb * NC, NC)].unsqueeze(2), [P, KD, HH, NC])).then_inc(rep_done, 1)

                def blocks():
                    base = 0 if b is None else AHEAD + b * RINGS
                    if fold:
                        dve.wait_ge(ring_free, base + 2 + at["pairs", b is None])
                        for n, (pair, t) in enumerate(((kpair, kT), (vpair, vT))):
                            ins = nc.vector.tensor_tensor(pair[:], wide(t.unsqueeze(2), [P, HH, 2, NC]),
                                                          wide(chip.headmask[:, 8:10].unsqueeze(1).unsqueeze(3), [P, HH, 2, NC]),
                                                          ALU.mult)
                        ins.then_inc(pairs_done, 1)
                        return
                    dve.wait_ge(ring_free, base + 2 + at["setup", b is None])
                    if b is not None:
                        dve.wait_ge(ring_free, base + 2 + at["out"])
                    for m in range(2):
                        nc.vector.tensor_tensor(kblk[:, m], wide(kT[:, m, :].unsqueeze(1), [P, HH, NC]),
                                                wide(chip.headmask[:, 0:HH].unsqueeze(2), [P, HH, NC]), ALU.mult)
                    for hf in range(2):
                        for r, cs in ((P, slice(0, KCH - 1)), (KLAST, slice(KCH - 1, KCH))):
                            ins = nc.vector.tensor_tensor(vrow[0:r, hf, cs, :], vraw[0:r, hf, cs, :], chip.rowmask[0:r, cs, :], ALU.mult)
                    ins.then_inc(blocks_done, 1)

                def stats(j):
                    g = 0 if b is None else 2 * b + j + 1
                    j = 1 - j
                    for i in range(CH):
                        ins = nc.vector.bn_stats(stat[:, j, i, :], chip.x[:, bass.ds((4 * g + i) * D, D)])
                    link(ins)
                    chip.settle(dve)
                    for i in range(CH):
                        ins = nc.vector.bn_aggr(mv[:, j, i, :], stat[:, j, i, :])
                    ins.then_inc(stats_done, 1)

                def early(j):
                    if kind != "L2":
                        stats(j)
                    if j:
                        replicate()

                def front(j):
                    g = 0 if b is None else 2 * b + j + 1
                    j = 1 - j
                    if kind == "L2":
                        return
                    dve.wait_ge(rstd_done, g + 1)
                    for i in range(CH):
                        nc.vector.tensor_scalar(xn[:, i, :], chip.x[:, bass.ds((4 * g + i) * D, D)], mv[:, j, i, 0:1],
                                                rs[:, j, i:i + 1], ALU.subtract, ALU.mult).then_inc(xn_done, 1)

                def unit(j, u):
                    U = 2 * UN * b + UN * j + u
                    dve.wait_ge(s_full, U + 1)
                    s = s_view(u)
                    shape = [P, 2, 4, NC]
                    if L == 0:
                        i = CH * j + u // 2
                        chip.settle(dve)
                        link(nc.vector.copy_predicated(s, wide(unmask[:, i, :].unsqueeze(1).unsqueeze(1), shape),
                                                       wide(floor[:].unsqueeze(1).unsqueeze(1), shape)))
                    m = mx[:, u % 2, :].rearrange("p (a h) -> p a h", a=2)
                    link(nc.vector.tensor_reduce(m, s, AX.X, ALU.max))
                    dve.wait_ge(t_full, U + 1)
                    nc.vector.tensor_tensor(p_view(u), s, wide(m.unsqueeze(3), shape), ALU.subtract).then_inc(shifted, 1)

                def total(j, u):
                    U = 2 * UN * b + UN * j + u
                    dve.wait_ge(exp_done, U + 1)
                    link(nc.vector.tensor_reduce(sm[:, u % 4, :], prob[:, u % PBUF, :].rearrange("p (h k) -> p h k", k=NC),
                                                 AX.X, ALU.add))
                    nc.vector.reciprocal(rc[:, u % 4, :], sm[:, u % 4, :]).then_inc(inv_done, 1)

                def norm2(j, n, src):
                    g = 2 * b + j
                    for i in range(CH):
                        ins = nc.vector.bn_stats(stat2[:, i, :], src[:, i, :])
                    link(ins)
                    chip.settle(dve)
                    for i in range(CH):
                        ins = nc.vector.bn_aggr(mv2[:, i, :], stat2[:, i, :])
                    ins.then_inc(stats2_done, 1)
                    dve.wait_ge(rstd2_done, g + 1)
                    for i in range(CH):
                        ins = nc.vector.tensor_scalar(src[:, i, :], src[:, i, :], mv2[:, i, 0:1], rs2[:, i:i + 1],
                                                      ALU.subtract, ALU.mult)
                    ins.then_inc(norm2_done, 1)

                def out(j, piece):
                    g = 2 * b + j
                    if kind == "L1" and piece == 5:
                        dve.wait_ge(ring_free, AHEAD + b * RINGS + 2 + at["res", j, more])
                        norm2(j, 0, res)
                if b is None:
                    early(1)
                    front(1)
                    blocks()
                    assert step.k == BEFORE
                    return
                if L == 0:
                    dve.wait_ge(mask_in, 16 * (b + 1))
                    link(nc.vector.tensor_scalar(unmask[:], mask_i[:], 0.0, None, ALU.is_equal))
                    dve.sem_inc(mask_used, 1)
                walk(more, early, front, unit, nothing, total, out, blocks, lag=1)
                assert step.k == PER - (0 if more else BEFORE), (kind, step.k)

            batch(None, True)
            with dve.Fori(0, B - 1) as b:
                batch(b, True)
            batch(B - 1, False)

        @block.gpsimd
        def _(pool):
            step = Count(pool_step)

            def link(ins):
                ins.then_inc(pool_step, 1)
                pool.wait_ge(pool_step, step.up())

            if kind != "L2":
                pool.sem_inc(x_done, 1)
            if L == 0:
                pool.wait_ge(chip.loaded, N_LOADED)
                link(nc.gpsimd.tensor_scalar(gvec[:, 0:D], chip.vec("L0_xattn_bo"), 1.0, gate, ALU.mult, ALU.mult))
            elif L == 1:
                link(nc.gpsimd.tensor_scalar(gvec[:, 0:D], chip.vec("L1_xattn_gamma"), 1.0, gate, ALU.mult, ALU.mult))
            first = step.k
            PER = {"L0": 6, "L1": 6, "L2": 0}[kind]
            BEFORE = 0 if kind == "L2" else 1

            def batch(b, more):
                step.enter(first if b is None else b * PER + first + BEFORE)

                def rstd(j):
                    if kind == "L2":
                        return
                    g = 0 if b is None else 2 * b + j + 1
                    j = 1 - j
                    pool.wait_ge(stats_done, g + 1)
                    chip.settle(pool)
                    link(nc.gpsimd.tensor_scalar(ve[:, j, :], mv[:, j, :, 1], 1e-5, None, ALU.add))
                    nc.gpsimd.tensor_tensor(rs[:, j, :], ve[:, j, :], chip.neghalf[:, 0:CH], ALU.pow).then_inc(rstd_done, 1)

                def rstd2(k, eps):
                    pool.wait_ge(stats2_done, k)
                    chip.settle(pool)
                    link(nc.gpsimd.tensor_scalar(ve2[:], mv2[:, :, 1], eps, None, ALU.add))
                    nc.gpsimd.tensor_tensor(rs2[:], ve2[:], chip.neghalf[:, 0:CH], ALU.pow).then_inc(rstd2_done, 1)

                def divide(j, u):
                    U = 2 * UN * b + UN * j + u
                    pool.wait_ge(inv_done, U + 1)
                    nc.gpsimd.tensor_tensor(prob[:, u % PBUF, :].rearrange("p (h k) -> p h k", k=NC),
                                            prob[:, u % PBUF, :].rearrange("p (h k) -> p h k", k=NC),
                                            wide(rc[:, u % 4, :].unsqueeze(2), [P, HH, NC]), ALU.mult).then_inc(p_done, 1)

                def out(j, piece):
                    if piece != 5:
                        return
                    g = 2 * b + j
                    r = res[:]
                    x = chip.x[:, bass.ds(4 * g * D, CH * D)].rearrange("p (i d) -> p i d", d=D)
                    full = [P, CH, D]

                    def bc(v):
                        return wide(v.unsqueeze(1), full)

                    if kind == "L0":
                        pool.wait_ge(ring_free, AHEAD + b * RINGS + 2 + at["res", j, more])
                        chip.settle(pool)
                        link(nc.gpsimd.tensor_scalar(r, r, 1.0, gate, ALU.mult, ALU.mult))
                        link(nc.gpsimd.tensor_tensor(r, r, bc(gvec[:, 0:D]), ALU.add))
                    if kind == "L1":
                        rstd2(g + 1, 1e-5)
                        pool.wait_ge(norm2_done, g + 1)
                        link(nc.gpsimd.tensor_tensor(r, r, bc(gvec[:, 0:D]), ALU.mult))
                    if kind == "L2":
                        return
                    nc.gpsimd.tensor_tensor(x, x, r, ALU.add).then_inc(x_done, 1)
                    pool.wait_ge(x_done, g + 2)

                if b is None:
                    rstd(1)
                    return
                walk(more, rstd, nothing, nothing, nothing, divide, out, nothing, lag=1)
                assert step.k == PER - (0 if more else BEFORE), (kind, step.k)

            batch(None, True)
            with pool.Fori(0, B - 1) as b:
                batch(b, True)
            batch(B - 1, False)

        if kind == "L2":
            @block.sync
            def _(sp):
                sp.sem_inc(x_done, 1)

                def load(g):
                    sp.wait_ge(xn_free, g + 1)
                    chip.settle(sp)
                    sp.dma_start(xn[:], dram["a"][:, bass.ds(g * CH, CH), :]).then_inc(xn_done, 16)

                def batch(b, more):
                    load(2 * b + 1)
                    if more:
                        load(2 * b + 2)
                    for j in range(2):
                        sp.wait_ge(ring_free, AHEAD + b * RINGS + 2 + at["res", j, more])
                        chip.settle(sp)
                        sp.dma_start(dram["b"][:, bass.ds((2 * b + j) * CH, CH), :], res[:]).then_inc(stored, 16)
                        sp.wait_ge(stored, (2 * b + j + 1) * 16)
                        sp.sem_inc(x_done, 1)

                load(0)
                with sp.Fori(0, B - 1) as b:
                    batch(b, True)
                batch(B - 1, False)


def pipelined(eng, phases, n=T, unroll=2, ring=2):
    depth = len(phases) - 1
    lead = depth + ring + (-depth - ring) % unroll

    def step(s, static):
        for k, phase in enumerate(phases):
            t = s - k
            if static:
                if 0 <= t < n:
                    phase(t, t % unroll)
            else:
                phase(t, (static_of[0] - k) % unroll)

    for s in range(lead):
        step(s, True)
    loops = (n - lead) // unroll
    static_of = [0]
    with eng.Fori(0, loops) as it:
        for r in range(unroll):
            static_of[0] = r + lead
            step(it * unroll + (lead + r), False)
    for s in range(lead + loops * unroll, n + depth):
        step(s, True)


class Links:

    def __init__(self, eng, sem, per, n=T, start=0):
        self.eng, self.sem, self.per, self.n, self.start = eng, sem, per, n, start
        self.value = start

    def enter(self, phase, t):
        clamp = (lambda v: max(0, min(v, self.n))) if isinstance(t, int) else (lambda v: v)
        done = sum(m * clamp(t + (phase - i) + (1 if i < phase else 0)) for i, m in enumerate(self.per) if m)
        self.value, self.k, self.expect = done + self.start, 0, self.per[phase]

    def __call__(self, ins):
        self.k += 1
        ins.then_inc(self.sem, 1)
        self.eng.wait_ge(self.sem, self.value + self.k)

    def leave(self):
        assert self.k == self.expect, (self.k, self.expect)


def tile_of(chip, t):
    return chip.x[:, bass.ds(t * D, D)]


def experts_stage(chip, dram):
    nc, w = chip.nc, chip.w
    NE, R = 32, 512
    RK = R // P
    gate = chip.gates[:, B:B + 1]
    with ExitStack() as ctx:
        def sb(name, shape, dt=F32):
            return ctx.enter_context(nc.sbuf_tensor(f"L0F_{name}", shape, dt))

        def sem(name):
            return ctx.enter_context(nc.semaphore(f"L0F_{name}"))

        def ps(name, shape):
            return ctx.enter_context(nc.psum_tensor(f"L0F_{name}", shape, F32))

        xT_ps, d_ps, o_ps = ps("xT_ps", [P, 512]), ps("d_ps", [P, 512]), ps("o_ps", [P, 512])
        h_ps = [ps(f"h_ps{i}", [P, R]) for i in range(2)]
        hT_ps, gT_ps = ps("hT_ps", [P, 512]), ps("gT_ps", [NE, 512])
        stat, mv, ve, rs = sb("stat", [P, 2, 6]), sb("mv", [P, 2, 2]), sb("ve", [P, 2]), sb("rs", [P, 2])
        xn, xT = sb("xn", [P, 2, D]), sb("xT", [P, 2, KD, P])
        square, x2 = sb("square", [P, 2, D]), sb("x2", [P, 2])
        protosq, p2, tinv = sb("protosq", [P, KD, NE]), sb("p2", [P, NE]), sb("tinv", [P, 1])
        dist = sb("dist", [P, 2, NE])
        top, idx, idxf = sb("top", [P, 2, 8]), sb("idx", [P, 2, 8], U32), sb("idxf", [P, 2, 2])
        e2, g1, g2 = sb("e2", [P, 2]), sb("g1", [P, 2]), sb("g2", [P, 2])
        near = sb("near", [P, 2, 2])
        G, Gb = sb("G", [P, 2, NE]), sb("Gb", [P, 2, NE])
        hg, hT, gT, res = sb("hg", [P, 2, R]), sb("hT", [P, 2, RK, P]), sb("gT", [NE, 2, P]), sb("res", [P, 2, D])
        names = """stats_done rstd_done xn_done xT_full xT_free d_full d_free h_full hg_done hT_full hT_free
            gT_full gT_free o_full o_free sc_done top_done near_done e2_done G_done x_done x2_done dve_step pool_step act_step pe_pre pre temp_in""".split()
        s = {n: sem(n) for n in names}
        block = ctx.enter_context(nc.Block())

        @block.sync
        def _(sp):
            sp.dma_start(tinv[:], dram["L0F_temp"].partition_broadcast(P)).then_inc(s["temp_in"], 16)

        @block.tensor
        def _(pe):
            for name in WEIGHTS["L0F"]:
                pe.wait_ge(chip.w_in[name], 16)
            pe.wait_ge(s["pre"], 1)
            for k in range(KD):
                mm = nc.tensor.matmul(d_ps[:, 0:NE], chip.ones[:], protosq[:, k, :], start=(k == 0), stop=(k == KD - 1))
            mm.then_inc(s["pe_pre"], 1)

            def turn_x(t, p):
                pe.wait_ge(s["xn_done"], t + 1)
                pe.wait_ge(s["xT_free"], t + 1)
                for k in range(KD):
                    mm = nc.tensor.transpose(xT_ps[:, k * P:(k + 1) * P], xn[:, p, k * P:(k + 1) * P], chip.ident[:])
                mm.then_inc(s["xT_full"], 1)

            def project(t, p):
                pe.wait_ge(s["xT_free"], t + 2)
                pe.wait_ge(s["d_free"], t + 1)
                for k in range(KD):
                    mm = nc.tensor.matmul(d_ps[:, 0:NE], xT[:, p, k, :], w["L0F_protoT"][:, k, :], start=(k == 0), stop=(k == KD - 1))
                mm.then_inc(s["d_full"], 1)
                pe.wait_ge(s["hg_done"], t + 1)
                for k in range(KD):
                    mm = nc.tensor.matmul(h_ps[p][:], xT[:, p, k, :], w["L0F_BT"][:, k, :], start=(k == 0), stop=(k == KD - 1))
                mm.then_inc(s["h_full"], 1)

            def turn_h(t, p):
                pe.wait_ge(s["hg_done"], t + 3)
                pe.wait_ge(s["hT_free"], t + 1)
                for k in range(RK):
                    mm = nc.tensor.transpose(hT_ps[:, k * P:(k + 1) * P], hg[:, p, k * P:(k + 1) * P], chip.ident[:])
                mm.then_inc(s["hT_full"], 1)
                pe.wait_ge(s["gT_free"], t + 1)
                nc.tensor.transpose(gT_ps[:, 0:P], G[:, p, :], chip.ident[:]).then_inc(s["gT_full"], 1)

            def expand(t, p):
                pe.wait_ge(s["hT_free"], t + 2)
                pe.wait_ge(s["gT_free"], t + 2)
                pe.wait_ge(s["o_free"], t + 1)
                for k in range(RK):
                    nc.tensor.matmul(o_ps[:, 0:D], hT[:, p, k, :], w["L0F_A"][:, k, :], start=(k == 0), stop=False)
                nc.tensor.matmul(o_ps[:, 0:D], gT[:, p, :], w["L0F_bias"], start=False, stop=True).then_inc(s["o_full"], 1)

            none = lambda t, p: None
            pipelined(pe, [none, turn_x, project, none, turn_h, expand])

        @block.scalar
        def _(act):
            for n in ("xT_free", "d_free", "hT_free", "gT_free", "o_free"):
                act.sem_inc(s[n], 1)

            def copy_x(t, p):
                act.wait_ge(s["xn_done"], t + 1)
                act.wait_ge(s["sc_done"], t + 1)
                nc.scalar.activation(square[:, p, :], xn[:, p, :], ACT.Square, accum_out=x2[:, p:p + 1])
                act.wait_ge(s["xT_full"], t + 1)
                nc.scalar.activation(xT[:, p, :, :].rearrange("p k t -> p (k t)"), xT_ps[:, 0:D], ACT.Copy).then_inc(s["xT_free"], 1)

            def distance(t, p):
                act.wait_ge(s["d_full"], t + 1)
                act.wait_ge(s["G_done"], t + 1)
                nc.scalar.activation(dist[:, p, :], d_ps[:, 0:NE], ACT.Copy, scale=2.0).then_inc(s["d_free"], 1)

            def ratio(t, p):
                act.wait_ge(s["near_done"], t + 1)
                nc.scalar.activation(e2[:, p:p + 1], near[:, p, 0:1], ACT.Exp, bias=near[:, p, 1:2], scale=-1.0).then_inc(s["e2_done"], 1)

            def copy_h(t, p):
                act.wait_ge(s["hT_full"], t + 1)
                nc.scalar.activation(hT[:, p, :, :].rearrange("p k t -> p (k t)"), hT_ps[:], ACT.Copy).then_inc(s["hT_free"], 1)
                act.wait_ge(s["gT_full"], t + 1)
                nc.scalar.activation(gT[:, p, :], gT_ps[:, 0:P], ACT.Copy).then_inc(s["gT_free"], 1)

            def result(t, p):
                act.wait_ge(s["o_full"], t + 1)
                act.wait_ge(s["x_done"], t + 1)
                nc.scalar.activation(res[:, p, :], o_ps[:, 0:D], ACT.Identity, scale=gate).then_inc(s["o_free"], 1)

            none = lambda t, p: None
            pipelined(act, [none, copy_x, distance, ratio, copy_h, result])

        @block.vector
        def _(dve):
            link = Links(dve, s["dve_step"], [1, 0, 2, 5, 0, 0])
            link.start, link.k, link.value = 4, 0, 0
            dve.wait_ge(chip.w_in["L0F_protoT"], 16)
            nc.vector.tensor_tensor(protosq[:], w["L0F_protoT"], w["L0F_protoT"], ALU.mult).then_inc(s["pre"], 1)
            dve.wait_ge(s["temp_in"], 16)
            link(nc.vector.tensor_scalar(p2[:, 0:1], tinv[:], -1.0, 0.1, ALU.mult, ALU.max))
            link(nc.vector.tensor_tensor(tinv[:], tinv[:], p2[:, 0:1], ALU.max))
            link(nc.vector.reciprocal(tinv[:], tinv[:]))
            link(nc.vector.tensor_scalar(tinv[:], tinv[:], -1.0, None, ALU.mult))
            dve.wait_ge(s["pe_pre"], 1)
            nc.vector.tensor_copy(p2[:], d_ps[:, 0:NE]).then_inc(s["pre"], 1)
            dve.sem_inc(s["hg_done"], 2)
            dve.sem_inc(s["G_done"], 2)

            def stats(t, p):
                link.enter(0, t)
                link(nc.vector.bn_stats(stat[:, p, :], tile_of(chip, t)))
                chip.settle(dve)
                nc.vector.bn_aggr(mv[:, p, :], stat[:, p, :]).then_inc(s["stats_done"], 1)
                link.leave()

            def normalise(t, p):
                dve.wait_ge(s["rstd_done"], t + 1)
                nc.vector.tensor_scalar(xn[:, p, :], tile_of(chip, t), mv[:, p, 0:1], rs[:, p:p + 1],
                                        ALU.subtract, ALU.mult).then_inc(s["xn_done"], 1)

            def pick(t, p):
                link.enter(2, t)
                dve.wait_ge(s["sc_done"], t + 3)
                chip.settle(dve)
                link(nc.vector.max(top[:, p, :], dist[:, p, :]))
                chip.settle(dve)
                link(nc.vector.max_index(idx[:, p, :], top[:, p, :], dist[:, p, :]))
                nc.vector.tensor_copy(idxf[:, p, :], idx[:, p, 0:2]).then_inc(s["top_done"], 1)
                link.leave()

            def weigh(t, p):
                link.enter(3, t)
                dve.wait_ge(s["top_done"], t + 1)
                dve.wait_ge(s["e2_done"], t + 1)
                link(nc.vector.tensor_scalar(g1[:, p:p + 1], e2[:, p:p + 1], 1.0, None, ALU.add))
                link(nc.vector.reciprocal(g1[:, p:p + 1], g1[:, p:p + 1]))
                link(nc.vector.tensor_tensor(g2[:, p:p + 1], g1[:, p:p + 1], e2[:, p:p + 1], ALU.mult))
                nc.vector.tensor_scalar(G[:, p, :], chip.iota[:], idxf[:, p, 0:1], g1[:, p:p + 1], ALU.is_equal, ALU.mult)
                link(nc.vector.tensor_scalar(Gb[:, p, :], chip.iota[:], idxf[:, p, 1:2], g2[:, p:p + 1], ALU.is_equal, ALU.mult))
                link(nc.vector.tensor_tensor(G[:, p, :], G[:, p, :], Gb[:, p, :], ALU.add))
                dve.sem_inc(s["G_done"], 1)
                dve.wait_ge(s["h_full"], t + 1)
                nc.vector.tensor_tensor(hg[:, p, :].rearrange("p (e r) -> p e r", e=NE), h_ps[p][:].rearrange("p (e r) -> p e r", e=NE),
                                        wide(G[:, p, :].unsqueeze(2), [P, NE, R // NE]), ALU.mult).then_inc(s["hg_done"], 1)
                link.leave()

            none = lambda t, p: None
            pipelined(dve, [stats, normalise, pick, weigh, none, none])

        @block.gpsimd
        def _(pool):
            link = Links(pool, s["pool_step"], [1, 0, 2, 2, 0, 0])
            pool.sem_inc(s["x_done"], 2)
            pool.sem_inc(s["sc_done"], 2)
            pool.wait_ge(s["pre"], 2)

            def rstd(t, p):
                link.enter(0, t)
                pool.wait_ge(s["stats_done"], t + 1)
                chip.settle(pool)
                link(nc.gpsimd.tensor_scalar(ve[:, p:p + 1], mv[:, p, 1:2], 1e-5, None, ALU.add))
                nc.gpsimd.tensor_tensor(rs[:, p:p + 1], ve[:, p:p + 1], chip.neghalf[:, 0:1], ALU.pow).then_inc(s["rstd_done"], 1)
                link.leave()

            def score(t, p):
                link.enter(2, t)
                d = dist[:, p, :]
                pool.wait_ge(s["d_free"], t + 2)
                chip.settle(pool)
                link(nc.gpsimd.tensor_scalar(d, d, x2[:, p:p + 1], None, ALU.subtract))
                link(nc.gpsimd.tensor_tensor(d, d, p2[:], ALU.subtract))
                chip.settle(pool)
                nc.gpsimd.tensor_scalar(d, d, 0.0, None, ALU.min).then_inc(s["sc_done"], 1)
                link.leave()

            def root(t, p):
                link.enter(3, t)
                pool.wait_ge(s["top_done"], t + 1)
                chip.settle(pool)
                link(nc.gpsimd.tensor_scalar(near[:, p, :], top[:, p, 0:2], -1.0, None, ALU.mult))
                link(nc.gpsimd.tensor_tensor(near[:, p, :], near[:, p, :], chip.half[:, 0:2], ALU.pow))
                nc.gpsimd.tensor_tensor(near[:, p, :], near[:, p, :], wide(tinv[:], [P, 2]), ALU.mult).then_inc(s["near_done"], 1)
                link.leave()

            def add(t, p):
                pool.wait_ge(s["o_free"], t + 2)
                nc.gpsimd.tensor_tensor(tile_of(chip, t), tile_of(chip, t), res[:, p, :], ALU.add).then_inc(s["x_done"], 1)

            none = lambda t, p: None
            pipelined(pool, [rstd, none, score, root, none, add])


ROUND = 1.5 * 2.0 ** 23


def ternary_stage(chip, dram):
    nc, w = chip.nc, chip.w
    INNER = 1024
    IK = INNER // P
    COUNT = float(D * INNER)
    gate = chip.gates[:, B + 1:B + 2]
    with ExitStack() as ctx:
        def sb(name, shape, dt=F32):
            return ctx.enter_context(nc.sbuf_tensor(f"L1F_{name}", shape, dt))

        def sem(name):
            return ctx.enter_context(nc.semaphore(f"L1F_{name}"))

        def ps(name, shape, dt=F32):
            return ctx.enter_context(nc.psum_tensor(f"L1F_{name}", shape, dt))

        g_ps, u_ps = ps("gate_ps", [P, INNER]), ps("up_ps", [P, INNER])
        xT_ps, hT_ps, o_ps = ps("xT_ps", [P, 1024], BF16), ps("hT_ps", [P, INNER], BF16), ps("o_ps", [P, 512])
        m_ps = ps("m_ps", [P, 512])
        identb = sb("identb", [P, P], BF16)
        tern = {"gate": sb("t_gate", [P, KD, INNER], BF16), "up": sb("t_up", [P, KD, INNER], BF16), "down": sb("t_down", [P, IK, D], BF16)}
        absw, rowsum = sb("absw", [P, 2048]), sb("rowsum", [P, 3])
        wmean, wscale = sb("wmean", [P, 3]), sb("wscale", [P, 3])
        stat, mv, ve, rs = sb("stat", [P, 2, 6]), sb("mv", [P, 2, 2]), sb("ve", [P, 2]), sb("rs", [P, 2])
        xn, xq, xqb, xT = sb("xn", [P, 2, D]), sb("xq", [P, 2, D]), sb("xqb", [P, 2, D], BF16), sb("xT", [P, 2, KD, P], BF16)
        am, ax, ix = sb("am", [P, 2]), sb("ax", [P, 4]), sb("ix", [P, 2])
        gs, us = sb("gs", [P, 4]), sb("us", [P, 4])
        h, hq, hqb, hT = sb("h", [P, 2, INNER]), sb("hq", [P, 2, INNER]), sb("hqb", [P, 2, INNER], BF16), sb("hT", [P, 2, IK, P], BF16)
        ah, ai, s2, ev = sb("ah", [P, 2]), sb("ai", [P, 2]), sb("s2", [P, 2]), sb("ev", [P, 4])
        minus1, res = sb("minus1", [P, 1]), sb("res", [P, 2, D])
        names = """pre abs_done mean_done tern_done stats_done rstd_done xn_done ix_done xq_done xT_full xT_free gu_full silu_done
            h_done ah_done s2_done hq_done hqb_done hT_full hT_free o_full o_free x_done dve_step pool_step act_step wmean_done""".split()
        s = {n: sem(n) for n in names}
        block = ctx.enter_context(nc.Block())
        order = ("gate", "up", "down")

        @block.sync
        def _(sp):
            chip.load(sp, WEIGHTS["L2S"] + WEIGHTS["L2"], dram)

        @block.tensor
        def _(pe):
            pe.sem_inc(s["xT_full"], 2)
            pe.sem_inc(s["hT_full"], 2)
            pe.wait_ge(s["abs_done"], 3)
            nc.tensor.matmul(m_ps[:, 0:3], chip.ones[:], rowsum[:], start=True, stop=True).then_inc(s["mean_done"], 1)
            pe.wait_ge(s["tern_done"], 4)

            def turn_x(t, q):
                p = q % 2
                pe.wait_ge(s["xq_done"], t + 1)
                pe.wait_ge(s["xT_free"], t + 1)
                for k in range(KD):
                    mm = nc.tensor.transpose(xT_ps[:, k * P:(k + 1) * P], xqb[:, p, k * P:(k + 1) * P], identb[:])
                mm.then_inc(s["xT_full"], 1)

            def widen(t, q):
                p = q % 2
                pe.wait_ge(s["xT_free"], t + 2)
                pe.wait_ge(s["h_done"], t + 1)
                for o, n in ((g_ps, "gate"), (u_ps, "up")):
                    for c in range(INNER // 512):
                        for k in range(KD):
                            mm = nc.tensor.matmul(o[:, c * 512:(c + 1) * 512], xT[:, p, k, :], tern[n][:, k, c * 512:(c + 1) * 512],
                                                  start=(k == 0), stop=(k == KD - 1))
                mm.then_inc(s["gu_full"], 1)

            def turn_h(t, q):
                p = q % 2
                pe.wait_ge(s["hqb_done"], t + 3)
                pe.wait_ge(s["hT_free"], t + 1)
                for k in range(IK):
                    mm = nc.tensor.transpose(hT_ps[:, k * P:(k + 1) * P], hqb[:, p, k * P:(k + 1) * P], identb[:])
                mm.then_inc(s["hT_full"], 1)

            def narrow(t, q):
                p = q % 2
                pe.wait_ge(s["hT_free"], t + 2)
                pe.wait_ge(s["o_free"], t + 1)
                for k in range(IK):
                    mm = nc.tensor.matmul(o_ps[:, 0:D], hT[:, p, k, :], tern["down"][:, k, :], start=(k == 0), stop=(k == IK - 1))
                mm.then_inc(s["o_full"], 1)

            none = lambda t, p: None
            pipelined(pe, [none, none, turn_x, widen, none, none, turn_h, narrow], unroll=4)

        @block.scalar
        def _(act):
            for n in ("xT_free", "hT_free", "o_free"):
                act.sem_inc(s[n], 1)
            act.sem_inc(s["hq_done"], 2)
            for n, name in enumerate(order):
                act.wait_ge(chip.w_in["L1F_" + name], 16)
                if n:
                    act.wait_ge(s["abs_done"], n)
                nc.scalar.activation(absw[:], w["L1F_" + name].rearrange("p a n -> p (a n)"), ACT.Abs,
                                     accum_out=rowsum[:, n:n + 1]).then_inc(s["abs_done"], 1)

            def copy_x(t, q):
                p = q % 2
                act.wait_ge(s["xT_full"], t + 3)
                nc.scalar.activation(xT[:, p, :, :].rearrange("p k t -> p (k t)"), xT_ps[:, 0:D], ACT.Copy).then_inc(s["xT_free"], 1)

            def silu(t, q):
                p = q % 2
                act.wait_ge(s["gu_full"], t + 1)
                act.wait_ge(s["ix_done"], t + 3)
                act.wait_ge(s["hq_done"], t + 1)
                nc.scalar.activation(h[:, p, :], g_ps[:], ACT.Silu, scale=gs[:, q:q + 1]).then_inc(s["silu_done"], 1)

            def quantise(t, q):
                p = q % 2
                act.wait_ge(s["s2_done"], t + 1)
                act.wait_ge(s["hqb_done"], t + 1)
                nc.scalar.activation(hq[:, p, :], h[:, p, :], ACT.Copy, scale=s2[:, p:p + 1], bias=ROUND).then_inc(s["hq_done"], 1)

            def copy_h(t, q):
                p = q % 2
                act.wait_ge(s["hT_full"], t + 3)
                nc.scalar.activation(hT[:, p, :, :].rearrange("p k t -> p (k t)"), hT_ps[:], ACT.Copy).then_inc(s["hT_free"], 1)

            def result(t, q):
                p = q % 2
                act.wait_ge(s["o_full"], t + 1)
                act.wait_ge(s["x_done"], t + 1)
                nc.scalar.activation(res[:, p, :], o_ps[:, 0:D], ACT.Identity, scale=ev[:, q:q + 1]).then_inc(s["o_free"], 1)

            none = lambda t, p: None
            pipelined(act, [none, none, copy_x, none, silu, quantise, copy_h, result], unroll=4)

        @block.vector
        def _(dve):
            link = Links(dve, s["dve_step"], [1, 1, 1, 0, 1, 0, 0, 0])
            link.k = 0
            link(nc.vector.tensor_copy(identb[:], chip.ident[:]))
            dve.wait_ge(s["mean_done"], 1)
            link(nc.vector.tensor_scalar(wmean[:], m_ps[:, 0:3], 1.0 / COUNT, 1e-5, ALU.mult, ALU.max))
            nc.vector.reciprocal(wscale[:], wmean[:]).then_inc(s["wmean_done"], 1)
            dve.wait_ge(s["wmean_done"], 1)
            for n, name in enumerate(order):
                dst = tern[name][:].rearrange("p a n -> p (a n)")
                link(nc.vector.tensor_scalar(absw[:], w["L1F_" + name].rearrange("p a n -> p (a n)"), wscale[:, n:n + 1], ROUND,
                                             ALU.mult, ALU.add))
                link(nc.vector.tensor_scalar(absw[:], absw[:], ROUND - 1.0, ROUND + 1.0, ALU.max, ALU.min))
                nc.vector.tensor_scalar(dst, absw[:], -ROUND, None, ALU.add).then_inc(s["tern_done"], 1)
                dve.wait_ge(s["tern_done"], n + 1)
            dve.sem_inc(s["tern_done"], 1)
            dve.sem_inc(s["h_done"], 1)
            dve.sem_inc(s["hqb_done"], 2)
            link.start = link.k

            def stats(t, q):
                p = q % 2
                link.enter(0, t)
                link(nc.vector.bn_stats(stat[:, p, :], tile_of(chip, t)))
                chip.settle(dve)
                nc.vector.bn_aggr(mv[:, p, :], stat[:, p, :]).then_inc(s["stats_done"], 1)
                link.leave()

            def normalise(t, q):
                p = q % 2
                link.enter(1, t)
                dve.wait_ge(s["rstd_done"], t + 1)
                link(nc.vector.tensor_scalar(xn[:, p, :], tile_of(chip, t), mv[:, p, 0:1], rs[:, p:p + 1], ALU.subtract, ALU.mult))
                nc.vector.tensor_reduce(am[:, p:p + 1], xn[:, p, :], AX.X, ALU.max, apply_absolute_value=True).then_inc(s["xn_done"], 1)
                link.leave()

            def quantise(t, q):
                p = q % 2
                link.enter(2, t)
                dve.wait_ge(s["ix_done"], t + 3)
                dve.wait_ge(s["xT_full"], t + 1)
                link(nc.vector.tensor_scalar(xq[:, p, :], xn[:, p, :], ix[:, p:p + 1], ROUND, ALU.mult, ALU.add))
                nc.vector.tensor_scalar(xqb[:, p, :], xq[:, p, :], ROUND + 127.0, -ROUND, ALU.min, ALU.add).then_inc(s["xq_done"], 1)
                link.leave()

            def multiply(t, q):
                p = q % 2
                link.enter(4, t)
                dve.wait_ge(s["silu_done"], t + 1)
                nc.vector.tensor_tensor(h[:, p, :], h[:, p, :], u_ps[:], ALU.mult).then_inc(s["h_done"], 1)
                dve.wait_ge(s["h_done"], t + 2)
                link(nc.vector.tensor_reduce(ah[:, p:p + 1], h[:, p, :], AX.X, ALU.max, apply_absolute_value=True))
                dve.sem_inc(s["ah_done"], 1)
                link.leave()

            def shift(t, q):
                p = q % 2
                dve.wait_ge(s["hq_done"], t + 3)
                dve.wait_ge(s["hT_full"], t + 1)
                nc.vector.tensor_scalar(hqb[:, p, :], hq[:, p, :], ROUND + 127.0, -ROUND, ALU.min, ALU.add).then_inc(s["hqb_done"], 1)

            none = lambda t, p: None
            pipelined(dve, [stats, normalise, quantise, none, multiply, shift, none, none], unroll=4)

        @block.gpsimd
        def _(pool):
            link = Links(pool, s["pool_step"], [1, 3, 0, 0, 5, 0, 0, 0])
            link.k = 0
            link(nc.gpsimd.memset(minus1[:], -1.0))
            pool.sem_inc(s["x_done"], 2)
            pool.sem_inc(s["ix_done"], 2)
            pool.wait_ge(s["wmean_done"], 1)
            link(nc.gpsimd.tensor_tensor(wmean[:, 2:3], wmean[:, 2:3], gate, ALU.mult))
            link.start = link.k

            def rstd(t, q):
                p = q % 2
                link.enter(0, t)
                pool.wait_ge(s["stats_done"], t + 1)
                chip.settle(pool)
                link(nc.gpsimd.tensor_scalar(ve[:, p:p + 1], mv[:, p, 1:2], 1e-5, None, ALU.add))
                nc.gpsimd.tensor_tensor(rs[:, p:p + 1], ve[:, p:p + 1], chip.neghalf[:, 0:1], ALU.pow).then_inc(s["rstd_done"], 1)
                link.leave()

            def scale_x(t, q):
                p = q % 2
                link.enter(1, t)
                pool.wait_ge(s["xn_done"], t + 1)
                chip.settle(pool)
                link(nc.gpsimd.tensor_scalar(ax[:, q:q + 1], am[:, p:p + 1], 1e-5, 1.0 / 127.0, ALU.max, ALU.mult))
                link(nc.gpsimd.tensor_tensor(gs[:, q:q + 1], ax[:, q:q + 1], wmean[:, 0:1], ALU.mult))
                link(nc.gpsimd.tensor_tensor(us[:, q:q + 1], ax[:, q:q + 1], wmean[:, 1:2], ALU.mult))
                nc.gpsimd.tensor_tensor(ix[:, p:p + 1], ax[:, q:q + 1], minus1[:], ALU.pow).then_inc(s["ix_done"], 1)
                link.leave()

            def scale_h(t, q):
                p = q % 2
                link.enter(4, t)
                pool.wait_ge(s["ah_done"], t + 1)
                link(nc.gpsimd.tensor_tensor(ah[:, p:p + 1], ah[:, p:p + 1], us[:, q:q + 1], ALU.mult))
                chip.settle(pool)
                link(nc.gpsimd.tensor_scalar(ah[:, p:p + 1], ah[:, p:p + 1], 1e-5, 1.0 / 127.0, ALU.max, ALU.mult))
                link(nc.gpsimd.tensor_tensor(ai[:, p:p + 1], ah[:, p:p + 1], minus1[:], ALU.pow))
                link(nc.gpsimd.tensor_tensor(ev[:, q:q + 1], ah[:, p:p + 1], wmean[:, 2:3], ALU.mult))
                link(nc.gpsimd.tensor_tensor(s2[:, p:p + 1], ai[:, p:p + 1], us[:, q:q + 1], ALU.mult))
                pool.sem_inc(s["s2_done"], 1)
                link.leave()

            def add(t, q):
                p = q % 2
                pool.wait_ge(s["o_free"], t + 2)
                nc.gpsimd.tensor_tensor(tile_of(chip, t), tile_of(chip, t), res[:, p, :], ALU.add).then_inc(s["x_done"], 1)

            none = lambda t, p: None
            pipelined(pool, [rstd, scale_x, none, none, scale_h, none, none, add], unroll=4)


def routed_stage(chip, dram):
    nc = chip.nc
    E, F, SEQ = 8, 256, 512
    NT = SEQ // P
    N = NT * E
    gate = chip.gates[:, B + 2:B + 3]
    with ExitStack() as ctx:
        def sb(name, shape, dt=F32):
            return ctx.enter_context(nc.sbuf_tensor(f"L2F_{name}", shape, dt))

        def ps(name, shape):
            return ctx.enter_context(nc.psum_tensor(f"L2F_{name}", shape, F32))

        acc = [ps(f"acc{i}", [P, 512]) for i in range(NT)]
        gu_ps = [ps(f"gu_ps{i}", [P, 512]) for i in range(2)]
        hT_ps = [ps(f"hT_ps{i}", [P, 512]) for i in range(2)]
        wgu, wdn, gub = sb("wgu", [P, KD, E * 2 * F]), sb("wdn", [P, KD, E * D]), sb("gub", [P, E * 2 * F])
        bdn, rw, ri = sb("bdn", [E, D]), sb("rw", [P, NT, E]), sb("ri", [P, NT, 2], I32)
        rif, hot, we, wrow, wT = sb("rif", [P, NT, 2]), sb("hot", [P, NT, E]), sb("we", [P, E, NT]), sb("wrow", [P, NT, E]), sb("wT", [E, SEQ])
        stat, mv, ve, rs = sb("stat", [P, NT, 6]), sb("mv", [P, NT, 2]), sb("ve", [P, NT]), sb("rs", [P, NT])
        xn, xT = sb("xn", [P, NT, D]), sb("xT", [P, NT, KD, P])
        gu, sig, glu, h, hT = sb("gu", [P, 2, 2 * F]), sb("sig", [P, 2, F]), sb("glu", [P, 2, F]), sb("h", [P, 2, F]), sb("hT", [P, 2, KD, P])
        res = sb("res", [P, NT, D])
        names = """router_in small_in weights_in ready stats_done rstd_done xn_done xT_full xT_copied w_done wT_full wT_copied acc_done
            gu_full added clipped sig_done h_done hT_full hT_free res_done dve_step pool_step x_done""".split()
        s = {n: ctx.enter_context(nc.semaphore(f"L2F_{n}")) for n in names}
        expert_in = [ctx.enter_context(nc.semaphore(f"L2F_expert_in{e}")) for e in range(E)]
        block = ctx.enter_context(nc.Block())

        @block.sync
        def _(sp):
            sp.dma_start(rw[:], dram["L2_rw"]).then_inc(s["router_in"], 16)
            sp.dma_start(ri[:], dram["L2_ri"]).then_inc(s["router_in"], 16)
            sp.dma_start(bdn[:], dram["L2_dn_bias"]).then_inc(s["small_in"], 16)
            for e in range(E):
                cols = slice(e * 2 * F, (e + 1) * 2 * F)
                sp.dma_start(wgu[:, :, cols], dram["L2_gu"][:, :, cols]).then_inc(expert_in[e], 16)
                sp.dma_start(gub[:, cols], dram["L2_gu_bias"][cols].partition_broadcast(P)).then_inc(expert_in[e], 16)
                sp.dma_start(wdn[:, :, e * D:(e + 1) * D], dram["L2_dn"][:, :, e * D:(e + 1) * D]).then_inc(expert_in[e], 16)
            for e in range(E):
                sp.wait_ge(expert_in[e], 48)
                sp.sem_inc(s["ready"], NT)

        @block.tensor
        def _(pe):
            pe.sem_inc(s["gu_full"], 2)
            for i in range(NT):
                pe.wait_ge(s["xn_done"], i + 1)
                if i >= 2:
                    pe.wait_ge(s["xT_copied"], i - 1)
                for k in range(KD):
                    mm = nc.tensor.transpose(hT_ps[i % 2][:, k * P:(k + 1) * P], xn[:, i, k * P:(k + 1) * P], chip.ident[:])
                mm.then_inc(s["xT_full"], 1)
            pe.wait_ge(s["w_done"], 1)
            for i in range(NT):
                mm = nc.tensor.transpose(gu_ps[0][0:E, i * P:(i + 1) * P], wrow[:, i, :], chip.ident[:])
            mm.then_inc(s["wT_full"], 1)
            pe.wait_ge(s["wT_copied"], 1)
            pe.wait_ge(s["small_in"], 16)
            pe.wait_ge(s["xT_copied"], NT)
            for i in range(NT):
                nc.tensor.matmul(acc[i][:, 0:D], wT[:, i * P:(i + 1) * P], bdn[:], start=True, stop=True, skip_group_check=True)

            def up(t, q):
                pe.wait_ge(s["ready"], t - q + NT)
                pe.wait_ge(s["added"], t + 1)
                for k in range(KD):
                    mm = nc.tensor.matmul(gu_ps[q % 2][:], xT[:, q, k, :], wgu[:, k, bass.ds((t - q) * P, 2 * F)],
                                          start=(k == 0), stop=(k == KD - 1))
                mm.then_inc(s["gu_full"], 1)

            def turn_h(t, q):
                pe.wait_ge(s["h_done"], t + 1)
                pe.wait_ge(s["hT_free"], t + 1)
                for k in range(KD):
                    mm = nc.tensor.transpose(hT_ps[q % 2][:, k * P:(k + 1) * P], h[:, q % 2, k * P:(k + 1) * P], chip.ident[:])
                mm.then_inc(s["hT_full"], 1)

            def down(t, q):
                pe.wait_ge(s["hT_free"], t + 3)
                for k in range(KD):
                    mm = nc.tensor.matmul(acc[q][:, 0:D], hT[:, q % 2, k, :], wdn[:, k, bass.ds((t - q) * (D // NT), D)],
                                          start=False, stop=True, skip_group_check=True)
                mm.then_inc(s["acc_done"], 1)

            none = lambda t, q: None
            pipelined(pe, [up, none, none, turn_h, down], n=N, unroll=NT)

        @block.scalar
        def _(act):
            act.sem_inc(s["hT_free"], 2)
            for i in range(NT):
                act.wait_ge(s["xT_full"], i + 1)
                nc.scalar.activation(xT[:, i, :, :].rearrange("p k t -> p (k t)"), hT_ps[i % 2][:, 0:D], ACT.Copy).then_inc(s["xT_copied"], 1)
            act.wait_ge(s["wT_full"], 1)
            nc.scalar.activation(wT[:], gu_ps[0][0:E, :], ACT.Copy).then_inc(s["wT_copied"], 1)

            def sigmoid(t, q):
                act.wait_ge(s["clipped"], t + 1)
                nc.scalar.activation(sig[:, q % 2, :], gu[:, q % 2, 0:F], ACT.Sigmoid, scale=1.702).then_inc(s["sig_done"], 1)

            def copy_h(t, q):
                act.wait_ge(s["hT_full"], t + 1)
                nc.scalar.activation(hT[:, q % 2, :, :].rearrange("p k t -> p (k t)"), hT_ps[q % 2][:, 0:D], ACT.Copy).then_inc(s["hT_free"], 1)

            none = lambda t, q: None
            pipelined(act, [none, sigmoid, none, copy_h, none], n=N, unroll=NT)
            act.wait_ge(s["acc_done"], N)
            for i in range(NT):
                nc.scalar.activation(res[:, i, :], acc[i][:, 0:D], ACT.Identity, scale=gate).then_inc(s["res_done"], 1)

        @block.vector
        def _(dve):
            link = Links(dve, s["dve_step"], [0, 3, 1, 0, 0], n=N)
            link.k = 0
            for i in range(NT):
                ins = nc.vector.bn_stats(stat[:, i, :], chip.x[:, i * D:(i + 1) * D])
            link(ins)
            for i in range(NT):
                ins = nc.vector.bn_aggr(mv[:, i, :], stat[:, i, :])
            ins.then_inc(s["stats_done"], 1)
            dve.wait_ge(s["router_in"], 32)
            link(nc.vector.tensor_copy(rif[:], ri[:]))
            for i in range(NT):
                link(nc.vector.tensor_scalar(hot[:, i, :], chip.iota[:, 0:E], rif[:, i, 0:1], None, ALU.is_equal))
                link(nc.vector.scalar_tensor_tensor(out=hot[:, i, :], in0=chip.iota[:, 0:E], scalar=rif[:, i, 1:2], in1=hot[:, i, :],
                                                    op0=ALU.is_equal, op1=ALU.add))
                nc.vector.tensor_tensor(we[:, :, i], hot[:, i, :], rw[:, i, :], ALU.mult)
                link(nc.vector.tensor_tensor(wrow[:, i, :], hot[:, i, :], rw[:, i, :], ALU.mult))
            dve.sem_inc(s["w_done"], 1)
            dve.wait_ge(s["rstd_done"], 1)
            for i in range(NT):
                nc.vector.tensor_scalar(xn[:, i, :], chip.x[:, i * D:(i + 1) * D], mv[:, i, 0:1], rs[:, i:i + 1],
                                        ALU.subtract, ALU.mult).then_inc(s["xn_done"], 1)
            dve.wait_ge(s["wT_copied"], 1)
            dve.sem_inc(s["added"], 2)
            link.start = link.k

            def clip(t, q):
                link.enter(1, t)
                p = q % 2
                dve.wait_ge(s["ready"], t - q + NT)
                dve.wait_ge(s["gu_full"], t + 3)
                if not (isinstance(t, int) and t < 2):
                    dve.wait_ge(s["h_done"], t - 1)
                nc.vector.tensor_tensor(gu[:, p, :], gu_ps[p][:], gub[:, bass.ds((t - q) * P, 2 * F)], ALU.add).then_inc(s["added"], 1)
                dve.wait_ge(s["added"], t + 3)
                link(nc.vector.tensor_scalar(gu[:, p, 0:F], gu[:, p, 0:F], 7.0, None, ALU.min))
                dve.sem_inc(s["clipped"], 1)
                link(nc.vector.tensor_scalar(gu[:, p, F:], gu[:, p, F:], -7.0, 7.0, ALU.max, ALU.min))
                link(nc.vector.tensor_scalar(gu[:, p, F:], gu[:, p, F:], 1.0, None, ALU.add))
                link.leave()

            def swiglu(t, q):
                link.enter(2, t)
                p = q % 2
                dve.wait_ge(s["sig_done"], t + 1)
                link(nc.vector.scalar_tensor_tensor(out=glu[:, p, :], in0=sig[:, p, :], scalar=we[:].rearrange("p e i -> p (e i)")[:, bass.ds(t, 1)],
                                                    in1=gu[:, p, 0:F], op0=ALU.mult, op1=ALU.mult))
                if not (isinstance(t, int) and t < 2):
                    dve.wait_ge(s["hT_full"], t - 1)
                nc.vector.tensor_tensor(h[:, p, :], glu[:, p, :], gu[:, p, F:], ALU.mult).then_inc(s["h_done"], 1)
                link.leave()

            none = lambda t, q: None
            pipelined(dve, [none, clip, swiglu, none, none], n=N, unroll=NT)

        @block.gpsimd
        def _(pool):
            pool.wait_ge(s["stats_done"], 1)
            nc.gpsimd.tensor_scalar(ve[:], mv[:, :, 1], 1e-5, None, ALU.add).then_inc(s["pool_step"], 1)
            pool.wait_ge(s["pool_step"], 1)
            nc.gpsimd.tensor_tensor(rs[:], ve[:], chip.neghalf[:, 0:NT], ALU.pow).then_inc(s["rstd_done"], 1)
            for i in range(NT):
                pool.wait_ge(s["res_done"], i + 1)
                nc.gpsimd.tensor_tensor(chip.x[:, i * D:(i + 1) * D], chip.x[:, i * D:(i + 1) * D], res[:, i, :], ALU.add)


def single_stage(chip, dram):
    nc, w = chip.nc, chip.w
    NCP = 80
    gate = chip.gates[:, 3:4]
    with ExitStack() as ctx:
        def sb(name, shape, dt=F32):
            return ctx.enter_context(nc.sbuf_tensor(f"L3_{name}", shape, dt))

        def ps(name, shape):
            return ctx.enter_context(nc.psum_tensor(f"L3_{name}", shape, F32))

        xT_ps, s_ps, pT_ps, o_ps = ps("xT_ps", [P, 512]), ps("s_ps", [P, 512]), ps("pT_ps", [P, 512]), ps("o_ps", [P, 512])
        pre_ps = [ps(f"pre_ps{i}", [P, 512]) for i in range(4)]
        kT, fold, fbias, v = sb("kT", [P, KD, B * NC]), sb("fold", [P, KD, B * NCP]), sb("fbias", [1, B * NCP]), sb("v", [NC, B, D])
        stat, mv, ve, rs = sb("stat", [P, 2, 6]), sb("mv", [P, 2, 2]), sb("ve", [P, 2]), sb("rs", [P, 2])
        xn, xT = sb("xn", [P, 2, D]), sb("xT", [P, 2, KD, P])
        mx, sm, rc = sb("mx", [P, 2]), sb("sm", [P, 4]), sb("rc", [P, 4])
        pr, pT, res = sb("pr", [P, 2, NC]), sb("pT", [NC, 2, P]), sb("res", [P, 2, D])
        names = """pre_full pre_copied v_done stats_done rstd_done xn_done xT_full xT_free s_full shifted exp_done pT_full pT_free
            o_full o_free x_done dve_step pool_step""".split()
        s = {n: ctx.enter_context(nc.semaphore(f"L3_{n}")) for n in names}
        block = ctx.enter_context(nc.Block())
        NU = 8

        @block.tensor
        def _(pe):
            for name in WEIGHTS["L3"]:
                pe.wait_ge(chip.w_in[name], 16)
            for m in range(KD):
                for k in range(KD):
                    mm = nc.tensor.matmul(pre_ps[m][:, 0:B * NC], w["L3_Wk"][:, k, m * P:(m + 1) * P], chip.ctxT[:, k, :],
                                          start=(k == 0), stop=(k == KD - 1))
                mm.then_inc(s["pre_full"], 1)
            for half in range(2):
                for n in range(2):
                    b = 2 * half + n
                    for k in range(KD):
                        mm = nc.tensor.matmul(pre_ps[2 + half][0:NC, n * D:(n + 1) * D], chip.ctxT[:, k, b * NC:(b + 1) * NC],
                                              w["L3_Wv"][:, k, :], start=(k == 0), stop=(k == KD - 1))
                mm.then_inc(s["pre_full"], 1)
            pe.wait_ge(s["pre_copied"], 2)
            for m in range(KD):
                for k in range(KD):
                    mm = nc.tensor.matmul(pre_ps[m][:, 0:B * NC], w["L3_WqT"][:, k, m * P:(m + 1) * P], kT[:, k, :],
                                          start=(k == 0), stop=(k == KD - 1))
                mm.then_inc(s["pre_full"], 1)
            for k in range(KD):
                mm = nc.tensor.matmul(s_ps[0:1, 0:B * NC], chip.col("L3_xattn_bq")[:, k:k + 1], kT[:, k, :],
                                      start=(k == 0), stop=(k == KD - 1))
            mm.then_inc(s["pre_full"], 1)
            pe.wait_ge(s["pre_copied"], 5)
            pe.wait_ge(s["v_done"], 4)

            def turn_x(t, q):
                pe.wait_ge(s["xn_done"], t + 1)
                pe.wait_ge(s["xT_free"], t + 1)
                for k in range(KD):
                    mm = nc.tensor.transpose(xT_ps[:, k * P:(k + 1) * P], xn[:, q % 2, k * P:(k + 1) * P], chip.ident[:])
                mm.then_inc(s["xT_full"], 1)

            def scores(t, q):
                cols = bass.ds((t - q) * (NCP // NU), NC)
                pe.wait_ge(s["xT_free"], t + 2)
                pe.wait_ge(s["shifted"], t + 1)
                for k in range(KD):
                    nc.tensor.matmul(s_ps[:, 0:NC], xT[:, q % 2, k, :], fold[:, k, cols], start=(k == 0), stop=False)
                nc.tensor.matmul(s_ps[:, 0:NC], chip.ones[0:1, :], fbias[:, cols], start=False, stop=True).then_inc(s["s_full"], 1)

            def turn_p(t, q):
                pe.wait_ge(s["exp_done"], t + 1)
                pe.wait_ge(s["pT_free"], t + 1)
                nc.tensor.transpose(pT_ps[0:NC, 0:P], pr[:, q % 2, :], chip.ident[:]).then_inc(s["pT_full"], 1)

            def values(t, q):
                pe.wait_ge(s["pT_free"], t + 2)
                pe.wait_ge(s["o_free"], t + 4)
                nc.tensor.matmul(o_ps[:, 0:D], pT[:, q % 2, :], v[:].rearrange("k b d -> k (b d)")[:, bass.ds((t - q) * (D // NU), D)],
                                 start=True, stop=True).then_inc(s["o_full"], 1)

            none = lambda t, q: None
            pipelined(pe, [none, turn_x, scores, none, turn_p, values], unroll=NU)

        @block.scalar
        def _(act):
            act.sem_inc(s["xT_free"], 1)
            act.sem_inc(s["pT_free"], 1)
            for m in range(KD):
                act.wait_ge(s["pre_full"], m + 1)
                nc.scalar.activation(kT[:, m, :], pre_ps[m][:, 0:B * NC], ACT.Identity,
                                     bias=chip.col("L3_xattn_bk")[:, m:m + 1]).then_inc(s["pre_copied"], 1)
            for m in range(KD):
                act.wait_ge(s["pre_full"], 5 + m)
                nc.scalar.activation(fold[:, m, :].rearrange("p (b c) -> p b c", c=NCP)[:, :, 0:NC],
                                     pre_ps[m][:, 0:B * NC].rearrange("p (b c) -> p b c", c=NC), ACT.Copy).then_inc(s["pre_copied"], 1)
            act.wait_ge(s["pre_full"], 7)
            nc.scalar.activation(fbias[:].rearrange("p (b c) -> p b c", c=NCP)[:, :, 0:NC],
                                 s_ps[0:1, 0:B * NC].rearrange("p (b c) -> p b c", c=NC), ACT.Copy).then_inc(s["pre_copied"], 1)

            def copy_x(t, q):
                act.wait_ge(s["xT_full"], t + 1)
                nc.scalar.activation(xT[:, q % 2, :, :].rearrange("p k t -> p (k t)"), xT_ps[:, 0:D], ACT.Copy).then_inc(s["xT_free"], 1)

            def exp(t, q):
                act.wait_ge(s["shifted"], t + 2)
                act.wait_ge(s["o_free"], t + 1)
                nc.scalar.activation(pr[:, q % 2, :], pr[:, q % 2, :], ACT.Exp, scale=1.0 / 16.0, accum_out=sm[:, q % 4:q % 4 + 1]).then_inc(s["exp_done"], 1)

            def copy_p(t, q):
                act.wait_ge(s["pT_full"], t + 1)
                nc.scalar.activation(pT[:, q % 2, :], pT_ps[0:NC, 0:P], ACT.Copy).then_inc(s["pT_free"], 1)

            none = lambda t, q: None
            pipelined(act, [none, copy_x, none, exp, copy_p, none], unroll=NU)

        @block.vector
        def _(dve):
            link = Links(dve, s["dve_step"], [1, 0, 1, 0, 0, 1])
            link.k = 0
            for half in range(2):
                dve.wait_ge(s["pre_full"], 3 + half)
                for n in range(2):
                    nc.vector.tensor_tensor(v[:, 2 * half + n, :], pre_ps[2 + half][0:NC, n * D:(n + 1) * D],
                                            chip.vec("L3_xattn_bv")[0:NC, :], ALU.add).then_inc(s["v_done"], 1)
            dve.sem_inc(s["shifted"], 1)
            dve.sem_inc(s["o_free"], 4)

            def stats(t, q):
                p = q % 2
                link.enter(0, t)
                link(nc.vector.bn_stats(stat[:, p, :], tile_of(chip, t)))
                chip.settle(dve)
                nc.vector.bn_aggr(mv[:, p, :], stat[:, p, :]).then_inc(s["stats_done"], 1)
                link.leave()

            def normalise(t, q):
                p = q % 2
                dve.wait_ge(s["rstd_done"], t + 1)
                nc.vector.tensor_scalar(xn[:, p, :], tile_of(chip, t), mv[:, p, 0:1], rs[:, p:p + 1],
                                        ALU.subtract, ALU.mult).then_inc(s["xn_done"], 1)

            def shift(t, q):
                p = q % 2
                link.enter(2, t)
                dve.wait_ge(s["s_full"], t + 1)
                link(nc.vector.tensor_reduce(mx[:, p:p + 1], s_ps[:, 0:NC], AX.X, ALU.max))
                if not (isinstance(t, int) and t < 2):
                    dve.wait_ge(s["pT_full"], t - 1)
                nc.vector.tensor_scalar(pr[:, p, :], s_ps[:, 0:NC], mx[:, p:p + 1], None, ALU.subtract).then_inc(s["shifted"], 1)
                link.leave()

            def result(t, q):
                p = q % 2
                link.enter(5, t)
                dve.wait_ge(s["exp_done"], t + 1)
                link(nc.vector.reciprocal(rc[:, q % 4:q % 4 + 1], sm[:, q % 4:q % 4 + 1]))
                dve.wait_ge(s["o_full"], t + 1)
                dve.wait_ge(s["x_done"], t + 1)
                nc.vector.tensor_scalar(res[:, p, :], o_ps[:, 0:D], rc[:, q % 4:q % 4 + 1], gate, ALU.mult, ALU.mult).then_inc(s["o_free"], 1)
                link.leave()

            none = lambda t, q: None
            pipelined(dve, [stats, normalise, shift, none, none, result], unroll=NU)

        @block.gpsimd
        def _(pool):
            link = Links(pool, s["pool_step"], [1, 0, 0, 0, 0, 0])
            pool.sem_inc(s["x_done"], 2)

            def rstd(t, q):
                p = q % 2
                link.enter(0, t)
                pool.wait_ge(s["stats_done"], t + 1)
                chip.settle(pool)
                link(nc.gpsimd.tensor_scalar(ve[:, p:p + 1], mv[:, p, 1:2], 1e-5, None, ALU.add))
                nc.gpsimd.tensor_tensor(rs[:, p:p + 1], ve[:, p:p + 1], chip.neghalf[:, 0:1], ALU.pow).then_inc(s["rstd_done"], 1)
                link.leave()

            def add(t, q):
                pool.wait_ge(s["o_free"], t + 5)
                nc.gpsimd.tensor_tensor(tile_of(chip, t), tile_of(chip, t), res[:, q % 2, :], ALU.add).then_inc(s["x_done"], 1)

            none = lambda t, q: None
            pipelined(pool, [rstd, none, none, none, none, add], unroll=NU)


def self_stage(chip, dram):
    nc, w = chip.nc, chip.w
    BIG = -1e30
    SK = 1.0 / 32.0
    HD = D // H
    KR = 6 * HD
    MR = KR + 2
    QUADS = H // 4
    VC = HD + 1
    STEPS = [(0, kt) for kt in range(TB // 2)] + [(1, kt) for kt in range(TB)]
    NS = len(STEPS)
    PEAKS = [(i, hs) for i in range(TB) for hs in (((0, 1), (2, 3)) if i < TB // 2 else ((0,), (1,), (2,), (3,)))]
    NP = len(PEAKS)
    SHARE = (5, 2, 1, 1, 4, 3, 3, 3, 2, 0, 0, 0)
    TURN_AT = 9
    with ExitStack() as ctx:
        def sb(name, shape, dt=F32):
            return ctx.enter_context(nc.sbuf_tensor(f"L2S_{name}", shape, dt))

        def ps(name, shape, dt=F32):
            return ctx.enter_context(nc.psum_tensor(f"L2S_{name}", shape, dt))

        s_ps = [ps(f"s_ps{i}", [P, S]) for i in range(2)]
        t_ps = [ps(f"t_ps{i}", [P, 512]) for i in range(2)]
        o_ps = ps("o_ps", [P, 512])
        r_ps = ps("r_ps", [P, 512])
        stat, mv, ve, rs = sb("stat", [P, TB, 6]), sb("mv", [P, TB, 2]), sb("ve", [P, TB]), sb("rs", [P, TB])
        xn = sb("xn", [P, TB, D])
        xT = sb("xT", [P, KD, S])
        part = sb("part", [P, 2, 3, S], BF16)
        q6 = sb("q6", [MR, 2, 4, S], BF16)
        k6 = sb("k6", [MR, 2, 4, S], BF16)
        v = sb("v", [P, TB, H * VC + 32 - VC])
        pT = sb("pT", [P, 2, 4, 512])
        rest = pT[:, 0, :, :].rearrange("p j t -> p (j t)").rearrange("p (r t) -> p r t", r=2)
        cmask, cmaskT, identb = sb("cmask", [P, P], BF16), sb("cmaskT", [P, P], BF16), sb("identb", [P, P], BF16)
        mx = sb("mx", [P, 2, 4, TB])
        mrow = sb("mrow", [4 * TB, 2, P], BF16)
        oT = sb("oT", [P, 512])
        rc = sb("rc", [P, 4, 4])
        att = sb("att", [P, TB, D])
        names = """const_done ones_done stats_done rstd_done xn_done pre_full act_pre rest_done split_done written0 written1 loaded_low0 loaded_low1
            loaded_high0 loaded_high1 s_full mx_done r_full r_free t_full exp_done pv_done o_copied att_free y_done
            rstd2_done stats2_done norm_done a_done a_out pool_step dve_step""".split()
        s = {n: ctx.enter_context(nc.semaphore(f"L2S_{n}")) for n in names}
        s["mrow_in"] = chip.queued["mrow_in"]
        block = ctx.enter_context(nc.Block())

        R_USES = 3 * QUADS
        R_AT, order = {}, []
        for q in range(QUADS):
            order += [("m", 0)] if q == 0 else [("o", q - 1, 1)]
            order += [("o", q, 0)] + ([("m", q + 1)] if q + 1 < QUADS else [])
        order += [("o", QUADS - 1, 1)]
        R_AT = {use: n + 1 for n, use in enumerate(order)}

        def nothing(*a):
            pass

        def self_walk(setup=nothing, peak=nothing, turn_max=nothing, unit=nothing, values=nothing, copy_out=nothing,
                      turn_out=nothing, finish=nothing):
            setup()
            for n in range(NP):
                peak(0, n)
            turn_max(0)
            for q in range(QUADS):
                pending = list(range(NP)) if q + 1 < QUADS else []
                for st in range(NS):
                    share = pending[:SHARE[st]]
                    pending = pending[SHARE[st]:]
                    for j in range(4):
                        unit(q, st, j)
                        for n in share[j:j + 1]:
                            peak(q + 1, n)
                    for n in share[4:]:
                        peak(q + 1, n)
                    before = (q, st - 1) if st else (q - 1, NS - 1)
                    if before[0] >= 0:
                        values(*before)
                        if before[1] in (TB // 2 - 1, NS - 1):
                            copy_out(before[0], STEPS[before[1]][0])
                    if st == TB // 2 + 1:
                        turn_out(q, 0)
                    if st == 1 and q:
                        turn_out(q - 1, 1)
                    if st == TURN_AT and q + 1 < QUADS:
                        turn_max(q + 1)
            values(QUADS - 1, NS - 1)
            copy_out(QUADS - 1, 1)
            turn_out(QUADS - 1, 1)
            finish()

        def low(st):
            c, kt = STEPS[st]
            return max(0, (kt - 4 * c) * P)

        @block.sync
        def _(sp):
            chip.load(sp, WEIGHTS["L3"], dram)

            def load(b, q, which, cols, sem):
                t = {"q": q6, "k": k6}[which]
                chip.settle(sp)
                src = dram["parts"][bass.ds(b * 2 + (0 if which == "q" else 1), 1)]
                for slot, p in enumerate({"q": (0, 0, 0, 1, 1, 2), "k": (0, 1, 2, 0, 1, 0)}[which]):
                    sp.dma_start(t[slot * HD:(slot + 1) * HD, q % 2, :, cols],
                                 src[:, q, p, :, :, cols].rearrange("o h d s -> (o d) h s")).then_inc(sem, 16)

            lowc, highc = slice(0, S // 2), slice(S // 2, S)
            sp.sem_inc(s["att_free"], 1)
            with sp.Fori(0, B) as b:
                def write(f):
                    which, m = f % 2, f // 2
                    sp.wait_ge(s["split_done"], 4 * b + f + 2)
                    chip.settle(sp)
                    for p in range(3):
                        for qq in range(2):
                            sp.dma_start(dram["parts"][bass.ds(b * 2 + which, 1), 2 * m + qq, p, :, :, :].rearrange("o h d s -> (o h d) s"),
                                         part[64 * qq:64 * qq + 64, f % 2, p, :]).then_inc(s[f"written{which}"], 16)

                write(0)
                write(1)
                for which in range(2):
                    sp.wait_ge(s[f"written{which}"], (2 * b + 1) * 96)
                    chip.settle(sp)
                for q in range(2):
                    for cols, n in ((lowc, "low"), (highc, "high")):
                        for which in "qk":
                            load(b, q, which, cols, s[f"loaded_{n}{q % 2}"])
                write(2)
                write(3)
                for which in range(2):
                    sp.wait_ge(s[f"written{which}"], (2 * b + 2) * 96)
                    chip.settle(sp)
                for q in range(2, QUADS):
                    done = b * QUADS * NS * 4 + (q - 2) * NS * 4
                    sp.wait_ge(s["t_full"], done + 4 * (TB // 2))
                    load(b, q, "q", lowc, s[f"loaded_low{q % 2}"])
                    sp.wait_ge(s["t_full"], done + 4 * TB)
                    load(b, q, "k", lowc, s[f"loaded_low{q % 2}"])
                    sp.wait_ge(s["t_full"], done + 4 * NS)
                    load(b, q, "q", highc, s[f"loaded_high{q % 2}"])
                    load(b, q, "k", highc, s[f"loaded_high{q % 2}"])
                sp.wait_ge(s["a_done"], b + 1)
                chip.settle(sp)
                sp.dma_start(dram["a"][:, bass.ts(b, TB), :], att[:]).then_inc(s["a_out"], 16)
                sp.wait_ge(s["a_out"], 16 * b + 16)
                sp.sem_inc(s["att_free"], 1)

        @block.tensor
        def _(pe):
            for name in WEIGHTS["L2S"]:
                pe.wait_ge(chip.w_in[name], 16)
            pe.wait_ge(s["const_done"], 1)
            pe.wait_ge(s["ones_done"], 1)
            pe.sem_inc(s["pv_done"], 1)
            pe.sem_inc(s["r_full"], 1)
            with pe.Fori(0, B) as b:
                def setup():
                    pe.wait_ge(s["y_done"], 2 * b + 1)
                    pe.wait_ge(s["xn_done"], TB * b + TB)
                    for dh in range(KD):
                        for i in range(TB):
                            mm = nc.tensor.transpose(s_ps[dh][:, i * P:(i + 1) * P], xn[:, i, dh * P:(dh + 1) * P], chip.ident[:])
                        mm.then_inc(s["pre_full"], 1)
                    pe.wait_ge(s["act_pre"], 10 * b + 2)
                    for half in range(2):
                        for i in range(4):
                            t = 4 * half + i
                            for k in range(KD):
                                mm = nc.tensor.matmul(s_ps[half][:, i * D:(i + 1) * D], xT[:, k, t * P:(t + 1) * P], w["L2S_Wv"][:, k, :],
                                                      start=(k == 0), stop=(k == KD - 1))
                        mm.then_inc(s["pre_full"], 1)
                    for f in range(4):
                        if f < 2:
                            pe.wait_ge(s["act_pre"], 10 * b + 3 + f)
                        else:
                            pe.wait_ge(s["rest_done"], 4 * b + f - 1)
                        m = f // 2
                        for c in range(2):
                            for k in range(KD):
                                mm = nc.tensor.matmul(s_ps[f % 2][:, c * 512:(c + 1) * 512], w[("L2S_Wq", "L2S_Wk")[f % 2]][:, k, m * P:(m + 1) * P],
                                                      xT[:, k, c * 512:(c + 1) * 512], start=(k == 0), stop=(k == KD - 1))
                        mm.then_inc(s["pre_full"], 1)
                    pe.wait_ge(s["rest_done"], 4 * b + 4)

                def peak(q, n):
                    i, hs = PEAKS[n]
                    number = NP * (QUADS * b + q) + n
                    if n == 0:
                        pe.wait_ge(s[f"loaded_low{q % 2}"], 192 * (2 * b + q // 2 + 1))
                    if n == TB:
                        pe.wait_ge(s[f"loaded_high{q % 2}"], 192 * (2 * b + q // 2 + 1))
                    pe.wait_ge(s["mx_done"], number + 1)
                    o = s_ps[n % 2]
                    for z, h in enumerate(hs):
                        lhs = q6[0:KR, q % 2, h, i * P:(i + 1) * P]
                        end = (i + 1) * P
                        for c in range(0, end, 512):
                            e = min(end, c + 512)
                            nc.tensor.matmul(o[:, z * 512 + c:z * 512 + e], lhs, k6[0:KR, q % 2, h, c:e], start=True, stop=(e < end))
                        mm = nc.tensor.matmul(o[:, z * 512 + end - P:z * 512 + end], identb[:], cmask[:], start=False, stop=True)
                    mm.then_inc(s["s_full"], 1)

                def turn_max(q):
                    k = R_USES * b + R_AT["m", q]
                    pe.wait_ge(s["r_free"], k)
                    pe.wait_ge(s["mx_done"], NP * (QUADS * b + q + 1) + 2)
                    nc.tensor.transpose(r_ps[0:4 * TB, 0:P], mx[:, q % 2, :, :].rearrange("p h i -> p (h i)"), chip.ident[:]).then_inc(s["r_full"], 1)

                def unit(q, st, j):
                    c, kt = STEPS[st]
                    number = ((QUADS * b + q) * NS + st) * 4 + j
                    if st == 0 and j == 0:
                        pe.wait_ge(s["mrow_in"], 32 * (QUADS * b + q + 1))
                    pe.wait_ge(s["exp_done"], number + 1)
                    o, lo = t_ps[j % 2], low(st)
                    diagonal = kt >= 4 * c
                    mm = nc.tensor.matmul(o[:, lo:512], k6[:, q % 2, j, kt * P:(kt + 1) * P], q6[:, q % 2, j, c * 512 + lo:(c + 1) * 512],
                                          start=True, stop=not diagonal)
                    if diagonal:
                        mm = nc.tensor.matmul(o[:, lo:lo + P], identb[:], cmaskT[:], start=False, stop=True)
                    mm.then_inc(s["t_full"], 1)

                def values(q, st):
                    c, kt = STEPS[st]
                    step = (QUADS * b + q) * NS + st
                    last = 3 if c == 0 else TB - 1
                    pe.wait_ge(s["exp_done"], 4 * step + 4 + 2)
                    if kt == 0:
                        pe.wait_ge(s["o_copied"], 2 * (QUADS * b + q) + c + 1)
                    lo = low(st)
                    for j in range(4):
                        h = 4 * q + j
                        mm = nc.tensor.matmul(o_ps[32 * j:32 * j + 32, lo:512], v[:, kt, h * VC:h * VC + 32], pT[:, st % 2, j, lo:512],
                                              start=(kt == 0), stop=(kt == last))
                    mm.then_inc(s["pv_done"], 1)

                def turn_out(q, c):
                    k = R_USES * b + R_AT["o", q, c]
                    pe.wait_ge(s["r_free"], k)
                    pe.wait_ge(s["o_copied"], 2 * (QUADS * b + q) + c + 2)
                    for i in range(4):
                        mm = nc.tensor.transpose(r_ps[:, i * P:(i + 1) * P], oT[:, i * P:(i + 1) * P], chip.ident[:])
                    mm.then_inc(s["r_full"], 1)

                def finish():
                    pe.wait_ge(s["r_free"], R_USES * b + R_USES + 1)
                    for dh in range(KD):
                        for i in range(TB):
                            mm = nc.tensor.transpose(s_ps[dh][:, i * P:(i + 1) * P], att[:, i, dh * P:(dh + 1) * P], chip.ident[:])
                        mm.then_inc(s["pre_full"], 1)
                    pe.wait_ge(s["act_pre"], 10 * b + 10)
                    for half in range(2):
                        for i in range(4):
                            t = 4 * half + i
                            for k in range(KD):
                                mm = nc.tensor.matmul(s_ps[half][:, i * D:(i + 1) * D], xT[:, k, t * P:(t + 1) * P], w["L2S_Wo"][:, k, :],
                                                      start=(k == 0), stop=(k == KD - 1))
                        mm.then_inc(s["pre_full"], 1)

                self_walk(setup, peak, turn_max, unit, values, nothing, turn_out, finish)

        @block.scalar
        def _(act):
            act.sem_inc(s["exp_done"], 2)
            act.sem_inc(s["o_copied"], 1)
            with act.Fori(0, B) as b:
                def copy(dst, src):
                    nc.scalar.activation(dst, src, ACT.Copy).then_inc(s["act_pre"], 1)

                def setup():
                    for f in range(2):
                        act.wait_ge(s["pre_full"], 12 * b + f + 1)
                        copy(xT[:, f, :], s_ps[f][:])
                    act.wait_ge(s["ones_done"], 1)
                    for f in range(2):
                        act.wait_ge(s["pre_full"], 12 * b + f + 3)
                        copy(v[:, 4 * f:4 * f + 4, 0:H * VC].rearrange("p t (h c) -> p t h c", c=VC)[:, :, :, 0:HD],
                             s_ps[f][:].rearrange("p (t h d) -> p t h d", t=4, d=HD))
                    for f in range(4):
                        act.wait_ge(s["pre_full"], 12 * b + f + 5)
                        if f >= 2:
                            act.wait_ge(s[f"written{f % 2}"], (2 * b + 1) * 96)
                        copy(part[:, f % 2, 0, :], s_ps[f % 2][:])

                def unit(q, st, j):
                    step = (QUADS * b + q) * NS + st
                    act.wait_ge(s["t_full"], 4 * step + j + 1)
                    if q == 0 and st == 0 and j == 0:
                        act.wait_ge(s["split_done"], 4 * b + 5)
                    if j == 0:
                        if st < 2 and q == 0:
                            act.wait_ge(s["pv_done"], QUADS * NS * b + 1)
                        else:
                            act.wait_ge(s["pv_done"], step)
                    lo = low(st)
                    nc.scalar.activation(pT[:, st % 2, j, lo:512], t_ps[j % 2][:, lo:512], ACT.Exp, scale=SK).then_inc(s["exp_done"], 1)

                def copy_out(q, c):
                    act.wait_ge(s["pv_done"], (QUADS * b + q) * NS + (TB // 2 if c == 0 else NS) + 1)
                    k = R_AT["o", q, 0] if c else (R_AT["o", q - 1, 1] if q else 0)
                    act.wait_ge(s["r_full"], R_USES * b + k + 1)
                    nc.scalar.activation(oT[:], o_ps[:], ACT.Copy).then_inc(s["o_copied"], 1)

                def finish():
                    for f in range(2):
                        act.wait_ge(s["pre_full"], 12 * b + f + 9)
                        copy(xT[:, f, :], s_ps[f][:])

                self_walk(setup=setup, unit=unit, copy_out=copy_out, finish=finish)

        @block.vector
        def _(dve):
            step = Count(s["dve_step"])

            def link(ins):
                ins.then_inc(s["dve_step"], 1)
                dve.wait_ge(s["dve_step"], step.up())

            nc.vector.memset(v[:], 1.0)
            nc.vector.memset(k6[KR:MR], 1.0).then_inc(s["ones_done"], 1)
            dve.sem_inc(s["mx_done"], 2)
            dve.sem_inc(s["r_free"], 1)
            dve.sem_inc(s["y_done"], 1)
            PER = 1 + QUADS + 2 * QUADS + 5
            with dve.Fori(0, B) as b:
                step.enter(PER * b)

                def setup():
                    for i in range(TB):
                        ins = nc.vector.bn_stats(stat[:, i, :], chip.x[:, bass.ds((TB * b + i) * D, D)])
                    link(ins)
                    chip.settle(dve)
                    for i in range(TB):
                        ins = nc.vector.bn_aggr(mv[:, i, :], stat[:, i, :])
                    ins.then_inc(s["stats_done"], 1)
                    dve.wait_ge(s["rstd_done"], b + 1)
                    for i in range(TB):
                        nc.vector.tensor_scalar(xn[:, i, :], chip.x[:, bass.ds((TB * b + i) * D, D)], mv[:, i, 0:1], rs[:, i:i + 1],
                                                ALU.subtract, ALU.mult).then_inc(s["xn_done"], 1)
                    for f in range(4):
                        dve.wait_ge(s["act_pre"], 10 * b + 5 + f)
                        dve.wait_ge(s["split_done"], 4 * b + max(f - 1, 0) + 1)
                        nc.vector.tensor_tensor(rest[:, f % 2, :], s_ps[f % 2][:], part[:, f % 2, 0, :], ALU.subtract).then_inc(s["rest_done"], 1)

                def peak(q, n):
                    i, hs = PEAKS[n]
                    dve.wait_ge(s["s_full"], NP * (QUADS * b + q) + n + 1)
                    if len(hs) == 2:
                        src = s_ps[n % 2][:].rearrange("p (h k) -> p h k", h=2)[:, :, 0:(i + 1) * P]
                        dst = mx[:, q % 2, hs[0]:hs[0] + 2, i]
                    else:
                        src, dst = s_ps[n % 2][:, 0:(i + 1) * P], mx[:, q % 2, hs[0], i:i + 1]
                    nc.vector.tensor_reduce(dst, src, AX.X, ALU.max).then_inc(s["mx_done"], 1)

                def turn_max(q):
                    dve.wait_ge(s["r_full"], R_USES * b + R_AT["m", q] + 1)
                    if q:
                        dve.wait_ge(s["mrow_in"], 32 * (QUADS * b + q))
                    link(nc.vector.tensor_scalar(mrow[:, 0, :], r_ps[0:4 * TB, 0:P], -1.0, None, ALU.mult))
                    nc.vector.scalar_tensor_tensor(out=mrow[:, 1, :], in0=r_ps[0:4 * TB, 0:P], scalar=-1.0, in1=mrow[:, 0, :],
                                                   op0=ALU.mult, op1=ALU.subtract).then_inc(s["r_free"], 1)

                def turn_out(q, c):
                    dve.wait_ge(s["r_full"], R_USES * b + R_AT["o", q, c] + 1)
                    dve.wait_ge(s["att_free"], b + 1)
                    o = r_ps[:].rearrange("p (i h d) -> p i h d", i=4, h=4)
                    link(nc.vector.reciprocal(rc[:], o[:, :, :, HD]))
                    dst = att[:, 4 * c:4 * c + 4, 4 * q * HD:4 * (q + 1) * HD].rearrange("p i (h d) -> p i h d", h=4)
                    nc.vector.tensor_tensor(dst, o[:, :, :, 0:HD], wide(rc[:].unsqueeze(3), [P, 4, 4, HD]), ALU.mult).then_inc(s["r_free"], 1)

                def finish():
                    for half in range(2):
                        y = att[:, 4 * half:4 * half + 4, :]
                        dve.wait_ge(s["pre_full"], 12 * b + 11 + half)
                        ins = nc.vector.tensor_tensor(y, s_ps[half][:].rearrange("p (i d) -> p i d", d=D),
                                                      wide(chip.vec("L2_xattn_bo1").unsqueeze(1), [P, 4, D]), ALU.add)
                        ins.then_inc(s["y_done"], 1)
                        dve.wait_ge(s["y_done"], 2 * b + half + 2)
                        link(nc.vector.scalar_tensor_tensor(out=y, in0=y, scalar=0.0, in1=xn[:, 4 * half:4 * half + 4, :],
                                                            op0=ALU.max, op1=ALU.add))
                    for i in range(TB):
                        ins = nc.vector.bn_stats(stat[:, i, :], att[:, i, :])
                    link(ins)
                    chip.settle(dve)
                    for i in range(TB):
                        ins = nc.vector.bn_aggr(mv[:, i, :], stat[:, i, :])
                    ins.then_inc(s["stats2_done"], 1)
                    dve.wait_ge(s["rstd2_done"], b + 1)
                    for i in range(TB):
                        ins = nc.vector.tensor_scalar(att[:, i, :], att[:, i, :], mv[:, i, 0:1], rs[:, i:i + 1], ALU.subtract, ALU.mult)
                    link(ins)
                    link(nc.vector.tensor_tensor(att[:], att[:], wide(chip.vec("L2_xattn_g1").unsqueeze(1), [P, TB, D]), ALU.mult))
                    nc.vector.tensor_tensor(att[:], att[:], wide(chip.vec("L2_xattn_b1").unsqueeze(1), [P, TB, D]), ALU.add).then_inc(s["a_done"], 1)

                self_walk(setup, peak, turn_max, nothing, nothing, nothing, turn_out, finish)
                assert step.k == PER, step.k

        @block.gpsimd
        def _(pool):
            nc.gpsimd.memset(cmask[:], 0.0)
            nc.gpsimd.memset(cmaskT[:], 0.0)
            nc.gpsimd.tensor_copy(identb[:], chip.ident[:]).then_inc(s["pool_step"], 1)
            pool.wait_ge(s["pool_step"], 1)
            nc.gpsimd.affine_select(out=cmask[:], in_=cmask[:], compare_op=ALU.is_ge, fill=BIG, base=0,
                                    pattern=[[-1, P]], channel_multiplier=1)
            nc.gpsimd.affine_select(out=cmaskT[:], in_=cmaskT[:], compare_op=ALU.is_ge, fill=BIG, base=0,
                                    pattern=[[1, P]], channel_multiplier=-1).then_inc(s["const_done"], 1)
            pool.sem_inc(s["split_done"], 1)
            first = 1
            PER = 6
            with pool.Fori(0, B) as b:
                def rstd(sem_in, sem_out, k, eps):
                    pool.wait_ge(s[sem_in], b + 1)
                    chip.settle(pool)
                    nc.gpsimd.tensor_scalar(ve[:], mv[:, :, 1], eps, None, ALU.add).then_inc(s["pool_step"], 1)
                    pool.wait_ge(s["pool_step"], first + PER * b + k)
                    nc.gpsimd.tensor_tensor(rs[:], ve[:], chip.neghalf[:, 0:TB], ALU.pow).then_inc(s[sem_out], 1)

                def setup():
                    rstd("stats_done", "rstd_done", 1, 1e-5)
                    for f in range(4):
                        pool.wait_ge(s["rest_done"], 4 * b + f + 1)
                        if f >= 2:
                            pool.wait_ge(s[f"written{f % 2}"], (2 * b + 1) * 96)
                        chip.settle(pool)
                        nc.gpsimd.tensor_scalar(part[:, f % 2, 1, :], rest[:, f % 2, :], 1.0, None, ALU.mult).then_inc(s["pool_step"], 1)
                        pool.wait_ge(s["pool_step"], first + PER * b + 2 + f)
                        nc.gpsimd.tensor_tensor(part[:, f % 2, 2, :], rest[:, f % 2, :], part[:, f % 2, 1, :], ALU.subtract).then_inc(s["split_done"], 1)

                def turn_max(q):
                    pool.wait_ge(s["r_free"], R_USES * b + R_AT["m", q] + 1)
                    chip.settle(pool)
                    for p in range(2):
                        nc.gpsimd.dma_start(q6[KR + p:KR + p + 1, q % 2, :, :].rearrange("o h (i t) -> o (h i) t", t=P),
                                            mrow[:, p, :]).then_inc(s["mrow_in"], 16)

                def finish():
                    rstd("stats2_done", "rstd2_done", 6, 1e-6)

                self_walk(setup=setup, turn_max=turn_max, finish=finish)


def mixture_stage(chip, dram):
    nc = chip.nc
    E, F = 8, 512
    FK = F // P
    BLOCKS = T * P * 2 // P + E - 1
    REGION = T * P + P
    NJ = BLOCKS + 1
    RING = 8
    gate = chip.gates[:, B + 3:B + 4]
    with ExitStack() as outer:
        def keep(name, shape, dt=F32):
            return outer.enter_context(nc.sbuf_tensor(f"L3F_{name}", shape, dt))

        w0 = chip.arena[:, 0:KD * E * F].rearrange("p (k n) -> p k n", k=KD)
        w1, wo = keep("w1", [P, KD, E * F]), keep("wo", [P, FK, E * D])
        where, share = keep("where", [P, T, 2], U32), keep("share", [P, T, 2])
        table = keep("table", [1, 2 * NJ + E], I32)
        weights_in = outer.enter_context(nc.semaphore("L3F_weights_in"))
        route_tokens(chip, dram, dict(E=E, F=F, NJ=NJ, REGION=REGION, BLOCKS=BLOCKS, RING=RING, w0=w0, w1=w1, wo=wo, where=where,
                                      share=share, table=table, weights_in=weights_in))
        clear_semaphores(nc)
        expert_blocks(chip, dram, dict(E=E, F=F, FK=FK, NJ=NJ, REGION=REGION, BLOCKS=BLOCKS, w0=w0, w1=w1, wo=wo, table=table,
                                       weights_in=weights_in))
        clear_semaphores(nc)
        combine_results(chip, dram, where, share, gate)


def route_tokens(chip, dram, a):
    nc = chip.nc
    E, F, NJ, REGION, RING = a["E"], a["F"], a["NJ"], a["REGION"], a["RING"]
    where, share, table, weights_in = a["where"], a["share"], a["table"], a["weights_in"]
    with ExitStack() as ctx:
        def sb(name, shape, dt=F32):
            return ctx.enter_context(nc.sbuf_tensor(f"L3R_{name}", shape, dt))

        def ps(name, shape):
            return ctx.enter_context(nc.psum_tensor(f"L3R_{name}", shape, F32))

        xT_ps = [ps(f"xT_ps{i}", [P, 512]) for i in range(2)]
        l_ps = [ps(f"l_ps{i}", [P, 512]) for i in range(2)]
        c_ps = [ps(f"c_ps{i}", [P, 512]) for i in range(2)]
        wg, before = sb("wg", [P, KD, E]), sb("before", [P, P])
        regions, steps, jota, seen = sb("regions", [P, E]), sb("steps", [P, T]), sb("jota", [1, NJ]), sb("seen", [P, 2, E])
        stat, mv, ve, rs = sb("stat", [P, 2, 6]), sb("mv", [P, 2, 2]), sb("ve", [P, 2]), sb("rs", [P, 2])
        xn, xT = sb("xn", [P, RING, D]), sb("xT", [P, 2, KD, P])
        lg, top, idx, idxf = sb("lg", [P, 2, E]), sb("top", [P, 2, 8]), sb("idx", [P, 2, 8], U32), sb("idxf", [P, 2, 2])
        hot, both, place = sb("hot", [P, 2, 2, E]), sb("both", [P, 2, E]), sb("place", [P, 2, E])
        picked, row, dest = sb("picked", [P, 2, 2, E]), sb("row", [P, 2, 2]), sb("dest", [P, RING, 2], U32)
        gap, zeros = sb("gap", [P, T]), sb("zeros", [P, D])
        count, blocks, upto, tri = sb("count", [P, E]), sb("blocks", [P, E]), sb("upto", [P, E]), sb("tri", [P, E, E])
        rows, experts, closer, hots = sb("rows", [P, 2 * T]), sb("experts", [P, 2 * T]), sb("closer", [P, E]), sb("hots", [P, 2 * T, E])
        past, used, ej, pj = sb("past", [1, NJ, E]), sb("used", [1, NJ, E]), sb("ej", [1, NJ]), sb("pj", [1, NJ])
        over, tabf = sb("over", [P, E, T]), sb("tabf", [1, 2 * NJ + E])
        names = """gates_in const_done zeros_done hot_done ranked stats_done rstd_done xn_done xT_full xT_free l_full picked c_full counted
            gap_done ratio_done rest_filled filled table_done dve_step pool_step """.split()
        s = {n: ctx.enter_context(nc.semaphore(f"L3R_{n}")) for n in names}
        s.update({f"scattered{q}": chip.queued[f"scattered{q}"] for q in range(RING)})
        block = ctx.enter_context(nc.Block())

        @block.sync
        def _(sp):
            sp.dma_start(wg[:], dram["L3_wg"]).then_inc(s["gates_in"], 16)
            for e in range(E):
                u, c = slice(e * F, (e + 1) * F), slice(e * D, (e + 1) * D)
                sp.dma_start(a["w0"][:, :, u], dram["L3_w0"][:, :, u]).then_inc(weights_in, 16)
                sp.dma_start(a["w1"][:, :, u], dram["L3_w1"][:, :, u]).then_inc(weights_in, 16)
                sp.dma_start(a["wo"][:, :, c], dram["L3_wo"][:, :, c]).then_inc(weights_in, 16)
            sp.wait_ge(s["zeros_done"], 1)
            for i in range(E):
                sp.dma_start(dram["rows"][E * REGION + i * P:E * REGION + (i + 1) * P, :], zeros[:]).then_inc(s["filled"], 16)
            sp.wait_ge(s["table_done"], 1)
            for e in range(E):
                end = sp.value_load(table[0:1, 2 * NJ + e:2 * NJ + e + 1], min_val=e * REGION, max_val=e * REGION + T * P)
                sp.dma_start(dram["rows"][bass.ds(end, P), :], zeros[:]).then_inc(s["rest_filled"], 16)
            sp.wait_ge(s["filled"], 16 * E)
            sp.wait_ge(s["rest_filled"], 16 * E)
            sp.wait_ge(weights_in, 48 * E)

        none = lambda t, q: None

        @block.tensor
        def _(pe):
            pe.wait_ge(s["gates_in"], 16)
            pe.wait_ge(s["const_done"], 1)

            def turn_x(t, q):
                pe.wait_ge(s["xn_done"], t + 1)
                pe.wait_ge(s["xT_free"], t + 1)
                for k in range(KD):
                    mm = nc.tensor.transpose(xT_ps[q % 2][:, k * P:(k + 1) * P], xn[:, q, k * P:(k + 1) * P], chip.ident[:])
                mm.then_inc(s["xT_full"], 1)

            def logits(t, q):
                pe.wait_ge(s["xT_free"], t + 3)
                pe.wait_ge(s["picked"], t + 1)
                for k in range(KD):
                    mm = nc.tensor.matmul(l_ps[q % 2][:, 0:E], xT[:, q % 2, k, :], wg[:, k, :], start=(k == 0), stop=(k == KD - 1))
                mm.then_inc(s["l_full"], 1)

            def ranks(t, q):
                pe.wait_ge(s["picked"], t + 3)
                pe.wait_ge(s["counted"], t + 1)
                nc.tensor.matmul(c_ps[q % 2][:, 0:E], before[:], both[:, q % 2, :], start=True, stop=False)
                nc.tensor.matmul(c_ps[q % 2][:, 0:E], chip.ones[:], seen[:, q % 2, :], start=False, stop=True).then_inc(s["c_full"], 1)

            pipelined(pe, [none, none, turn_x, logits, ranks, none], unroll=RING, ring=RING)
            pe.wait_ge(s["counted"], T + 1)
            nc.tensor.matmul(c_ps[0][:, 0:E], chip.ones[:], seen[:, 0, :], start=True, stop=True).then_inc(s["c_full"], 1)

        @block.scalar
        def _(act):
            act.sem_inc(s["xT_free"], 2)

            def copy_x(t, q):
                act.wait_ge(s["xT_full"], t + 1)
                if not (isinstance(t, int) and t < 2):
                    act.wait_ge(s["l_full"], t - 1)
                nc.scalar.activation(xT[:, q % 2, :, :].rearrange("p k t -> p (k t)"), xT_ps[q % 2][:, 0:D], ACT.Copy).then_inc(s["xT_free"], 1)

            pipelined(act, [none, none, copy_x, none, none, none], unroll=RING, ring=RING)
            act.wait_ge(s["gap_done"], 1)
            nc.scalar.activation(gap[:], gap[:], ACT.Exp).then_inc(s["ratio_done"], 1)

        @block.vector
        def _(dve):
            link = Links(dve, s["dve_step"], [1, 0, 0, 4, 3, 0])
            link.k = 0
            link(nc.vector.memset(seen[:], 0.0))
            link.start = link.k
            dve.sem_inc(s["picked"], 2)
            dve.sem_inc(s["counted"], 1)
            dve.wait_ge(s["const_done"], 1)

            def stats(t, q):
                p = q % 2
                link.enter(0, t)
                link(nc.vector.bn_stats(stat[:, p, :], tile_of(chip, t)))
                chip.settle(dve)
                nc.vector.bn_aggr(mv[:, p, :], stat[:, p, :]).then_inc(s["stats_done"], 1)
                link.leave()

            def normalise(t, q):
                p = q % 2
                dve.wait_ge(s["rstd_done"], t + 1)
                if not (isinstance(t, int) and t < RING):
                    dve.wait_ge(s[f"scattered{q}"], (t - q) * (32 // RING))
                nc.vector.tensor_scalar(xn[:, q, :], tile_of(chip, t), mv[:, p, 0:1], rs[:, p:p + 1],
                                        ALU.subtract, ALU.mult).then_inc(s["xn_done"], 1)

            def pick(t, q):
                p = q % 2
                link.enter(3, t)
                dve.wait_ge(s["l_full"], t + 1)
                link(nc.vector.tensor_copy(lg[:, p, :], l_ps[p][:, 0:E]))
                chip.settle(dve)
                link(nc.vector.max(top[:, p, :], lg[:, p, :]))
                chip.settle(dve)
                link(nc.vector.max_index(idx[:, p, :], top[:, p, :], lg[:, p, :]))
                nc.vector.tensor_tensor(gap[:, bass.ds(t, 1)], top[:, p, 1:2], top[:, p, 0:1], ALU.subtract)
                link(nc.vector.tensor_copy(idxf[:, p, :], idx[:, p, 0:2]))
                nc.vector.tensor_copy(experts[:, bass.ds(t * 2, 2)], idxf[:, p, :])
                nc.vector.tensor_tensor(hot[:, p, :, :], wide(chip.iota[:, 0:E].unsqueeze(1), [P, 2, E]),
                                        wide(idxf[:, p, :].unsqueeze(2), [P, 2, E]), ALU.is_equal).then_inc(s["hot_done"], 1)
                dve.wait_ge(s["hot_done"], t + 1)
                nc.vector.tensor_tensor(both[:, p, :], hot[:, p, 0, :], hot[:, p, 1, :], ALU.add).then_inc(s["picked"], 1)
                link.leave()

            def rank(t, q):
                p = q % 2
                link.enter(4, t)
                dve.wait_ge(s["c_full"], t + 1)
                dve.wait_ge(s["picked"], t + 3)
                nc.vector.tensor_tensor(seen[:, 1 - p, :], seen[:, p, :], both[:, p, :], ALU.add)
                link(nc.vector.tensor_tensor(place[:, p, :], c_ps[p][:, 0:E], regions[:], ALU.add))
                dve.sem_inc(s["counted"], 1)
                link(nc.vector.tensor_tensor(picked[:, p, :, :], hot[:, p, :, :], wide(place[:, p, :].unsqueeze(1), [P, 2, E]), ALU.mult))
                link(nc.vector.tensor_reduce(row[:, p, :], picked[:, p, :, :], AX.X, ALU.add))
                nc.vector.tensor_copy(rows[:, bass.ds(t * 2, 2)], row[:, p, :])
                nc.vector.tensor_copy(dest[:, q, :], row[:, p, :]).then_inc(s["ranked"], 1)
                link.leave()

            pipelined(dve, [stats, normalise, none, pick, rank, none], unroll=RING, ring=RING)
            total = T * 8 + link.start
            step = Count(s["dve_step"], total)

            def link(ins):
                ins.then_inc(s["dve_step"], 1)
                dve.wait_ge(s["dve_step"], step.up())

            dve.sem_inc(s["gap_done"], 1)
            dve.wait_ge(s["c_full"], T + 1)
            link(nc.vector.tensor_copy(count[:], c_ps[0][:, 0:E]))
            link(nc.vector.tensor_tensor(over[:], wide(count[:].unsqueeze(2), [P, E, T]), wide(steps[:].unsqueeze(1), [P, E, T]), ALU.is_gt))
            link(nc.vector.tensor_reduce(blocks[:], over[:], AX.X, ALU.add))
            link(nc.vector.tensor_tensor(tri[:], wide(chip.iota[:, 0:E].unsqueeze(2), [P, E, E]), wide(chip.iota[:, 0:E].unsqueeze(1), [P, E, E]), ALU.is_ge))
            link(nc.vector.tensor_tensor(tri[:], tri[:], wide(blocks[:].unsqueeze(1), [P, E, E]), ALU.mult))
            link(nc.vector.tensor_reduce(upto[:], tri[:], AX.X, ALU.add))
            link(nc.vector.tensor_tensor(past[:], wide(jota[:].unsqueeze(2), [1, NJ, E]), wide(upto[0:1, :].unsqueeze(1), [1, NJ, E]), ALU.is_ge))
            link(nc.vector.tensor_reduce(ej[:], past[:], AX.X, ALU.add))
            link(nc.vector.tensor_tensor(used[:], past[:], wide(blocks[0:1, :].unsqueeze(1), [1, NJ, E]), ALU.mult))
            link(nc.vector.tensor_reduce(pj[:], used[:], AX.X, ALU.add))
            link(nc.vector.tensor_tensor(pj[:], jota[:], pj[:], ALU.subtract))
            link(nc.vector.tensor_scalar(pj[:], pj[:], float(P), None, ALU.mult))
            link(nc.vector.scalar_tensor_tensor(out=tabf[:, NJ:2 * NJ], in0=ej[:], scalar=float(REGION), in1=pj[:], op0=ALU.mult, op1=ALU.add))
            link(nc.vector.tensor_scalar(tabf[:, 0:NJ], ej[:], float(E - 1), None, ALU.min))
            link(nc.vector.tensor_tensor(tabf[:, 2 * NJ:], count[0:1, :], regions[0:1, :], ALU.add))
            nc.vector.tensor_copy(table[:], tabf[:]).then_inc(s["table_done"], 1)
            link(nc.vector.tensor_tensor(closer[:], upto[:], blocks[:], ALU.subtract))
            link(nc.vector.scalar_tensor_tensor(out=closer[:], in0=closer[:], scalar=float(P), in1=regions[:], op0=ALU.mult, op1=ALU.subtract))
            link(nc.vector.tensor_tensor(hots[:], wide(chip.iota[:, 0:E].unsqueeze(1), [P, 2 * T, E]), wide(experts[:].unsqueeze(2), [P, 2 * T, E]), ALU.is_equal))
            link(nc.vector.tensor_tensor(hots[:], hots[:], wide(closer[:].unsqueeze(1), [P, 2 * T, E]), ALU.mult))
            link(nc.vector.tensor_reduce(experts[:], hots[:], AX.X, ALU.add))
            link(nc.vector.tensor_tensor(rows[:], rows[:], experts[:], ALU.add))
            nc.vector.tensor_copy(where[:].rearrange("p t k -> p (t k)"), rows[:])
            dve.wait_ge(s["ratio_done"], 1)
            link(nc.vector.tensor_scalar(share[:, :, 0], gap[:], 1.0, None, ALU.add))
            link(nc.vector.reciprocal(share[:, :, 0], share[:, :, 0]))
            link(nc.vector.tensor_tensor(share[:, :, 1], share[:, :, 0], gap[:], ALU.mult))
            nc.vector.tensor_scalar(share[:].rearrange("p t k -> p (t k)"), share[:].rearrange("p t k -> p (t k)"),
                                    1.0, chip.gates[:, B + 3:B + 4], ALU.mult, ALU.mult)

        @block.gpsimd
        def _(pool):
            nc.gpsimd.memset(before[:], 0.0).then_inc(s["pool_step"], 1)
            nc.gpsimd.iota(regions[:], [[REGION, E]], base=0, channel_multiplier=0, allow_small_or_imprecise_dtypes=True)
            nc.gpsimd.iota(steps[:], [[P, T]], base=0, channel_multiplier=0, allow_small_or_imprecise_dtypes=True).then_inc(s["pool_step"], 1)
            pool.wait_ge(s["pool_step"], 2)
            nc.gpsimd.iota(jota[:], [[1, NJ]], base=0, channel_multiplier=0, allow_small_or_imprecise_dtypes=True).then_inc(s["pool_step"], 1)
            nc.gpsimd.memset(zeros[:], 0.0).then_inc(s["zeros_done"], 1)
            nc.gpsimd.affine_select(out=before[:], in_=before[:], compare_op=ALU.is_ge, fill=1.0, base=0,
                                    pattern=[[-1, P]], channel_multiplier=1).then_inc(s["const_done"], 1)
            link = Links(pool, s["pool_step"], [1, 0, 0, 0, 0, 0], start=3)

            def rstd(t, q):
                p = q % 2
                link.enter(0, t)
                pool.wait_ge(s["stats_done"], t + 1)
                chip.settle(pool)
                link(nc.gpsimd.tensor_scalar(ve[:, p:p + 1], mv[:, p, 1:2], 1e-5, None, ALU.add))
                nc.gpsimd.tensor_tensor(rs[:, p:p + 1], ve[:, p:p + 1], chip.neghalf[:, 0:1], ALU.pow).then_inc(s["rstd_done"], 1)
                link.leave()

            def scatter(t, q):
                pool.wait_ge(s["ranked"], t + 1)
                chip.settle(pool)
                for k in range(2):
                    nc.gpsimd.indirect_dma_start(dram["rows"], bass.IndirectOffsetOnAxis(dest[:, q, k:k + 1], 0), xn[:, q, :], None
                                                 ).then_inc(s[f"scattered{q}"], 16)

            pipelined(pool, [rstd, none, none, none, none, scatter], unroll=RING, ring=RING)
            for q in range(RING):
                pool.wait_ge(s[f"scattered{q}"], 32 * T // RING)


def expert_blocks(chip, dram, a):
    nc = chip.nc
    E, F, FK, NJ, REGION, BLOCKS = a["E"], a["F"], a["FK"], a["NJ"], a["REGION"], a["BLOCKS"]
    w0, w1, wo, table = a["w0"], a["w1"], a["wo"], a["table"]
    with ExitStack() as ctx:
        def sb(name, shape, dt=F32):
            return ctx.enter_context(nc.sbuf_tensor(f"L3B_{name}", shape, dt))

        def ps(name, shape):
            return ctx.enter_context(nc.psum_tensor(f"L3B_{name}", shape, F32))

        g_ps, u_ps = [ps(f"g_ps{i}", [P, F]) for i in range(2)], [ps(f"u_ps{i}", [P, F]) for i in range(2)]
        xT_ps, hT_ps = ps("xT_ps", [P, 512]), ps("hT_ps", [P, 512])
        o_ps = [ps(f"o_ps{i}", [P, 512]) for i in range(2)]
        xb, xT, y = sb("xb", [P, 2, D]), sb("xT", [P, 2, KD, P]), sb("y", [P, 2, D])
        si, h, hT = sb("si", [P, 2, F]), sb("h", [P, 2, F]), sb("hT", [P, 2, FK, P])
        names = """loaded0 loaded1 xT_full xT_free g_full u_full si_done h_done hT_full hT_free o_full y_done stored0 stored1""".split()
        s = {n: ctx.enter_context(nc.semaphore(f"L3B_{n}")) for n in names}
        block = ctx.enter_context(nc.Block())
        none = lambda j, q: None

        def run(eng, phases):
            pipelined(eng, phases, n=BLOCKS, unroll=2)

        @block.sync
        def _(sp):
            def load(j, q):
                if not (isinstance(j, int) and j < 2):
                    sp.wait_ge(s["xT_full"], j - 1)
                    chip.settle(sp)
                row = sp.value_load(table[0:1, bass.ds(j + NJ, 1)], min_val=0, max_val=E * REGION + (E - 1) * P)
                sp.dma_start(xb[:, q, :], dram["rows"][bass.ds(row, P), :]).then_inc(s[f"loaded{q}"], 16)

            def store(j, q):
                sp.wait_ge(s["y_done"], j + 3)
                chip.settle(sp)
                sp.dma_start(dram["results"][bass.ds(j * P, P), :], y[:, q, :]).then_inc(s[f"stored{q}"], 16)

            run(sp, [load, none, none, none, none, store])
            sp.wait_ge(s["stored0"], 16 * -(-BLOCKS // 2))
            sp.wait_ge(s["stored1"], 16 * (BLOCKS // 2))

        @block.tensor
        def _(pe):
            def turn_x(j, q):
                pe.wait_ge(s[f"loaded{q}"], (j - q) * 8 + 16)
                pe.wait_ge(s["xT_free"], j + 1)
                for k in range(KD):
                    mm = nc.tensor.transpose(xT_ps[:, k * P:(k + 1) * P], xb[:, q, k * P:(k + 1) * P], chip.ident[:])
                mm.then_inc(s["xT_full"], 1)

            def up(j, q):
                pe.wait_ge(s["xT_free"], j + 2)
                pe.wait_ge(s["h_done"], j + 1)
                chip.settle(pe)
                e = pe.value_load(table[0:1, bass.ds(j, 1)], min_val=0, max_val=E - 1)
                for o, wt, done in ((g_ps, w0, "g_full"), (u_ps, w1, "u_full")):
                    for k in range(KD):
                        mm = nc.tensor.matmul(o[q][:], xT[:, q, k, :], wt[:, k, bass.ds(e * F, F)], start=(k == 0), stop=(k == KD - 1))
                    mm.then_inc(s[done], 1)

            def turn_h(j, q):
                pe.wait_ge(s["h_done"], j + 3)
                pe.wait_ge(s["hT_free"], j + 1)
                for k in range(FK):
                    mm = nc.tensor.transpose(hT_ps[:, k * P:(k + 1) * P], h[:, q, k * P:(k + 1) * P], chip.ident[:])
                mm.then_inc(s["hT_full"], 1)

            def down(j, q):
                pe.wait_ge(s["hT_free"], j + 2)
                pe.wait_ge(s["y_done"], j + 1)
                chip.settle(pe)
                e = pe.value_load(table[0:1, bass.ds(j, 1)], min_val=0, max_val=E - 1)
                for k in range(FK):
                    mm = nc.tensor.matmul(o_ps[q][:, 0:D], hT[:, q, k, :], wo[:, k, bass.ds(e * D, D)], start=(k == 0), stop=(k == FK - 1))
                mm.then_inc(s["o_full"], 1)

            run(pe, [none, turn_x, up, turn_h, down, none])

        @block.scalar
        def _(act):
            act.sem_inc(s["xT_free"], 1)
            act.sem_inc(s["hT_free"], 1)

            def copy_x(j, q):
                act.wait_ge(s["xT_full"], j + 1)
                if not (isinstance(j, int) and j < 2):
                    act.wait_ge(s["u_full"], j - 1)
                nc.scalar.activation(xT[:, q, :, :].rearrange("p k t -> p (k t)"), xT_ps[:, 0:D], ACT.Copy).then_inc(s["xT_free"], 1)

            def gate(j, q):
                act.wait_ge(s["g_full"], j + 1)
                act.wait_ge(s["h_done"], j + 1)
                nc.scalar.activation(si[:, q, :], g_ps[q][:], ACT.Silu).then_inc(s["si_done"], 1)

            def copy_h(j, q):
                act.wait_ge(s["hT_full"], j + 1)
                if not (isinstance(j, int) and j < 2):
                    act.wait_ge(s["o_full"], j - 1)
                nc.scalar.activation(hT[:, q, :, :].rearrange("p k t -> p (k t)"), hT_ps[:], ACT.Copy).then_inc(s["hT_free"], 1)

            run(act, [none, copy_x, gate, copy_h, none, none])

        @block.vector
        def _(dve):
            dve.sem_inc(s["h_done"], 2)
            dve.sem_inc(s["y_done"], 2)

            def mul(j, q):
                dve.wait_ge(s["si_done"], j + 1)
                dve.wait_ge(s["u_full"], j + 1)
                if not (isinstance(j, int) and j < 2):
                    dve.wait_ge(s["hT_full"], j - 1)
                nc.vector.tensor_tensor(h[:, q, :], si[:, q, :], u_ps[q][:], ALU.mult).then_inc(s["h_done"], 1)

            def result(j, q):
                dve.wait_ge(s["o_full"], j + 1)
                if not (isinstance(j, int) and j < 2):
                    dve.wait_ge(s[f"stored{q}"], (j - q) * 8)
                nc.vector.tensor_copy(y[:, q, :], o_ps[q][:, 0:D]).then_inc(s["y_done"], 1)

            run(dve, [none, none, mul, none, result, none])


def combine_results(chip, dram, where, share, gate):
    nc = chip.nc
    RING = 4
    with ExitStack() as ctx:
        got = ctx.enter_context(nc.sbuf_tensor("L3C_got", [P, RING, 2, D], F32))
        at = ctx.enter_context(nc.sbuf_tensor("L3C_at", [P, RING, 2], U32))
        s = {n: ctx.enter_context(nc.semaphore(f"L3C_{n}")) for n in ("at_done", "half_done")}
        s.update({f"gathered{q}": chip.queued[f"gathered{q}"] for q in range(RING)})
        block = ctx.enter_context(nc.Block())
        none = lambda t, q: None

        @block.gpsimd
        def _(pool):
            def gather(t, q):
                pool.wait_ge(s["at_done"], t + 1)
                chip.settle(pool)
                for k in range(2):
                    nc.gpsimd.indirect_dma_start(got[:, q, k, :], None, dram["results"], bass.IndirectOffsetOnAxis(at[:, q, k:k + 1], 0)
                                                 ).then_inc(s[f"gathered{q}"], 16)

            pipelined(pool, [gather, none, none, none], unroll=RING, ring=RING)

        @block.vector
        def _(dve):
            def indices(t, q):
                nc.vector.tensor_copy(at[:, q, :], where[:, bass.ds(t, 1), :].rearrange("p t k -> p (t k)")).then_inc(s["at_done"], 1)

            def add(t, q):
                dve.wait_ge(s[f"gathered{q}"], (t - q) * (32 // RING) + 32)
                nc.vector.scalar_tensor_tensor(out=tile_of(chip, t), in0=got[:, q, 0, :], scalar=share[:, bass.ds(t, 1), 0], in1=tile_of(chip, t),
                                               op0=ALU.mult, op1=ALU.add).then_inc(s["half_done"], 1)
                dve.wait_ge(s["half_done"], 2 * t + 1)
                nc.vector.scalar_tensor_tensor(out=tile_of(chip, t), in0=got[:, q, 1, :], scalar=share[:, bass.ds(t, 1), 1], in1=tile_of(chip, t),
                                               op0=ALU.mult, op1=ALU.add).then_inc(s["half_done"], 1)
                dve.wait_ge(s["half_done"], 2 * t + 2)

            pipelined(dve, [indices, none, none, add], unroll=RING, ring=RING)


def post_stage(chip, dram):
    nc, w = chip.nc, chip.w
    RING = 4
    gate = chip.gates[:, 2:3]
    with ExitStack() as ctx:
        def sb(name, shape, dt=F32):
            return ctx.enter_context(nc.sbuf_tensor(f"L2P_{name}", shape, dt))

        cT_ps, f_ps = ([ctx.enter_context(nc.psum_tensor(f"L2P_{n}_ps{i}", [P, 512], F32)) for i in range(2)] for n in ("cT", "f"))
        r, c, f, cT = sb("r", [P, RING, D]), sb("c", [P, RING, D]), sb("f", [P, RING, D]), sb("cT", [P, RING, KD, P])
        stat, mv, ve, rs = sb("stat", [P, 2, RING, 6]), sb("mv", [P, 2, RING, 2]), sb("ve", [P, 2, RING]), sb("rs", [P, 2, RING])
        gain, shift = sb("gain", [P, D]), sb("shift", [P, D])
        names = """loaded0 loaded1 loaded2 loaded3 biased relu_done stats_done rstd_done norm_done c_done cT_full cT_copied f_full
            f_taken stats2_done rstd2_done norm2_done x_done dve_step pool_step""".split()
        s = {n: ctx.enter_context(nc.semaphore(f"L2P_{n}")) for n in names}
        block = ctx.enter_context(nc.Block())
        none = lambda t, q: None

        def run(eng, phases):
            pipelined(eng, [phases.get(k, none) for k in range(8)], unroll=RING, ring=RING)

        def later(t):
            return not (isinstance(t, int) and t < RING)

        @block.sync
        def _(sp):
            def load(t, q):
                if later(t):
                    sp.wait_ge(s["c_done"], t - RING + 1)
                    chip.settle(sp)
                sp.dma_start(r[:, q, :], dram["b"][:, bass.ds(t, 1), :].rearrange("p t d -> p (t d)")).then_inc(s[f"loaded{q}"], 16)

            run(sp, {0: load})

        @block.tensor
        def _(pe):
            def turn(t, q):
                pe.wait_ge(s["c_done"], t + 1)
                pe.wait_ge(s["cT_copied"], t + 1)
                for k in range(KD):
                    mm = nc.tensor.transpose(cT_ps[q % 2][:, k * P:(k + 1) * P], c[:, q, k * P:(k + 1) * P], chip.ident[:])
                mm.then_inc(s["cT_full"], 1)

            def multiply(t, q):
                pe.wait_ge(s["cT_copied"], t + 3)
                pe.wait_ge(s["f_taken"], t + 1)
                for k in range(KD):
                    mm = nc.tensor.matmul(f_ps[q % 2][:, 0:D], cT[:, q, k, :], w["L2_Wf"][:, k, :], start=(k == 0), stop=(k == KD - 1))
                mm.then_inc(s["f_full"], 1)

            run(pe, {4: turn, 5: multiply})

        @block.scalar
        def _(act):
            act.sem_inc(s["cT_copied"], 2)

            def relu(t, q):
                act.wait_ge(s["biased"], t + 1)
                nc.scalar.activation(r[:, q, :], r[:, q, :], ACT.Relu, scale=2.0).then_inc(s["relu_done"], 1)

            def copy(t, q):
                act.wait_ge(s["cT_full"], t + 1)
                if later(t):
                    act.wait_ge(s["f_full"], t - RING + 1)
                nc.scalar.activation(cT[:, q, :, :].rearrange("p k t -> p (k t)"), cT_ps[q % 2][:, 0:D], ACT.Copy).then_inc(s["cT_copied"], 1)

            run(act, {1: relu, 4: copy})

        @block.vector
        def _(dve):
            link = Links(dve, s["dve_step"], [0, 0, 1, 0, 0, 0, 2, 0])
            dve.sem_inc(s["f_taken"], 2)

            def bias(t, q):
                dve.wait_ge(s[f"loaded{q}"], (t - q) * (16 // RING) + 16)
                nc.vector.tensor_tensor(r[:, q, :], r[:, q, :], chip.vec("L2_xattn_bo2"), ALU.add).then_inc(s["biased"], 1)

            def stats(t, q):
                link.enter(2, t)
                dve.wait_ge(s["relu_done"], t + 1)
                link(nc.vector.bn_stats(stat[:, 0, q, :], r[:, q, :]))
                chip.settle(dve)
                nc.vector.bn_aggr(mv[:, 0, q, :], stat[:, 0, q, :]).then_inc(s["stats_done"], 1)
                link.leave()

            def normalise(t, q):
                dve.wait_ge(s["rstd_done"], t + 1)
                nc.vector.tensor_scalar(r[:, q, :], r[:, q, :], mv[:, 0, q, 0:1], rs[:, 0, q:q + 1], ALU.subtract, ALU.mult
                                        ).then_inc(s["norm_done"], 1)

            def add(t, q):
                link.enter(6, t)
                dve.wait_ge(s["f_full"], t + 1)
                if later(t):
                    dve.wait_ge(s["x_done"], t - RING + 1)
                nc.vector.tensor_tensor(f[:, q, :], f_ps[q % 2][:, 0:D], chip.vec("L2_xattn_bf"), ALU.add).then_inc(s["f_taken"], 1)
                dve.wait_ge(s["f_taken"], t + 3)
                link(nc.vector.scalar_tensor_tensor(out=f[:, q, :], in0=f[:, q, :], scalar=0.0, in1=c[:, q, :], op0=ALU.max, op1=ALU.add))
                link(nc.vector.bn_stats(stat[:, 1, q, :], f[:, q, :]))
                chip.settle(dve)
                nc.vector.bn_aggr(mv[:, 1, q, :], stat[:, 1, q, :]).then_inc(s["stats2_done"], 1)
                link.leave()

            def normalise2(t, q):
                dve.wait_ge(s["rstd2_done"], t + 1)
                nc.vector.tensor_scalar(f[:, q, :], f[:, q, :], mv[:, 1, q, 0:1], rs[:, 1, q:q + 1], ALU.subtract, ALU.mult
                                        ).then_inc(s["norm2_done"], 1)

            run(dve, {1: bias, 2: stats, 3: normalise, 6: add, 7: normalise2})

        @block.gpsimd
        def _(pool):
            nc.gpsimd.tensor_scalar(gain[:], chip.vec("L2_xattn_g3"), 1.0, gate, ALU.mult, ALU.mult).then_inc(s["pool_step"], 1)
            nc.gpsimd.tensor_scalar(shift[:], chip.vec("L2_xattn_b3"), 1.0, gate, ALU.mult, ALU.mult).then_inc(s["pool_step"], 1)
            pool.wait_ge(s["pool_step"], 2)
            link = Links(pool, s["pool_step"], [0, 0, 1, 1, 0, 0, 1, 2], start=2)

            def rstd(which, phase):
                def go(t, q):
                    link.enter(phase, t)
                    pool.wait_ge(s[("stats_done", "stats2_done")[which]], t + 1)
                    chip.settle(pool)
                    link(nc.gpsimd.tensor_scalar(ve[:, which, q:q + 1], mv[:, which, q, 1:2], 1e-6, None, ALU.add))
                    nc.gpsimd.tensor_tensor(rs[:, which, q:q + 1], ve[:, which, q:q + 1], chip.neghalf[:, 0:1], ALU.pow
                                            ).then_inc(s[("rstd_done", "rstd2_done")[which]], 1)
                    link.leave()
                return go

            def make_c(t, q):
                link.enter(3, t)
                pool.wait_ge(s["norm_done"], t + 1)
                link(nc.gpsimd.tensor_tensor(r[:, q, :], r[:, q, :], chip.vec("L2_xattn_g2"), ALU.mult))
                if later(t):
                    pool.wait_ge(s["stats2_done"], t - RING + 1)
                nc.gpsimd.tensor_tensor(c[:, q, :], r[:, q, :], chip.vec("L2_xattn_b2"), ALU.add).then_inc(s["c_done"], 1)
                link.leave()

            def finish(t, q):
                link.enter(7, t)
                pool.wait_ge(s["norm2_done"], t + 1)
                link(nc.gpsimd.tensor_tensor(f[:, q, :], f[:, q, :], gain[:], ALU.mult))
                link(nc.gpsimd.tensor_tensor(f[:, q, :], f[:, q, :], shift[:], ALU.add))
                nc.gpsimd.tensor_tensor(tile_of(chip, t), tile_of(chip, t), f[:, q, :], ALU.add).then_inc(s["x_done"], 1)
                link.leave()

            run(pool, {2: rstd(0, 2), 3: make_c, 6: rstd(1, 6), 7: finish})


def clear_semaphores(nc):
    with nc.Block() as block:
        @block.gpsimd
        def _(pool):
            for number in sorted(set(nc.released_uncleared_semaphores)):
                pool.sem_clear(range(number, number + 1))


def build(nc, dram):
    ctx = ExitStack()
    with ctx:
        chip = Chip(nc, ctx)
        chip.x = chip.keep("x_sb", [P, T * D])
        chip.ident = chip.keep("ident", [P, P])
        chip.ones = chip.keep("ones", [P, P])
        chip.neghalf = chip.keep("neghalf", [P, 32])
        chip.half = chip.keep("half", [P, 32])
        chip.iota = chip.keep("iota", [P, 32])
        chip.gates = chip.keep("gates", [P, 2 * B])
        chip.vecs = chip.keep("vecs", [P, len(VEC) * D])
        chip.cols = chip.keep("cols", [P, 2 * len(COL)])
        chip.ctxT = chip.keep("ctxT_sb", [P, KD, B * NC])
        chip.headmask = chip.keep("headmask_sb", [P, HH + 2])
        chip.rowmask = chip.keep("rowmask_sb", [P, KCH, P])
        chip.loaded = ctx.enter_context(nc.semaphore("loaded"))
        chip.arena = chip.keep("weights", [P, ARENA])
        chip.w, chip.w_in = {}, {}
        chip.zone(WEIGHTS["L1"], dram, 0)
        chip.zone(WEIGHTS["L2S"] + WEIGHTS["L2"], dram, 0)
        chip.zone(WEIGHTS["L0"] + WEIGHTS["L0F"], dram, ZONE_B)
        chip.zone(WEIGHTS["L1F"], dram, ZONE_B)
        chip.zone(WEIGHTS["L3"], dram, ZONE_B)
        for name in chip.w:
            chip.w_in[name] = ctx.enter_context(nc.semaphore("in_" + name))
        chip.queued = {n: ctx.enter_context(nc.semaphore(n)) for n in ["mrow_in"] + [f"scattered{q}" for q in range(8)] + [f"gathered{q}" for q in range(4)]}
        chip.settled = {str(e.engine): ctx.enter_context(nc.semaphore(f"settled{i}")) for i, e in enumerate((nc.vector, nc.gpsimd, nc.scalar, nc.sync, nc.tensor))}
        dram = dict(dram)
        dram["a"] = nc.dram_tensor("self_attended", (P, T, D), F32, kind="Internal").ap()
        dram["b"] = nc.dram_tensor("context_attended", (P, T, D), F32, kind="Internal").ap()
        dram["parts"] = nc.dram_tensor("qk_parts", (2 * B, H // 4, 3, 4, D // H, S), BF16, kind="Internal").ap()
        dram["rows"] = nc.dram_tensor("expert_rows", (8 * (T + 1) * P + 8 * P, D), F32, kind="Internal").ap()
        dram["results"] = nc.dram_tensor("expert_results", ((2 * T + 7) * P, D), F32, kind="Internal").ap()
        load_stage(chip, dram)
        stages = [lambda: context_stage(chip, dram, "L0"),
                  lambda: experts_stage(chip, dram),
                  lambda: context_stage(chip, dram, "L1"),
                  lambda: ternary_stage(chip, dram),
                  lambda: (self_stage(chip, dram), clear_semaphores(nc), context_stage(chip, dram, "L2"), clear_semaphores(nc), post_stage(chip, dram)),
                  lambda: routed_stage(chip, dram),
                  lambda: single_stage(chip, dram),
                  lambda: mixture_stage(chip, dram)]
        for stage in stages:
            stage()
            clear_semaphores(nc)
        with nc.semaphore("stored") as stored, nc.Block() as block:
            @block.sync
            def _(sp):
                sp.dma_start(dram["out"], chip.x[:].rearrange("p (t d) -> p t d", d=D)).then_inc(stored, 16)
                sp.wait_ge(stored, 16)


def rows_first(w):
    k, n = w.shape
    return w.reshape(k // P, P, n).transpose(1, 0, 2)


def by_head(w):
    h, e, d = w.shape
    return w.transpose(1, 0, 2).reshape(e, h * d)


def lay_out(a):
    tiles = lambda m: m.reshape(T, P, m.shape[-1]).transpose(1, 0, 2)
    ins = {"x": tiles(a["x"]), "mask": tiles(a["mask_BxSxS2_ik1"]), "g_xattn": a["g_xattn"], "g_ffn": a["g_ffn"],
           "ctxT": rows_first(a["ctx_1024"].reshape(B * NC, D).T)}
    p = np.arange(P)
    head = (p[:, None] // 16 == np.arange(HH)[None]).astype(np.float32)
    pair = (p[:, None] // 64 == np.arange(2)[None]).astype(np.float32)
    ins["headmask"] = np.concatenate([head, pair], 1)
    row = np.arange(KCH)[None, :, None] * P + p[:, None, None]
    ins["rowmask"] = (row // NC == p[None, None, :] // 16).astype(np.float32)
    for n in VEC:
        ins[n] = a[n]
    for n in COL:
        ins[n] = a[n].reshape(KD, P).T
    ins["L0_Wq"] = rows_first(a["L0_xattn_Wq"].T)
    ins["L0_Wk"] = rows_first(a["L0_xattn_Wk"].T)
    ins["L0_Wv"] = rows_first(a["L0_xattn_Wv"].T)
    ins["L0_Wo"] = rows_first(a["L0_xattn_Wo"].T)
    ins["L0F_protoT"] = rows_first(a["L0_ffn_prototypes"].T)
    ins["L0F_BT"] = rows_first(a["L0_ffn_B"].reshape(512, D).T)
    ins["L0F_A"] = rows_first(a["L0_ffn_A"].transpose(0, 2, 1).reshape(512, D))
    ins["L0F_bias"] = a["L0_ffn_bias"]
    ins["L0F_temp"] = a["L0_ffn_temp"].reshape(1)
    ins["L1F_gate"] = rows_first(a["L1_ffn_w_gate"].T)
    ins["L1F_up"] = rows_first(a["L1_ffn_w_up"].T)
    ins["L1F_down"] = rows_first(a["L1_ffn_w_down"].T)
    ins["L1_Wk"] = rows_first(a["L1_xattn_w_kv"][:, :1024])
    ins["L1_Wv"] = rows_first(a["L1_xattn_w_kv"][:, 1024:])
    ins["L1_WqT"] = rows_first(a["L1_xattn_w_q"].T)
    ins["L1_Wo1"] = rows_first(a["L1_xattn_w_out1"])
    ins["L1_Wo"] = rows_first(a["L1_xattn_w_out2"])
    ins["L2S_Wq"] = rows_first(by_head(a["L2_xattn_Wq1"]))
    ins["L2S_Wk"] = rows_first(by_head(a["L2_xattn_Wk1"]))
    ins["L2S_Wv"] = rows_first(by_head(a["L2_xattn_Wv1"]))
    ins["L2S_Wo"] = rows_first(a["L2_xattn_Wo1"])
    ins["L2_rw"] = a["L2_ffn_routing_weights"].reshape(4, P, 8).transpose(1, 0, 2)
    ins["L2_ri"] = a["L2_ffn_router_indices"].reshape(4, P, 2).transpose(1, 0, 2)
    gu = a["L2_ffn_gate_up_proj"]
    gu = np.concatenate([gu[:, :, 0::2], gu[:, :, 1::2]], 2)
    ins["L2_gu"] = rows_first(by_head(gu))
    gb = a["L2_ffn_gate_up_proj_bias"]
    ins["L2_gu_bias"] = np.concatenate([gb[:, 0::2], gb[:, 1::2]], 1).reshape(-1)
    ins["L2_dn"] = rows_first(by_head(a["L2_ffn_down_proj"]))
    ins["L2_dn_bias"] = a["L2_ffn_down_proj_bias"]
    ins["L3_wg"] = rows_first(a["L3_ffn_gate_kernel"])
    ins["L3_w0"] = rows_first(by_head(a["L3_ffn_w0_kernel"]))
    ins["L3_w1"] = rows_first(by_head(a["L3_ffn_w1_kernel"]))
    ins["L3_wo"] = rows_first(by_head(a["L3_ffn_wo_kernel"]))
    ins["L3_WqT"] = rows_first(a["L3_xattn_Wq"].T)
    ins["L3_Wk"] = rows_first(a["L3_xattn_Wk"])
    ins["L3_Wv"] = rows_first(a["L3_xattn_Wv"])
    ins["L2_Wq"] = rows_first(by_head(a["L2_xattn_Wq2"]))
    ins["L2_Wk"] = rows_first(by_head(a["L2_xattn_Wk2"]))
    ins["L2_Wv"] = rows_first(by_head(a["L2_xattn_Wv2"]))
    ins["L2_Wo"] = rows_first(a["L2_xattn_Wo2"])
    ins["L2_Wf"] = rows_first(a["L2_xattn_Wf"])
    return {k: np.ascontiguousarray(v) for k, v in ins.items()}


def kernel(**inputs):
    import concourse.bacc as bacc
    from concourse.bass_utils import run_bass_kernel_spmd

    arrays = lay_out({k: np.asarray(v) for k, v in inputs.items()})
    nc = bacc.Bacc("TRN2", target_bir_lowering=False, num_devices=1)
    dram = {k: nc.dram_tensor("in_" + k, v.shape, mybir.dt.from_np(v.dtype), kind="ExternalInput").ap()
            for k, v in arrays.items()}
    dram["out"] = nc.dram_tensor("out", (P, T, D), F32, kind="ExternalOutput").ap()
    build(nc, dram)
    got = run_bass_kernel_spmd(nc, [{"in_" + k: v for k, v in arrays.items()}], core_ids=[0]).results[0]["out"]
    return got.transpose(1, 0, 2).reshape(B, S, D)
```
